# Optimizing a Trainium2 kernel written in Bass

```python
import numpy as np
import jax
import jax.numpy as jnp

def _softmax(x, axis=-1):
    return jax.nn.softmax(x, axis=axis)

def _gelu(x):
    return jax.nn.gelu(x, approximate=True)

def _silu(x):
    return jax.nn.silu(x)

def _sigmoid(x):
    return jax.nn.sigmoid(x)

def _layernorm(x, axis=-1, eps=1e-05):
    m = jnp.mean(x, axis=axis, keepdims=True)
    v = jnp.var(x, axis=axis, keepdims=True)
    return (x - m) / jnp.sqrt(v + eps)

def _scatter_add(tgt, idx, src, axis=0):
    return tgt.at[idx].add(src)

def _segment_sum(src, seg, n):
    return jax.ops.segment_sum(src, seg, n)
kernel_name = 'mk_metaformer_d2_conv_nchw256_r4_a5b920'

def setup_inputs(seed: int=0):
    np.random.seed(seed)
    _w = jnp.asarray

    def _rec_inputs():
        import jax
        import jax.numpy as jnp
        _gk = jax.random.key(seed)
        x = -8.268e-05 + 0.9999 * jax.random.normal(jax.random.fold_in(_gk, 1), (16, 64, 56, 56), jnp.float32)
        return x
    x = _rec_inputs()

    def _L0_conv_setup():
        import jax, jax.numpy as jnp
        import numpy as np
        from jax import lax
        FPLANE = 64
        RATIO = 0.5
        C_SHIFT = int(FPLANE * RATIO)
        HALF = C_SHIFT // 2

        def _cyclic_pad_t(x):
            return jnp.concatenate([x[:, :, -1:], x, x[:, :, :1]], axis=2)

        def _conv3d(x, w, b):
            y = lax.conv_general_dilated(x, w, window_strides=(1, 1, 1), padding=[(0, 0), (1, 1), (1, 1)], dimension_numbers=('NCDHW', 'OIDHW', 'NCDHW'))
            return y + b[None, :, None, None, None]
        key = jax.random.key(seed)
        k_x, k_wl, k_bl, k_wr, k_br = jax.random.split(key, 5)
        T, C, H, W = (16, FPLANE, 56, 56)
        x = jax.random.normal(k_x, (T, C, H, W), dtype=jnp.float32)
        scale = 1.0 / np.sqrt(HALF * 27)
        w_l = jax.random.normal(k_wl, (1, HALF, 3, 3, 3), dtype=jnp.float32) * scale
        b_l = jax.random.normal(k_bl, (1,), dtype=jnp.float32) * 0.01
        w_r = jax.random.normal(k_wr, (1, HALF, 3, 3, 3), dtype=jnp.float32) * scale
        b_r = jax.random.normal(k_br, (1,), dtype=jnp.float32) * 0.01
        return {'x': x, 'w_l': w_l, 'b_l': b_l, 'w_r': w_r, 'b_r': b_r}
    _L0_conv_all = _L0_conv_setup()
    _L0_conv_in = {k: v for k, v in _L0_conv_all.items() if k in ('w_l', 'b_l', 'w_r', 'b_r')}
    del _L0_conv_all

    def _L0_ffn_setup():
        import jax, jax.numpy as jnp
        import numpy as np
        TOP_K = 2
        key = jax.random.key(seed)
        ks = jax.random.split(key, 4)
        B, L, D, H, E = (8, 1024, 64, 256, 8)
        s = 0.02
        return {'x': jax.random.normal(ks[0], (B, L, D), jnp.float32), 'Wg': jax.random.normal(ks[1], (D, E), jnp.float32) * s, 'bg': jnp.zeros((E,), jnp.float32), 'W1': jax.random.normal(ks[2], (E, D, H), jnp.float32) * s, 'b1': jnp.zeros((E, H), jnp.float32), 'W2': jax.random.normal(ks[3], (E, H, D), jnp.float32) * s, 'b2': jnp.zeros((E, D), jnp.float32)}
    _L0_ffn_all = _L0_ffn_setup()
    _L0_ffn_in = {k: v for k, v in _L0_ffn_all.items() if k in ('Wg', 'bg', 'W1', 'b1', 'W2', 'b2')}
    del _L0_ffn_all

    def _L1_conv_setup():
        import jax, jax.numpy as jnp
        import numpy as np
        OUT_CHN, IN_CHN, K = (64, 64, 3)
        STRIDE, PAD = (1, 1)
        key = jax.random.key(seed)
        kx, kw, ks = jax.random.split(key, 3)
        x = jax.random.normal(kx, (32, IN_CHN, 56, 56), dtype=jnp.float32)
        weights = jax.random.uniform(kw, (OUT_CHN * IN_CHN * K * K, 1), dtype=jnp.float32) * 0.001
        sf = jax.random.uniform(ks, (1, OUT_CHN, K, K), dtype=jnp.float32) * 0.001
        real_scaling_factor = jnp.mean(jnp.abs(sf), axis=(0, 2, 3), keepdims=True)
        return {'x': x, 'weights': weights, 'real_scaling_factor': real_scaling_factor}
    _L1_conv_all = _L1_conv_setup()
    _L1_conv_in = {k: v for k, v in _L1_conv_all.items() if k in ('weights', 'real_scaling_factor')}
    del _L1_conv_all

    def _L1_ffn_setup():
        import math
        import jax, jax.numpy as jnp
        import numpy as np
        CAPACITY_FACTOR = 1.25
        TOP_K = 2
        LN_EPS = 1e-05

        def _layer_norm(x, gamma, beta):
            mu = jnp.mean(x, axis=-1, keepdims=True)
            var = jnp.var(x, axis=-1, keepdims=True)
            return (x - mu) * jax.lax.rsqrt(var + LN_EPS) * gamma + beta
        key = jax.random.key(seed)
        ks = jax.random.split(key, 4)
        B, S, D, F, E = (8, 1024, 64, 128, 8)
        x = jax.random.normal(ks[0], (B, S, D), dtype=jnp.float32)
        Wr = jax.random.normal(ks[1], (D, E), dtype=jnp.float32) / np.sqrt(D)
        br = jnp.zeros((E,), jnp.float32)
        W1 = jax.random.normal(ks[2], (E, D, F), dtype=jnp.float32) / np.sqrt(D)
        b1 = jnp.zeros((E, F), jnp.float32)
        W2 = jax.random.normal(ks[3], (E, F, D), dtype=jnp.float32) / np.sqrt(F)
        b2 = jnp.zeros((E, D), jnp.float32)
        gamma = jnp.ones((D,), jnp.float32)
        beta = jnp.zeros((D,), jnp.float32)
        return {'x': x, 'Wr': Wr, 'br': br, 'W1': W1, 'b1': b1, 'W2': W2, 'b2': b2, 'gamma': gamma, 'beta': beta}
    _L1_ffn_all = _L1_ffn_setup()
    _L1_ffn_in = {k: v for k, v in _L1_ffn_all.items() if k in ('Wr', 'br', 'W1', 'b1', 'W2', 'b2', 'gamma', 'beta')}
    del _L1_ffn_all
    return {'x': x, 'L0_conv_w_l': _L0_conv_in['w_l'], 'L0_conv_b_l': _L0_conv_in['b_l'], 'L0_conv_w_r': _L0_conv_in['w_r'], 'L0_conv_b_r': _L0_conv_in['b_r'], 'L0_ffn_Wg': _L0_ffn_in['Wg'], 'L0_ffn_bg': _L0_ffn_in['bg'], 'L0_ffn_W1': _L0_ffn_in['W1'], 'L0_ffn_b1': _L0_ffn_in['b1'], 'L0_ffn_W2': _L0_ffn_in['W2'], 'L0_ffn_b2': _L0_ffn_in['b2'], 'L1_conv_weights': _L1_conv_in['weights'], 'L1_conv_real_scaling_factor': _L1_conv_in['real_scaling_factor'], 'L1_ffn_Wr': _L1_ffn_in['Wr'], 'L1_ffn_br': _L1_ffn_in['br'], 'L1_ffn_W1': _L1_ffn_in['W1'], 'L1_ffn_b1': _L1_ffn_in['b1'], 'L1_ffn_W2': _L1_ffn_in['W2'], 'L1_ffn_b2': _L1_ffn_in['b2'], 'L1_ffn_gamma': _L1_ffn_in['gamma'], 'L1_ffn_beta': _L1_ffn_in['beta']}

def reference(x, L0_conv_w_l, L0_conv_b_l, L0_conv_w_r, L0_conv_b_r, L0_ffn_Wg, L0_ffn_bg, L0_ffn_W1, L0_ffn_b1, L0_ffn_W2, L0_ffn_b2, L1_conv_weights, L1_conv_real_scaling_factor, L1_ffn_Wr, L1_ffn_br, L1_ffn_W1, L1_ffn_b1, L1_ffn_W2, L1_ffn_b2, L1_ffn_gamma, L1_ffn_beta):
    import jax
    import jax.numpy as jnp

    def _L0_conv_ref(x, w_l, b_l, w_r, b_r):
        import jax, jax.numpy as jnp
        import numpy as np
        from jax import lax
        FPLANE = 64
        RATIO = 0.5
        C_SHIFT = int(FPLANE * RATIO)
        HALF = C_SHIFT // 2

        def _cyclic_pad_t(x):
            return jnp.concatenate([x[:, :, -1:], x, x[:, :, :1]], axis=2)

        def _conv3d(x, w, b):
            y = lax.conv_general_dilated(x, w, window_strides=(1, 1, 1), padding=[(0, 0), (1, 1), (1, 1)], dimension_numbers=('NCDHW', 'OIDHW', 'NCDHW'))
            return y + b[None, :, None, None, None]
        x5 = x.transpose(1, 0, 2, 3)[None]
        x_l = x5[:, :HALF]
        x_r = x5[:, HALF:C_SHIFT]
        x_keep = x5[:, C_SHIFT:]
        gate_l = jnp.tanh(_conv3d(_cyclic_pad_t(x_l), w_l, b_l))
        gate_r = jnp.tanh(_conv3d(_cyclic_pad_t(x_r), w_r, b_r))
        y_l = gate_l * x_l
        y_r = gate_r * x_r
        y_l = jnp.roll(y_l, -1, axis=2) + (x_l - y_l)
        y_r = jnp.roll(y_r, 1, axis=2) + (x_r - y_r)
        y_all = jnp.concatenate([y_l, y_r, x_keep], axis=1)
        return y_all[0].transpose(1, 0, 2, 3)

    def _L0_ffn_ref(x, Wg, bg, W1, b1, W2, b2):
        import jax, jax.numpy as jnp
        import numpy as np
        TOP_K = 2
        B, L, D = x.shape
        E = W1.shape[0]
        xf = x.reshape(-1, D)
        gate_logits = xf @ Wg + bg
        top_w, top_i = jax.lax.top_k(gate_logits, TOP_K)
        top_w = jax.nn.softmax(top_w, axis=-1)
        w_dense = jnp.sum(jax.nn.one_hot(top_i, E, dtype=xf.dtype) * top_w[..., None], axis=1)
        out = jnp.zeros_like(xf)
        for e in range(E):
            h = jax.nn.gelu(xf @ W1[e] + b1[e], approximate=False)
            out = out + w_dense[:, e:e + 1] * (h @ W2[e] + b2[e])
        return out.reshape(B, L, D)

    def _L1_conv_ref(x, weights, real_scaling_factor):
        import jax, jax.numpy as jnp
        import numpy as np
        OUT_CHN, IN_CHN, K = (64, 64, 3)
        STRIDE, PAD = (1, 1)
        real_w = weights.reshape(OUT_CHN, IN_CHN, K, K)
        clipped = jnp.clip(real_w, -1.0, 1.0)
        binary_w = jax.lax.stop_gradient(jnp.sign(real_w) - clipped) + clipped
        y = jax.lax.conv_general_dilated(x, binary_w, window_strides=(STRIDE, STRIDE), padding=[(PAD, PAD), (PAD, PAD)], dimension_numbers=('NCHW', 'OIHW', 'NCHW'))
        return y * real_scaling_factor

    def _L1_ffn_ref(x, Wr, br, W1, b1, W2, b2, gamma, beta):
        import math
        import jax, jax.numpy as jnp
        import numpy as np
        CAPACITY_FACTOR = 1.25
        TOP_K = 2
        LN_EPS = 1e-05

        def _layer_norm(x, gamma, beta):
            mu = jnp.mean(x, axis=-1, keepdims=True)
            var = jnp.var(x, axis=-1, keepdims=True)
            return (x - mu) * jax.lax.rsqrt(var + LN_EPS) * gamma + beta
        B, S, D = x.shape
        E = Wr.shape[1]
        N = B * S
        K = TOP_K
        logits = jnp.mean(x, axis=1) @ Wr + br
        routing_weights = jax.nn.softmax(logits, axis=-1)
        capacity = float(math.ceil(N * CAPACITY_FACTOR / E))
        expected_loads = routing_weights.sum(axis=0) * (N / B)
        scale = jnp.where(expected_loads > capacity, capacity / expected_loads, 1.0)
        routing_weights = jax.nn.softmax(routing_weights * scale, axis=-1)
        rw_tok = jnp.broadcast_to(routing_weights[:, None, :], (B, S, E)).reshape(N, E)
        top_w, top_i = jax.lax.top_k(rw_tok, K)
        top_w = jax.nn.softmax(top_w, axis=-1)
        xf = x.reshape(N, D)
        h = jax.nn.gelu(jnp.einsum('nd,edf->enf', xf, W1) + b1[:, None, :], approximate=False)
        y = jnp.einsum('enf,efd->end', h, W2) + b2[:, None, :]
        w_dense = jnp.zeros((N, E), x.dtype).at[jnp.arange(N)[:, None], top_i].add(top_w)
        out = jnp.einsum('ne,end->nd', w_dense, y).reshape(B, S, D)
        out = _layer_norm(out + x, gamma, beta)
        return out

    def _gn(v, G=32, eps=1e-05):
        B_, C_, H_, W_ = v.shape
        g = v.reshape(B_, G, C_ // G, H_, W_)
        m = jnp.mean(g, axis=(2, 3, 4), keepdims=True)
        s = jnp.var(g, axis=(2, 3, 4), keepdims=True)
        return ((g - m) / jnp.sqrt(s + eps)).reshape(v.shape)

    def _ln_c(v, eps=1e-06):
        m = jnp.mean(v, axis=1, keepdims=True)
        s = jnp.var(v, axis=1, keepdims=True)
        return (v - m) / jnp.sqrt(s + eps)

    def _ln_t(v, eps=1e-05):
        m = jnp.mean(v, axis=-1, keepdims=True)
        s = jnp.var(v, axis=-1, keepdims=True)
        return (v - m) / jnp.sqrt(s + eps)

    def _to_tokens(v):
        B_, C_, H_, W_ = v.shape
        return v.reshape(B_, C_, H_ * W_).transpose(0, 2, 1)

    def _from_tokens(t, like):
        B_, C_, H_, W_ = like.shape
        return t.transpose(0, 2, 1).reshape(B_, C_, H_, W_)
    x = x + _L0_conv_ref(_ln_c(x), L0_conv_w_l, L0_conv_b_l, L0_conv_w_r, L0_conv_b_r)
    t = _to_tokens(x)
    t = t + _L0_ffn_ref(_ln_t(t), L0_ffn_Wg, L0_ffn_bg, L0_ffn_W1, L0_ffn_b1, L0_ffn_W2, L0_ffn_b2)
    x = _from_tokens(t, x)
    x = x + _L1_conv_ref(_ln_c(x), L1_conv_weights, L1_conv_real_scaling_factor)
    t = _to_tokens(x)
    t = t + _L1_ffn_ref(_ln_t(t), L1_ffn_Wr, L1_ffn_br, L1_ffn_W1, L1_ffn_b1, L1_ffn_W2, L1_ffn_b2, L1_ffn_gamma, L1_ffn_beta)
    x = _from_tokens(t, x)
    return x

_drawn_inputs = setup_inputs


def setup_inputs(seed=0):
    import zlib

    import numpy as np

    out = dict(_drawn_inputs(seed))
    spreads = {'L0_ffn_bg': (0.0, 0.1),
     'L0_ffn_b1': (0.0, 0.1),
     'L0_ffn_b2': (0.0, 0.1),
     'L1_ffn_br': (0.0, 0.1),
     'L1_ffn_b1': (0.0, 0.598),
     'L1_ffn_b2': (0.0, 0.411),
     'L1_ffn_gamma': (1.0, 0.2),
     'L1_ffn_beta': (0.0, 0.1)}
    factors = {'L1_conv_real_scaling_factor': 8.0}
    for name, (base, spread) in spreads.items():
        noise = np.random.default_rng([zlib.crc32(name.encode()), seed]).standard_normal(out[name].shape)
        drawn = base * np.exp(spread * noise) if base else spread * noise
        out[name] = jnp.asarray(drawn.astype(out[name].dtype))
    for name, factor in factors.items():
        out[name] = (out[name] * factor).astype(out[name].dtype)
    return out
```

```python
from contextlib import ExitStack

import concourse.bass as bass
from concourse import mybir

F32 = mybir.dt.float32
F32R = mybir.dt.float32r
I32 = mybir.dt.int32
ALU = mybir.AluOpType
ACT = mybir.ActivationFunctionType
AX = mybir.AxisListType

P = 128
T, C, HH, WW = 16, 64, 56, 56
PIX = HH * WW
NP = T // 2
ROWS = 8
KT = HH // ROWS
NT = NP * KT
TW = ROWS * WW
SUB = 4
GW = TW // SUB
HALF = 16
E = 8
H0 = 256
CH0 = H0 // P
F1 = 128
PADW = WW + 2
NQ = 4
GM = NQ * 2 * 3
CAPACITY = float(-(-T * PIX * 5 // (4 * E)))
EPS_C, EPS_T = 1e-6, 1e-5


def build(nc, A, out):
    top = ExitStack()

    def sem(ctx, name):
        return ctx.enter_context(nc.semaphore(name))

    def sbuf(ctx, name, shape, dt=F32):
        return ctx.enter_context(nc.sbuf_tensor(name, shape, dt))

    def psum(ctx, name, shape, dt=F32):
        return ctx.enter_context(nc.psum_tensor(name, shape, dt))

    def dram(name, shape, dt=F32):
        return nc.dram_tensor(name, shape, dt).ap()

    XN1 = dram("scr_xn1", [NT, P, TW])
    GPART = dram("scr_gate_part", [NP, GM, PIX])
    GATES = dram("scr_gates", [2 * T, PIX])
    Z = dram("scr_gated", [T + 2, 2 * HALF, PIX])
    SD2 = dram("scr_split2", [NT, 2, P, TW])
    WT = dram("scr_wtok", [NT, 2 * E, TW])
    SD4 = dram("scr_split4", [NT, 2, P, TW])
    XN4 = dram("scr_xn4", [NT, P, TW])
    W1D = dram("scr_w1split", [E, P, 2, F1])
    IDX = dram("scr_idx", [NP, 4], I32)
    WSEL = dram("scr_wsel", [NP, 4])

    X = sbuf(top, "X", [P, NT, TW])
    CEN = sbuf(top, "centre", [P, P])
    AVG = sbuf(top, "average", [P, P])
    EPS = sbuf(top, "eps", [P, 2])
    MSUM = sbuf(top, "msum", [P, NT])

    def tile(x, n):
        return x[:, bass.ds(n, 1), :].rearrange("p o w -> p (o w)")

    def rows(ap):
        return ap.rearrange("p (r w) -> p r w", w=WW)

    def wait(engine, s, value):
        if not isinstance(value, int) or value > 0:
            engine.wait_ge(s, value)

    def units(engine, n):
        yield 0
        with engine.Fori(1, n) as i:
            yield i

    def before(base, m):
        return base + max(m - 1, 0)

    class Norm:

        def __init__(self, ctx, tag):
            self.xc = psum(ctx, tag + "_xc", [P, 2, 512])
            self.var = psum(ctx, tag + "_var", [P, 2, 512])
            self.sq = sbuf(ctx, tag + "_sq", [P, 2, TW])
            self.r = sbuf(ctx, tag + "_r", [P, 2, TW])
            self.rr = sbuf(ctx, tag + "_rr", [P, 2, TW])
            self.q = sbuf(ctx, tag + "_q", [P, 2, TW])
            self.g = sbuf(ctx, tag + "_g", [P, 2, TW])
            self.centred, self.squared, self.var_ready, self.seeded = (
                sem(ctx, tag + s) for s in ("_centred", "_squared", "_var_ready", "_seeded"))
            self.seed_squared, self.q_done, self.g_done, self.normed = (
                sem(ctx, tag + s) for s in ("_seed_squared", "_q_done", "_g_done", "_normed"))

        def pe_centre(self, pe, base, m, x):
            wait(pe, self.normed, before(base, m))
            pe.matmul(self.xc[:, m % 2, 0:TW], CEN[:], x, start=True, stop=True).then_inc(self.centred, 1)

        def act_square(self, act, base, m):
            act.wait_ge(self.centred, base + m + 1)
            wait(act, self.var_ready, before(base, m))
            act.activation(self.sq[:, m % 2], self.xc[:, m % 2, 0:TW], ACT.Square).then_inc(self.squared, 1)

        def pe_var(self, pe, base, m):
            pe.wait_ge(self.squared, base + m + 1)
            wait(pe, self.q_done, before(base, m))
            pe.matmul(self.var[:, m % 2, 0:TW], AVG[:], self.sq[:, m % 2], start=True, stop=True)\
                .then_inc(self.var_ready, 1)

        def act_seed(self, act, base, m, eps_col):
            act.wait_ge(self.var_ready, base + m + 1)
            wait(act, self.g_done, before(base, m))
            act.activation(self.r[:, m % 2], self.var[:, m % 2, 0:TW], ACT.Abs_reciprocal_sqrt,
                           bias=EPS[:, eps_col:eps_col + 1]).then_inc(self.seeded, 1)
            act.wait_ge(self.seeded, base + m + 1)
            act.activation(self.rr[:, m % 2], self.r[:, m % 2], ACT.Square).then_inc(self.seed_squared, 1)

        def dve_norm(self, dve, base, m, eps, dst, accum=None):
            dve.wait_ge(self.seed_squared, base + m + 1)
            dve.scalar_tensor_tensor(out=self.q[:, m % 2], in0=self.var[:, m % 2, 0:TW], scalar=eps,
                                     in1=self.rr[:, m % 2], op0=ALU.add, op1=ALU.mult).then_inc(self.q_done, 1)
            dve.wait_ge(self.q_done, base + m + 1)
            dve.scalar_tensor_tensor(out=self.g[:, m % 2], in0=self.q[:, m % 2], scalar=-3.0,
                                     in1=self.r[:, m % 2], op0=ALU.add, op1=ALU.mult).then_inc(self.g_done, 1)
            dve.wait_ge(self.g_done, base + m + 1)
            xc, g = self.xc[:, m % 2, 0:TW], self.g[:, m % 2]
            if len(dst.shape) == 3:
                xc, g = rows(xc), rows(g)
            dve.scalar_tensor_tensor(out=dst, in0=xc, scalar=-0.5, in1=g, op0=ALU.mult, op1=ALU.mult,
                                     accum_out=accum).then_inc(self.normed, 1)

    with top:
        with ExitStack() as ctx:
            gw = sbuf(ctx, "gate_w", [P, 3, GM])
            xn = sbuf(ctx, "xn1", [P, 2, TW])
            gp = sbuf(ctx, "gate_part", [GM, 2, TW])
            gps = psum(ctx, "gate_psum", [P, 2, 512])
            ln = Norm(ctx, "ln1")
            consts, eps_set, x_in = sem(ctx, "p1_consts"), sem(ctx, "p1_eps"), sem(ctx, "p1_x")
            part_ready, part_copied = sem(ctx, "p1_part"), sem(ctx, "p1_part_copied")
            xn_stored = [sem(ctx, f"p1_xn_stored{b}") for b in range(2)]
            gp_stored = [sem(ctx, f"p1_gp_stored{b}") for b in range(2)]
            U = 2 * KT
            with nc.Block() as block:
                @block.sync
                def _(sp):
                    sp.dma_start(CEN[:], A["centre"]).then_inc(consts, 16)
                    sp.dma_start(AVG[:], A["average"]).then_inc(consts, 16)
                    sp.dma_start(gw[:], A["gate_w"]).then_inc(consts, 16)
                    for j in units(sp, NP):
                        wait(sp, x_in, 16 * j)
                        sp.dma_start(X[:, bass.ds(j * KT, KT), :].rearrange("p k w -> p (k w)"),
                                     A["x"][bass.ds(j, 1)].rearrange("o p w -> (o p) w")).then_inc(x_in, 16)

                @block.tensor
                def _(pe):
                    pe.wait_ge(consts, 48)

                    def gate(i, m):
                        pe.wait_ge(ln.normed, U * i + m + 1)
                        wait(pe, part_copied, before(U * i, m))
                        o = rows(gps[0:GM, m % 2, 0:TW])
                        src = rows(xn[:, m % 2])
                        pe.matmul(o, gw[:, 1, :], src, start=True, stop=False)
                        pe.matmul(o[:, :, 1:WW], gw[:, 0, :], src[:, :, 0:WW - 1], start=False, stop=False)
                        pe.matmul(o[:, :, 0:WW - 1], gw[:, 2, :], src[:, :, 1:WW], start=False, stop=True)\
                            .then_inc(part_ready, 1)

                    for i in units(pe, NT // U):
                        for m in range(U):
                            if m % KT == 0:
                                pe.wait_ge(x_in, 32 * i + 16 * (m // KT) + 16)
                            ln.pe_centre(pe, U * i, m, tile(X, U * i + m))
                            if m >= 1:
                                ln.pe_var(pe, U * i, m - 1)
                            if m >= 2:
                                gate(i, m - 2)
                        ln.pe_var(pe, U * i, U - 1)
                        gate(i, U - 2)
                        gate(i, U - 1)

                @block.scalar
                def _(act):
                    act.wait_ge(eps_set, 2)

                    def copy_part(i, m):
                        act.wait_ge(part_ready, U * i + m + 1)
                        wait(act, gp_stored[m % 2], 16 * (KT * i + m // 2))
                        act.activation(gp[:, m % 2], gps[0:GM, m % 2, 0:TW], ACT.Copy).then_inc(part_copied, 1)

                    for i in units(act, NT // U):
                        for m in range(U):
                            ln.act_square(act, U * i, m)
                            if m >= 1:
                                ln.act_seed(act, U * i, m - 1, 0)
                            if m >= 3:
                                copy_part(i, m - 3)
                        ln.act_seed(act, U * i, U - 1, 0)
                        for m in range(U - 3, U):
                            copy_part(i, m)

                @block.vector
                def _(dve):
                    dve.memset(EPS[:, 0:1], EPS_C).then_inc(eps_set, 1)
                    dve.memset(EPS[:, 1:2], EPS_T).then_inc(eps_set, 1)
                    for i in units(dve, NT // U):
                        for m in range(U):
                            wait(dve, xn_stored[m % 2], 16 * (KT * i + m // 2))
                            wait(dve, part_ready, before(U * i, m))
                            ln.dve_norm(dve, U * i, m, EPS_C, xn[:, m % 2])

                @block.gpsimd
                def _(pool):
                    def store_part(i, m):
                        pool.wait_ge(part_copied, U * i + m + 1)
                        pool.dma_start(GPART[bass.ds(2 * i + m // KT, 1), :, (m % KT) * TW:(m % KT + 1) * TW]
                                       .rearrange("o g w -> (o g) w"), gp[:, m % 2]).then_inc(gp_stored[m % 2], 16)

                    for i in units(pool, NT // U):
                        for m in range(U):
                            pool.wait_ge(ln.normed, U * i + m + 1)
                            pool.dma_start(XN1[bass.ds(U * i + m, 1)].rearrange("o p w -> (o p) w"), xn[:, m % 2])\
                                .then_inc(xn_stored[m % 2], 16)
                            if m >= 2:
                                store_part(i, m - 2)
                        store_part(i, U - 2)
                        store_part(i, U - 1)
                    for b in range(2):
                        pool.wait_ge(xn_stored[b], 16 * NT // 2)
                        pool.wait_ge(gp_stored[b], 16 * NT // 2)

        with ExitStack() as ctx:
            pb = [sbuf(ctx, f"gate_rows{h}", [4 * GM, HH + 2, WW]) for h in range(2)]
            gs = sbuf(ctx, "gate_sel", [4 * GM, 2, 3, 2 * T])
            gb = sbuf(ctx, "gate_bias", [2 * T, 1])
            gt = sbuf(ctx, "gates", [2 * T, PIX])
            gps = psum(ctx, "gate_sum", [2 * T, 2, 512])
            loaded, zeroed, summed, tanhed, stored = (sem(ctx, "p2_" + s) for s in
                                                      ("loaded", "zeroed", "summed", "tanhed", "stored"))
            with nc.Block() as block:
                @block.sync
                def _(sp):
                    for h in range(2):
                        sp.dma_start(pb[h][:, 1:HH + 1, :].rearrange("p r w -> p (r w)"),
                                     GPART[4 * h:4 * h + 4].rearrange("j g w -> (j g) w")).then_inc(loaded, 16)
                    sp.dma_start(gs[:], A["gate_sel"]).then_inc(loaded, 16)
                    sp.dma_start(gb[0:T, :], A["b_l"].partition_broadcast(T)).then_inc(loaded, 16)
                    sp.dma_start(gb[T:2 * T, :], A["b_r"].partition_broadcast(T)).then_inc(loaded, 16)
                    sp.wait_ge(tanhed, KT)
                    sp.dma_start(GATES, gt[:]).then_inc(stored, 16)
                    sp.wait_ge(stored, 16)

                @block.vector
                def _(dve):
                    for h in range(2):
                        for r in (0, HH + 1):
                            dve.memset(pb[h][:, r, :], 0.0).then_inc(zeroed, 1)

                @block.tensor
                def _(pe):
                    pe.wait_ge(loaded, 80)
                    pe.wait_ge(zeroed, 4)
                    for k in range(KT):
                        if k >= 2:
                            pe.wait_ge(tanhed, k - 1)
                        for h in range(2):
                            for dy in range(3):
                                mm = pe.matmul(rows(gps[:, k % 2, 0:TW]), gs[:, h, dy, :],
                                               pb[h][:, ROWS * k + dy:ROWS * k + dy + ROWS, :],
                                               start=(h == 0 and dy == 0), stop=(h == 1 and dy == 2))
                        mm.then_inc(summed, 1)

                @block.scalar
                def _(act):
                    for k in range(KT):
                        act.wait_ge(summed, k + 1)
                        act.activation(gt[:, TW * k:TW * (k + 1)], gps[:, k % 2, 0:TW], ACT.Tanh, bias=gb[:])\
                            .then_inc(tanhed, 1)

        with ExitStack() as ctx:
            gbc = sbuf(ctx, "gate_bc", [P, 2, PIX])
            xn = sbuf(ctx, "xn_again", [P, 2, PIX])
            z = sbuf(ctx, "gated", [P, 2, PIX])
            zeroed = sem(ctx, "p3_zeroed")
            loaded = [sem(ctx, f"p3_loaded{b}") for b in range(2)]
            gated, kept, moved, wrapped = (sem(ctx, "p3_" + s) for s in ("gated", "kept", "moved", "wrapped"))
            stored = [sem(ctx, f"p3_stored{b}") for b in range(2)]
            with nc.Block() as block:
                def pair(j):
                    return X[:, bass.ds(j * KT, KT), :].rearrange("p k w -> p (k w)")

                @block.sync
                def _(sp):
                    sp.wait_ge(zeroed, 1)
                    for i in units(sp, NP // 2):
                        for b in range(2):
                            j = 2 * i + b
                            wait(sp, moved, 2 * i)
                            for a in range(2):
                                for lr in range(2):
                                    r = C * a + HALF * lr
                                    sp.dma_start(gbc[r:r + HALF, b, :],
                                                 GATES[bass.ds(lr * T + 2 * j + a, 1), :]
                                                 .rearrange("o w -> (o w)").partition_broadcast(HALF))\
                                        .then_inc(loaded[b], 16)
                            sp.dma_start(xn[:, b, :].rearrange("p (k w) -> p k w", w=TW),
                                         XN1[bass.ds(j * KT, KT)].rearrange("k p w -> p k w"))\
                                .then_inc(loaded[b], 16)

                @block.gpsimd
                def _(pool):
                    pool.memset(gbc[:], 0.0).then_inc(zeroed, 1)

                @block.vector
                def _(dve):
                    for i in units(dve, NP // 2):
                        for b in range(2):
                            j = 2 * i + b
                            dve.wait_ge(loaded[b], 80 * i + 80)
                            wait(dve, stored[b], 32 * i)
                            dve.tensor_tensor(z[:, b], gbc[:, b], xn[:, b], ALU.mult).then_inc(gated, 1)
                            dve.tensor_tensor(pair(j), pair(j), xn[:, b], ALU.add).then_inc(kept, 1)
                            dve.wait_ge(gated, j + 1)
                            dve.wait_ge(kept, j + 1)
                            dve.tensor_tensor(pair(j), pair(j), z[:, b], ALU.subtract).then_inc(moved, 1)

                @block.scalar
                def _(act):
                    for i in units(act, NP // 2):
                        for b in range(2):
                            act.wait_ge(gated, 2 * i + b + 1)
                            for a in range(2):
                                act.dma_start(Z[bass.ds(4 * i + 2 * b + a + 1, 1)].rearrange("o c w -> (o c) w"),
                                              z[C * a:C * a + 2 * HALF, b, :]).then_inc(stored[b], 16)
                    for b in range(2):
                        act.wait_ge(stored[b], 32 * (NP // 2))
                    act.dma_start(Z[0], Z[T]).then_inc(wrapped, 16)
                    act.dma_start(Z[T + 1], Z[1]).then_inc(wrapped, 16)
                    act.wait_ge(wrapped, 32)

        moe0 = ExitStack()
        LG = sbuf(moe0, "logits", [GW, NT * SUB * 2, E])
        with ExitStack() as ctx:
            zs = sbuf(ctx, "shifted", [P, 2, PIX])
            wg = sbuf(ctx, "w_gate", [P, 2 * E])
            bg = sbuf(ctx, "b_gate", [GW, SUB * 2, E])
            xn = sbuf(ctx, "xn2", [P, 2, TW])
            hi = sbuf(ctx, "hi2", [P, 2, TW], F32R)
            lo = sbuf(ctx, "lo2", [P, 2, TW], F32R)
            lps = psum(ctx, "logit_psum", [P, 2, 512])
            ln = Norm(ctx, "ln2")
            consts, zeroed, added, hi_done, lo_done, lg_ready, lg_done = (
                sem(ctx, "p4_" + s) for s in ("consts", "zeroed", "added", "hi", "lo", "lg_ready", "lg_done"))
            z_in = [sem(ctx, f"p4_z{b}") for b in range(2)]
            stored = [sem(ctx, f"p4_stored{b}") for b in range(2)]
            U = 2 * KT
            with nc.Block() as block:
                @block.gpsimd
                def _(pool):
                    pool.memset(zs[:], 0.0).then_inc(zeroed, 1)
                    for i in units(pool, NT // U):
                        for m in range(U):
                            pool.wait_ge(hi_done, U * i + m + 1)
                            pool.dma_start(SD2[bass.ds(U * i + m, 1), 0].rearrange("o p w -> (o p) w"), hi[:, m % 2].bitcast(F32))\
                                .then_inc(stored[m % 2], 16)
                            pool.wait_ge(lo_done, U * i + m + 1)
                            pool.dma_start(SD2[bass.ds(U * i + m, 1), 1].rearrange("o p w -> (o p) w"), lo[:, m % 2].bitcast(F32))\
                                .then_inc(stored[m % 2], 16)
                    for b in range(2):
                        pool.wait_ge(stored[b], 32 * NT // 2)

                @block.sync
                def _(sp):
                    sp.dma_start(wg[:], A["w_gate"]).then_inc(consts, 16)
                    sp.dma_start(bg[:].rearrange("p s e -> p (s e)"), A["b_gate"].partition_broadcast(GW))\
                        .then_inc(consts, 16)
                    sp.wait_ge(zeroed, 1)
                    for i in units(sp, NT // U):
                        for b in range(2):
                            wait(sp, added, U * i)
                            for a in range(2):
                                for lr in range(2):
                                    r = C * a + HALF * lr
                                    slot = 4 * i + 2 * b + a + 1 + (1 - 2 * lr)
                                    sp.dma_start(zs[r:r + HALF, b, :],
                                                 Z[bass.ds(slot, 1), HALF * lr:HALF * lr + HALF]
                                                 .rearrange("o c w -> (o c) w")).then_inc(z_in[b], 16)

                @block.tensor
                def _(pe):
                    pe.wait_ge(consts, 32)

                    def logits(i, m):
                        pe.wait_ge(ln.normed, U * i + m + 1)
                        wait(pe, lg_done, before(U * i, m))
                        for s in range(SUB):
                            mm = pe.matmul(lps[0:GW, m % 2, s * 2 * E:(s + 1) * 2 * E], xn[:, m % 2, GW * s:GW * (s + 1)],
                                           wg[:], start=True, stop=True)
                        mm.then_inc(lg_ready, 1)

                    for i in units(pe, NT // U):
                        for m in range(U):
                            pe.wait_ge(added, U * i + m + 1)
                            ln.pe_centre(pe, U * i, m, tile(X, U * i + m))
                            if m >= 1:
                                ln.pe_var(pe, U * i, m - 1)
                            if m >= 2:
                                logits(i, m - 2)
                        ln.pe_var(pe, U * i, U - 1)
                        logits(i, U - 2)
                        logits(i, U - 1)

                @block.scalar
                def _(act):
                    for i in units(act, NT // U):
                        for m in range(U):
                            ln.act_square(act, U * i, m)
                            if m >= 1:
                                ln.act_seed(act, U * i, m - 1, 1)
                        ln.act_seed(act, U * i, U - 1, 1)

                @block.vector
                def _(dve):
                    dve.wait_ge(consts, 32)

                    def add_shifted(i, m):
                        if m % KT == 0:
                            dve.wait_ge(z_in[m // KT], 64 * i + 64)
                        x = tile(X, U * i + m)
                        dve.tensor_tensor(x, x, zs[:, m // KT, (m % KT) * TW:(m % KT + 1) * TW], ALU.add)\
                            .then_inc(added, 1)

                    def keep_logits(i, m):
                        dve.wait_ge(lg_ready, U * i + m + 1)
                        dve.tensor_tensor(LG[:, bass.ds((U * i + m) * SUB * 2, SUB * 2), :],
                                          lps[0:GW, m % 2, 0:SUB * 2 * E].rearrange("p (s e) -> p s e", e=E),
                                          bg[:], ALU.add).then_inc(lg_done, 1)

                    for i in units(dve, NT // U):
                        add_shifted(i, 0)
                        add_shifted(i, 1)
                        for m in range(U):
                            if m + 2 < U:
                                add_shifted(i, m + 2)
                            wait(dve, lg_ready, before(U * i, m))
                            ln.dve_norm(dve, U * i, m, EPS_T, xn[:, m % 2])
                            dve.wait_ge(ln.normed, U * i + m + 1)
                            wait(dve, stored[m % 2], 32 * (KT * i + m // 2))
                            dve.tensor_copy(hi[:, m % 2], xn[:, m % 2]).then_inc(hi_done, 1)
                            dve.wait_ge(hi_done, U * i + m + 1)
                            dve.tensor_tensor(lo[:, m % 2], xn[:, m % 2], hi[:, m % 2].bitcast(F32), ALU.subtract)\
                                .then_inc(lo_done, 1)
                            if m >= 2:
                                keep_logits(i, m - 2)
                        keep_logits(i, U - 2)
                        keep_logits(i, U - 1)

        with ExitStack() as ctx:
            G = NT * SUB * 2
            rank = sbuf(ctx, "rank", [GW, G, E])
            gt = sbuf(ctx, "beats", [GW, G, E])
            best = sbuf(ctx, "best", [GW, 2, G])
            w12 = sbuf(ctx, "w12", [GW, 2, G])
            th = sbuf(ctx, "th", [GW, 2, G])
            ident = sbuf(ctx, "ident", [P, P])
            wst = sbuf(ctx, "w_stage", [GW, 2, SUB * 2, E])
            wtt = sbuf(ctx, "wtt", [2 * E, 2, TW])
            wps = psum(ctx, "w_psum", [P, 2, 512])
            s_v, s_th, s_tr, s_cp, s_id, s_st = (sem(ctx, "p5_" + s) for s in ("v", "th", "tr", "cp", "id", "st"))
            stored = [sem(ctx, f"p5_stored{b}") for b in range(2)]
            steps = [0]
            with nc.Block() as block:
                @block.vector
                def _(dve):
                    def link(ins):
                        steps[0] += 1
                        ins.then_inc(s_v, 1)
                        dve.wait_ge(s_v, steps[0])

                    for e in range(E):
                        ms = dve.memset(rank[:, :, e], float(e))
                    link(ms)
                    for s in range(1, E):
                        lo_, hi_ = slice(0, E - s), slice(s, E)
                        link(dve.tensor_tensor(gt[:, :, lo_], LG[:, :, hi_], LG[:, :, lo_], ALU.is_gt))
                        link(dve.tensor_tensor(rank[:, :, lo_], rank[:, :, lo_], gt[:, :, lo_], ALU.add))
                        link(dve.tensor_tensor(rank[:, :, hi_], rank[:, :, hi_], gt[:, :, lo_], ALU.subtract))
                    for k in range(2):
                        link(dve.scalar_tensor_tensor(out=gt[:], in0=rank[:], scalar=float(k), in1=LG[:],
                                                      op0=ALU.is_equal, op1=ALU.mult))
                        link(dve.tensor_reduce(best[:, k, :], gt[:], AX.X, ALU.add))
                    link(dve.tensor_tensor(th[:, 0, :], best[:, 0, :], best[:, 1, :], ALU.subtract))
                    dve.wait_ge(s_th, 1)
                    link(dve.tensor_scalar(w12[:, 0, :], th[:, 1, :], 0.5, 0.5, ALU.mult, ALU.add))
                    link(dve.tensor_scalar(w12[:, 1, :], th[:, 1, :], -0.5, 0.5, ALU.mult, ALU.add))
                    for k in range(2):
                        dst = gt if k == 0 else LG
                        link(dve.scalar_tensor_tensor(out=dst[:], in0=rank[:], scalar=float(k),
                                                      in1=w12[:, k, :].unsqueeze(2).broadcast_to([GW, G, E]),
                                                      op0=ALU.is_equal, op1=ALU.mult))
                    for i in units(dve, NT // 2):
                        for b in range(2):
                            g = bass.ds((2 * i + b) * SUB * 2, SUB * 2)
                            wait(dve, s_tr, 2 * i)
                            dve.tensor_tensor(wst[:, b], LG[:, g, :], gt[:, g, :], ALU.add).then_inc(s_st, 1)

                before_tanh = 1 + 3 * (E - 1) + 4 + 1

                @block.scalar
                def _(act):
                    act.wait_ge(s_v, before_tanh)
                    act.activation(th[:, 1, :], th[:, 0, :], ACT.Tanh, scale=0.5).then_inc(s_th, 1)
                    for i in units(act, NT // 2):
                        for b in range(2):
                            act.wait_ge(s_tr, 2 * i + b + 1)
                            wait(act, stored[b], 16 * i)
                            act.activation(wtt[:, b], wps[0:2 * E, b, 0:TW], ACT.Copy).then_inc(s_cp, 1)

                @block.tensor
                def _(pe):
                    pe.wait_ge(s_id, 16)
                    for i in units(pe, NT // 2):
                        for b in range(2):
                            wait(pe, s_cp, 2 * i)
                            pe.wait_ge(s_st, 2 * i + b + 1)
                            for s in range(SUB):
                                w = wst[:, b, 2 * s:2 * s + 2, :].rearrange("p s e -> p (s e)")
                                tr = pe.transpose(wps[0:2 * E, b, GW * s:GW * (s + 1)], w, ident[0:GW, 0:GW])
                            tr.then_inc(s_tr, 1)

                @block.sync
                def _(sp):
                    sp.dma_start(ident[:], A["ident"]).then_inc(s_id, 16)
                    for i in units(sp, NT // 2):
                        for b in range(2):
                            sp.wait_ge(s_cp, 2 * i + b + 1)
                            sp.dma_start(WT[bass.ds(2 * i + b, 1)].rearrange("o r w -> (o r) w"), wtt[:, b])\
                                .then_inc(stored[b], 16)
                    for b in range(2):
                        sp.wait_ge(stored[b], 16 * NT // 2)
        moe0.close()

        with ExitStack() as ctx:
            w1raw = sbuf(ctx, "w1raw", [P, E * H0])
            w1hi = sbuf(ctx, "w1hi", [P, E * H0], F32R)
            w1lo = sbuf(ctx, "w1lo", [P, E * H0], F32R)
            w2 = sbuf(ctx, "w2", [P, E, CH0, C])
            b1 = sbuf(ctx, "b1", [P, E, CH0])
            b2 = sbuf(ctx, "b2", [P, E])
            S = sbuf(ctx, "tokens", [P, 2, 2, TW], F32R)
            WB = sbuf(ctx, "w_bc", [P, 2, E, TW])
            hs = sbuf(ctx, "hidden", [P, 2, 2, TW])
            pr = sbuf(ctx, "weighted", [P, 2, TW])
            hp = psum(ctx, "hidden_psum", [P, 2, 2, 512])
            yp = psum(ctx, "y_psum", [P, 2, 512])
            consts, whi, wlo, up_done, gelu_done, down_done, weighted, summed = (
                sem(ctx, "p6_" + s) for s in ("consts", "whi", "wlo", "up", "gelu", "down", "weighted", "summed"))
            tok_in = [sem(ctx, f"p6_tok{b}") for b in range(2)]
            SN = E * CH0
            PER = 96

            with nc.Block() as block:
                @block.sync
                def _(sp):
                    def load(n, b):
                        for a in range(2):
                            for part in range(2):
                                sp.dma_start(S[C * part:C * part + C, b, a, :].bitcast(F32),
                                             SD2[bass.ds(n, 1), part, C * a:C * a + C].rearrange("o p w -> (o p) w"))\
                                    .then_inc(tok_in[b], 16)
                            sp.dma_start(WB[C * a:C * a + C, b], WT[bass.ds(n, 1), E * a:E * a + E]
                                         .rearrange("o e w -> (o e) w").partition_broadcast(C)).then_inc(tok_in[b], 16)

                    sp.dma_start(w1raw[:], A["w1"]).then_inc(consts, 16)
                    sp.dma_start(w2[:], A["w2"]).then_inc(consts, 16)
                    sp.dma_start(b1[:], A["b1"]).then_inc(consts, 16)
                    sp.dma_start(b2[:], A["b2"]).then_inc(consts, 16)
                    load(0, 0)
                    load(1, 1)
                    for i in units(sp, NT // 2 - 1):
                        for b in range(2):
                            n = 2 * i + b
                            sp.wait_ge(up_done, SN * n + SN)
                            sp.wait_ge(weighted, E * n + E)
                            load(n + 2, b)

                @block.tensor
                def _(pe):
                    pe.wait_ge(consts, 64)
                    pe.wait_ge(wlo, 1)

                    def up(i, b, s, first=False):
                        if s == 0:
                            pe.wait_ge(tok_in[b], PER * i + PER)
                        if not first:
                            wait(pe, gelu_done, SN * (2 * i + b) + s - 1)
                        for a in range(2):
                            o = hp[:, s % 2, a, 0:TW]
                            pe.matmul(o, w1hi[:, s * P:(s + 1) * P], S[:, b, a, :], start=True, stop=False)
                            mm = pe.matmul(o, w1lo[:, s * P:(s + 1) * P], S[:, b, a, :], start=False, stop=True)
                        mm.then_inc(up_done, 1)

                    def down(i, b, s):
                        e, c = divmod(s, CH0)
                        pe.wait_ge(gelu_done, SN * (2 * i + b) + s + 1)
                        if c == 0:
                            wait(pe, weighted, E * 2 * i + max(E * b + e - 1, 0))
                        for a in range(2):
                            mm = pe.matmul(yp[C * a:C * a + C, e % 2, 0:TW], w2[:, e, c, :], hs[:, s % 2, a, :],
                                           start=(c == 0), stop=(c == CH0 - 1))
                        mm.then_inc(down_done, 1)

                    def two_tiles(i, last):
                        for k in range(2 * SN):
                            if k + 1 < 2 * SN:
                                up(i, (k + 1) // SN, (k + 1) % SN)
                            elif not last:
                                up(i + 1, 0, 0)
                            down(i, k // SN, k % SN)

                    up(0, 0, 0, first=True)
                    for i in units(pe, NT // 2 - 1):
                        two_tiles(i, False)
                    two_tiles(NT // 2 - 1, True)

                @block.scalar
                def _(act):
                    act.wait_ge(consts, 64)
                    for i in units(act, NT // 2):
                        for k in range(2 * SN):
                            e, c = divmod(k % SN, CH0)
                            act.wait_ge(up_done, 2 * SN * i + k + 1)
                            wait(act, down_done, before(2 * SN * i, k))
                            act.activation(hs[:, k % 2], hp[:, k % 2, :, 0:TW], ACT.Gelu, bias=b1[:, e, c:c + 1])\
                                .then_inc(gelu_done, 1)

                @block.vector
                def _(dve):
                    dve.wait_ge(consts, 64)
                    dve.tensor_copy(w1hi[:], w1raw[:]).then_inc(whi, 1)
                    dve.wait_ge(whi, 1)
                    dve.tensor_tensor(w1lo[:], w1raw[:], w1hi[:].bitcast(F32), ALU.subtract).then_inc(wlo, 1)
                    for i in units(dve, NT // 2):
                        for b in range(2):
                            x = tile(X, 2 * i + b)
                            dve.wait_ge(tok_in[b], PER * i + PER)
                            for e in range(E):
                                dve.wait_ge(down_done, SN * (2 * i + b) + CH0 * (e + 1))
                                dve.scalar_tensor_tensor(out=pr[:, e % 2], in0=yp[:, e % 2, 0:TW], scalar=b2[:, e:e + 1],
                                                         in1=WB[:, b, e, :], op0=ALU.add, op1=ALU.mult)\
                                    .then_inc(weighted, 1)
                                dve.wait_ge(weighted, E * (2 * i + b) + e + 1)
                                if e or b:
                                    dve.wait_ge(summed, E * (2 * i + b) + e)
                                dve.tensor_tensor(x, x, pr[:, e % 2], ALU.add).then_inc(summed, 1)

        with ExitStack() as ctx:
            cwraw = sbuf(ctx, "conv_raw", [P, 9, P])
            cw = sbuf(ctx, "conv_sign", [P, 9, P], F32R)
            sf = sbuf(ctx, "factor", [P, 1])
            hp_ = sbuf(ctx, "pad_hi", [P, 2, HH + 2, PADW], F32R)
            lp_ = sbuf(ctx, "pad_lo", [P, 2, HH + 2, PADW], F32R)
            x3n = sbuf(ctx, "xn3", [P, 2, TW])
            xn = sbuf(ctx, "xn4", [P, 2, TW])
            hi = sbuf(ctx, "hi4", [P, 2, TW], F32R)
            lo = sbuf(ctx, "lo4", [P, 2, TW], F32R)
            cps = psum(ctx, "conv_psum", [P, 2, 512])
            ln = Norm(ctx, "ln34")
            w1raw = sbuf(ctx, "w1raw_l1", [P, E, F1])
            w1s = sbuf(ctx, "w1split_l1", [P, E, 2, F1], F32R)
            consts, signed, zeroed, p_hi, p_lo, conv_done, x3_done, hi_done, lo_done, whi, wlo, wst = (
                sem(ctx, "p7_" + s) for s in ("consts", "signed", "zeroed", "p_hi", "p_lo", "conv", "x3", "hi", "lo",
                                              "whi", "wlo", "wst"))
            stored = [sem(ctx, f"p7_stored{b}") for b in range(2)]
            U = 4 * KT
            V = 2 * KT
            with nc.Block() as block:
                @block.sync
                def _(sp):
                    sp.dma_start(cwraw[:], A["conv_w"]).then_inc(consts, 16)
                    for a in range(2):
                        sp.dma_start(sf[C * a:C * a + C, :], A["factor"]).then_inc(consts, 16)
                    sp.dma_start(w1raw[:], A["w1_l1"]).then_inc(consts, 16)
                    sp.wait_ge(wlo, 1)
                    sp.dma_start(W1D.rearrange("e p s f -> p e (s f)"), w1s[:].bitcast(F32).rearrange("p e s f -> p e (s f)"))\
                        .then_inc(wst, 16)
                    sp.wait_ge(wst, 16)

                @block.gpsimd
                def _(pool):
                    pool.memset(hp_[:].bitcast(F32), 0.0).then_inc(zeroed, 1)
                    pool.memset(lp_[:].bitcast(F32), 0.0).then_inc(zeroed, 1)
                    for i in units(pool, NT // V):
                        for v in range(V):
                            n = V * i + v
                            pool.wait_ge(ln.normed, U * i + 2 * KT * (v // KT) + KT + v % KT + 1)
                            pool.dma_start(XN4[bass.ds(n, 1)].rearrange("o p w -> (o p) w"), xn[:, v % 2])\
                                .then_inc(stored[v % 2], 16)
                            pool.wait_ge(hi_done, n + 1)
                            pool.dma_start(SD4[bass.ds(n, 1), 0].rearrange("o p w -> (o p) w"), hi[:, v % 2].bitcast(F32))\
                                .then_inc(stored[v % 2], 16)
                            pool.wait_ge(lo_done, n + 1)
                            pool.dma_start(SD4[bass.ds(n, 1), 1].rearrange("o p w -> (o p) w"), lo[:, v % 2].bitcast(F32))\
                                .then_inc(stored[v % 2], 16)
                    for b in range(2):
                        pool.wait_ge(stored[b], 48 * NT // 2)

                @block.tensor
                def _(pe):
                    pe.wait_ge(signed, 1)
                    pe.wait_ge(zeroed, 2)

                    def conv(i, b, k):
                        v = KT * b + k
                        pe.wait_ge(p_lo, V * i + KT * b + min(k + 2, KT))
                        wait(pe, x3_done, before(V * i, v))
                        o = rows(cps[:, v % 2, 0:TW])
                        for t9 in range(9):
                            dy, dx = divmod(t9, 3)
                            for n_, src in enumerate((hp_, lp_)):
                                mm = pe.matmul(o, cw[:, t9, :], src[:, b, ROWS * k + dy:ROWS * k + dy + ROWS, dx:dx + WW],
                                               start=(t9 == 0 and n_ == 0), stop=(t9 == 8 and n_ == 1))
                        mm.then_inc(conv_done, 1)

                    for i in units(pe, NT // V):
                        for b in range(2):
                            m0 = 2 * KT * b
                            for k in range(KT):
                                ln.pe_centre(pe, U * i, m0 + k, tile(X, V * i + KT * b + k))
                                if k >= 1:
                                    ln.pe_var(pe, U * i, m0 + k - 1)
                            ln.pe_var(pe, U * i, m0 + KT - 1)
                            for k in range(KT + 2):
                                if k < KT:
                                    conv(i, b, k)
                                if 1 <= k < KT + 1:
                                    pe.wait_ge(x3_done, V * i + KT * b + k)
                                    ln.pe_centre(pe, U * i, m0 + KT + k - 1, tile(X, V * i + KT * b + k - 1))
                                if k >= 2:
                                    ln.pe_var(pe, U * i, m0 + KT + k - 2)

                @block.scalar
                def _(act):
                    act.wait_ge(consts, 64)
                    act.activation(cw[:], cwraw[:], ACT.Sign).then_inc(signed, 1)
                    for i in units(act, NT // V):
                        for g in range(4):
                            for m in range(KT * g, KT * g + KT):
                                ln.act_square(act, U * i, m)
                                if m > KT * g:
                                    ln.act_seed(act, U * i, m - 1, g % 2)
                            ln.act_seed(act, U * i, KT * g + KT - 1, g % 2)

                @block.vector
                def _(dve):
                    dve.wait_ge(consts, 64)
                    dve.wait_ge(zeroed, 2)
                    dve.tensor_copy(w1s[:, :, 0, :], w1raw[:]).then_inc(whi, 1)
                    dve.wait_ge(whi, 1)
                    dve.tensor_tensor(w1s[:, :, 1, :], w1raw[:], w1s[:, :, 0, :].bitcast(F32), ALU.subtract)\
                        .then_inc(wlo, 1)

                    def x3(i, b, k):
                        v = KT * b + k
                        dve.wait_ge(conv_done, V * i + v + 1)
                        x = tile(X, V * i + v)
                        dve.scalar_tensor_tensor(out=x, in0=cps[:, v % 2, 0:TW], scalar=sf[:, 0:1], in1=x,
                                                 op0=ALU.mult, op1=ALU.add).then_inc(x3_done, 1)

                    for i in units(dve, NT // V):
                        for b in range(2):
                            for k in range(KT):
                                m, n = 2 * KT * b + k, V * i + KT * b + k
                                ln.dve_norm(dve, U * i, m, EPS_C, x3n[:, m % 2])
                                dve.wait_ge(ln.normed, U * i + m + 1)
                                src = rows(x3n[:, m % 2])
                                r = slice(ROWS * k + 1, ROWS * k + 1 + ROWS)
                                if k == 0:
                                    wait(dve, conv_done, V * i)
                                dve.tensor_copy(hp_[:, b, r, 1:WW + 1], src).then_inc(p_hi, 1)
                                dve.wait_ge(p_hi, n + 1)
                                dve.tensor_tensor(lp_[:, b, r, 1:WW + 1], src, hp_[:, b, r, 1:WW + 1].bitcast(F32),
                                                  ALU.subtract).then_inc(p_lo, 1)
                            x3(i, b, 0)
                            for k in range(KT):
                                m, v, n = 2 * KT * b + KT + k, KT * b + k, V * i + KT * b + k
                                if k + 1 < KT:
                                    x3(i, b, k + 1)
                                wait(dve, stored[v % 2], 48 * (KT * i + v // 2))
                                ln.dve_norm(dve, U * i, m, EPS_T, xn[:, v % 2], accum=MSUM[:, bass.ds(n, 1)])
                                dve.wait_ge(ln.normed, U * i + m + 1)
                                dve.tensor_copy(hi[:, v % 2], xn[:, v % 2]).then_inc(hi_done, 1)
                                dve.wait_ge(hi_done, n + 1)
                                dve.tensor_tensor(lo[:, v % 2], xn[:, v % 2], hi[:, v % 2].bitcast(F32), ALU.subtract)\
                                    .then_inc(lo_done, 1)

        with ExitStack() as ctx:
            wr = sbuf(ctx, "w_route", [P, E])
            br = sbuf(ctx, "b_route", [NP, 2, E])
            ones = sbuf(ctx, "ones8", [NP, NP])
            ms = sbuf(ctx, "mean", [P, NP])
            ms2 = sbuf(ctx, "mean_scaled", [P, NP])
            names = ("lg", "shift", "ex", "rw", "rs", "ex2", "rank", "beats", "tmp", "iota")
            t3 = {n: sbuf(ctx, "r_" + n, [NP, 2, E]) for n in names}
            mx, sm, ri = (sbuf(ctx, "r_" + n, [NP, 2]) for n in ("mx", "sm", "ri"))
            loads, scale = sbuf(ctx, "r_loads", [NP, E]), sbuf(ctx, "r_scale", [NP, E])
            pick = sbuf(ctx, "r_pick", [NP, 2, 2])
            pidx = sbuf(ctx, "r_pidx", [NP, 2, 2])
            pidi = sbuf(ctx, "r_pidi", [NP, 2, 2], I32)
            dd, ee, wse = (sbuf(ctx, "r_" + n, [NP, 2]) for n in ("dd", "ee", "wse"))
            wsel = sbuf(ctx, "r_wsel", [NP, 2, 2])
            lp = [psum(ctx, f"r_lg{a}", [NP, 512]) for a in range(2)]
            ldp = psum(ctx, "r_ldp", [NP, 512])
            consts, s_v, s_mm, s_a, s_out = (sem(ctx, "p8_" + s) for s in ("consts", "v", "mm", "a", "out"))
            steps, marks = [0], {}
            with nc.Block() as block:
                @block.vector
                def _(dve):
                    def link(ins, mark=None):
                        steps[0] += 1
                        ins.then_inc(s_v, 1)
                        dve.wait_ge(s_v, steps[0])
                        marks[mark] = steps[0]

                    def bc(x):
                        return x.unsqueeze(2).broadcast_to([NP, 2, E])

                    def shifted_exp(src, dst, mark, count):
                        link(dve.tensor_reduce(mx[:], src[:], AX.X, ALU.max))
                        link(dve.tensor_tensor(t3["shift"][:], src[:], bc(mx[:]), ALU.subtract), mark)
                        dve.wait_ge(s_a, count)
                        link(dve.tensor_reduce(sm[:], t3["ex"][:], AX.X, ALU.add))
                        link(dve.reciprocal(ri[:], sm[:]))
                        link(dve.tensor_tensor(dst[:], t3["ex"][:], bc(ri[:]), ALU.mult))

                    dve.wait_ge(consts, 48)
                    link(dve.memset(ones[:], 1.0))
                    for e in range(E):
                        mset = dve.memset(t3["iota"][:, :, e], float(e))
                    link(mset)
                    link(dve.tensor_copy(t3["rank"][:], t3["iota"][:]))
                    link(dve.tensor_reduce(ms[:], MSUM[:].rearrange("p (j k) -> p j k", k=KT), AX.X, ALU.add))
                    link(dve.tensor_scalar(ms2[:], ms[:], 1.0 / PIX, None, ALU.mult), "mean")
                    dve.wait_ge(s_mm, 1)
                    for a in range(2):
                        link(dve.tensor_tensor(t3["lg"][:, a], lp[a][:, 0:E], br[:, a], ALU.add))
                    shifted_exp(t3["lg"], t3["rw"], "exp1", 1)
                    marks["rw"] = steps[0]
                    dve.wait_ge(s_mm, 2)
                    link(dve.tensor_scalar(loads[:], ldp[:, 0:E], float(PIX), None, ALU.mult))
                    link(dve.reciprocal(scale[:], loads[:]))
                    link(dve.tensor_scalar(scale[:], scale[:], CAPACITY, 1.0, ALU.mult, ALU.min))
                    for a in range(2):
                        link(dve.tensor_tensor(t3["lg"][:, a], t3["rw"][:, a], scale[:], ALU.mult))
                    shifted_exp(t3["lg"], t3["rs"], "exp2", 2)
                    for s in range(1, E):
                        l_, h_ = slice(0, E - s), slice(s, E)
                        rs, rk, bt = t3["rs"], t3["rank"], t3["beats"]
                        link(dve.tensor_tensor(bt[:, :, l_], rs[:, :, h_], rs[:, :, l_], ALU.is_gt))
                        link(dve.tensor_tensor(rk[:, :, l_], rk[:, :, l_], bt[:, :, l_], ALU.add))
                        link(dve.tensor_tensor(rk[:, :, h_], rk[:, :, h_], bt[:, :, l_], ALU.subtract))
                    for k in range(2):
                        for src, dst in ((t3["rs"], pick), (t3["iota"], pidx)):
                            link(dve.scalar_tensor_tensor(out=t3["tmp"][:], in0=t3["rank"][:], scalar=float(k),
                                                          in1=src[:], op0=ALU.is_equal, op1=ALU.mult))
                            link(dve.tensor_reduce(dst[:, :, k], t3["tmp"][:], AX.X, ALU.add))
                    link(dve.tensor_copy(pidi[:], pidx[:]))
                    link(dve.tensor_tensor(dd[:], pick[:, :, 1], pick[:, :, 0], ALU.subtract), "exp3")
                    dve.wait_ge(s_a, 3)
                    link(dve.tensor_scalar(wse[:], ee[:], 1.0, None, ALU.add))
                    link(dve.reciprocal(wsel[:, :, 0], wse[:]))
                    link(dve.tensor_tensor(wsel[:, :, 1], wsel[:, :, 0], ee[:], ALU.mult), "out")

                @block.scalar
                def _(act):
                    for n, mark in enumerate(("exp1", "exp2")):
                        act.wait_ge(s_v, marks[mark])
                        act.activation(t3["ex"][:], t3["shift"][:], ACT.Exp).then_inc(s_a, 1)
                    act.wait_ge(s_v, marks["exp3"])
                    act.activation(ee[:], dd[:], ACT.Exp).then_inc(s_a, 1)

                @block.tensor
                def _(pe):
                    pe.wait_ge(consts, 48)
                    pe.wait_ge(s_v, marks["mean"])
                    for a in range(2):
                        mm = pe.matmul(lp[a][:, 0:E], ms2[C * a:C * a + C, :], wr[C * a:C * a + C, :],
                                       start=True, stop=True)
                    mm.then_inc(s_mm, 1)
                    pe.wait_ge(s_v, marks["rw"])
                    for a in range(2):
                        mm = pe.matmul(ldp[:, 0:E], ones[:], t3["rw"][:, a], start=(a == 0), stop=(a == 1))
                    mm.then_inc(s_mm, 1)

                @block.sync
                def _(sp):
                    sp.dma_start(wr[0:C, :], A["w_route"]).then_inc(consts, 16)
                    sp.dma_start(wr[C:P, :], A["w_route"]).then_inc(consts, 16)
                    sp.dma_start(br[:].rearrange("p a e -> p (a e)"), A["b_route"].partition_broadcast(NP))\
                        .then_inc(consts, 16)
                    sp.wait_ge(s_v, marks["out"])
                    sp.dma_start(IDX, pidi[:].rearrange("p a s -> p (a s)")).then_inc(s_out, 16)
                    sp.dma_start(WSEL, wsel[:].rearrange("p a s -> p (a s)")).then_inc(s_out, 16)
                    sp.wait_ge(s_out, 32)

        with ExitStack() as ctx:
            w1s = sbuf(ctx, "w1sel", [P, 2, 4, 2, F1], F32R)
            w2r = sbuf(ctx, "w2raw", [P, 2, 4, C])
            w2s = sbuf(ctx, "w2sel", [P, 2, 4, C])
            b1s = sbuf(ctx, "b1sel", [P, 2, 4])
            b2r = sbuf(ctx, "b2raw", [P, 2, 2])
            b2t = sbuf(ctx, "b2tmp", [P, 2, 1])
            b2s = sbuf(ctx, "b2sel", [P, 2, 1])
            wse = sbuf(ctx, "w_all", [P, NP, 4])
            wsh = sbuf(ctx, "w_half", [P, NP, 2])
            gam = sbuf(ctx, "gamma", [P, 1])
            bet = sbuf(ctx, "beta", [P, 1])
            idr = sbuf(ctx, "idx", [1, NP * 4], I32)
            S = sbuf(ctx, "tokens4", [P, 2, 2, TW], F32R)
            xn = sbuf(ctx, "xn4_in", [P, 2, TW])
            hs = sbuf(ctx, "hidden1", [P, 2, 4, TW])
            u = sbuf(ctx, "u", [P, KT, TW])
            nrm = sbuf(ctx, "ln5", [P, 2, TW])
            o1 = sbuf(ctx, "scaled", [P, 2, TW])
            o2 = sbuf(ctx, "out_tile", [P, 2, TW])
            hp = psum(ctx, "hidden1_psum", [P, 2, 512])
            yp = psum(ctx, "y1_psum", [P, 2, 512])
            ln = Norm(ctx, "ln5")
            consts, idx_in, w2_done, b2_a, b2_done, up_done, gelu_done, down_done, u_done, scaled, out_done = (
                sem(ctx, "p9_" + s) for s in ("consts", "idx", "w2", "b2a", "b2", "up", "gelu", "down", "u",
                                              "scaled", "out"))
            w_in = [sem(ctx, f"p9_w{b}") for b in range(2)]
            tok_in = [sem(ctx, f"p9_tok{b}") for b in range(2)]
            out_st = [sem(ctx, f"p9_out{b}") for b in range(2)]
            U = 2 * KT
            WIN = 16 * (4 * 3 + 4)
            TIN = 80
            with nc.Block() as block:
                @block.gpsimd
                def _(pool):
                    def load(i, v):
                        n, b = U * i + v, v % 2
                        for a in range(2):
                            for part in range(2):
                                pool.dma_start(S[C * part:C * part + C, b, a, :].bitcast(F32),
                                               SD4[bass.ds(n, 1), part, C * a:C * a + C].rearrange("o p w -> (o p) w"))\
                                    .then_inc(tok_in[b], 16)
                        pool.dma_start(xn[:, b, :], XN4[bass.ds(n, 1)].rearrange("o p w -> (o p) w"))\
                            .then_inc(tok_in[b], 16)

                    for i in units(pool, NT // U):
                        for v in range(U):
                            wait(pool, up_done, 4 * (U * i + max(v - 1, 0)))
                            wait(pool, u_done, before(U * i, v))
                            load(i, v)

                @block.sync
                def _(sp):
                    sp.dma_start(idr[:], IDX.rearrange("(o j) s -> o (j s)", o=1)).then_inc(idx_in, 16)
                    sp.dma_start(wse[:], WSEL.rearrange("j s -> (j s)").partition_broadcast(P)
                                 .rearrange("p (j s) -> p j s", s=4)).then_inc(consts, 16)
                    for a in range(2):
                        sp.dma_start(wsh[C * a:C * a + C], WSEL[:, 2 * a:2 * a + 2].partition_broadcast(C))\
                            .then_inc(consts, 16)
                        sp.dma_start(gam[C * a:C * a + C, :], A["gamma"]).then_inc(consts, 16)
                        sp.dma_start(bet[C * a:C * a + C, :], A["beta"]).then_inc(consts, 16)
                    sp.wait_ge(idx_in, 16)

                    def load_w(i, b):
                        for q in range(4):
                            e = sp.value_load(idr[0:1, bass.ds((2 * i + b) * 4 + q, 1)], min_val=0, max_val=E - 1)
                            sp.dma_start(w1s[:, b, q].bitcast(F32), W1D[bass.ds(e, 1)].rearrange("o p s f -> (o p) s f"))\
                                .then_inc(w_in[b], 16)
                            sp.dma_start(w2r[:, b, q], A["w2_l1"][bass.ds(e, 1)].rearrange("o f c -> (o f) c"))\
                                .then_inc(w_in[b], 16)
                            sp.dma_start(b1s[:, b, q:q + 1], A["b1_l1"][bass.ds(e, 1)].rearrange("o f u -> (o f) u"))\
                                .then_inc(w_in[b], 16)
                            a, s = divmod(q, 2)
                            sp.dma_start(b2r[C * a:C * a + C, b, s:s + 1],
                                         A["b2_l1"][bass.ds(e, 1)].rearrange("o c u -> (o c) u")).then_inc(w_in[b], 16)

                    def wait_w(i, b):
                        p = 2 * i + b
                        wait(sp, gelu_done, 4 * KT * (p - 1))
                        wait(sp, w2_done, p - 1)
                        wait(sp, b2_done, p - 1)

                    def store(i, b):
                        for k in range(KT):
                            v = KT * b + k
                            sp.wait_ge(out_done, U * i + v + 1)
                            sp.dma_start(out[bass.ds(2 * i + b, 1), :, TW * k:TW * (k + 1)]
                                         .rearrange("o p w -> (o p) w"), o2[:, v % 2]).then_inc(out_st[v % 2], 16)

                    def two_pairs(i, last):
                        wait_w(i, 1)
                        load_w(i, 1)
                        store(i, 0)
                        if not last:
                            wait_w(i + 1, 0)
                            load_w(i + 1, 0)
                        store(i, 1)

                    load_w(0, 0)
                    for i in units(sp, NP // 2 - 1):
                        two_pairs(i, False)
                    two_pairs(NP // 2 - 1, True)
                    for b in range(2):
                        sp.wait_ge(out_st[b], 16 * NT // 2)

                @block.tensor
                def _(pe):
                    def up(i, v):
                        b, t = v // KT, v % 2
                        pe.wait_ge(tok_in[t], TIN * (KT * i + v // 2) + TIN)
                        for q in range(4):
                            a = q // 2
                            g = 4 * (U * i + v) + q
                            wait(pe, gelu_done, 4 * U * i + max(4 * v + q - 1, 0))
                            pe.matmul(hp[:, q % 2, 0:TW], w1s[:, b, q, 0, :], S[:, t, a, :], start=True, stop=False)
                            pe.matmul(hp[:, q % 2, 0:TW], w1s[:, b, q, 1, :], S[:, t, a, :], start=False, stop=True)\
                                .then_inc(up_done, 1)

                    def down(i, v):
                        b, t = v // KT, v % 2
                        pe.wait_ge(gelu_done, 4 * (U * i + v) + 4)
                        wait(pe, u_done, before(U * i, v))
                        if v % KT == 0:
                            pe.wait_ge(w2_done, 2 * i + b + 1)
                        for s in range(2):
                            for a in range(2):
                                mm = pe.matmul(yp[C * a:C * a + C, t, 0:TW], w2s[:, b, 2 * a + s, :],
                                               hs[:, t, 2 * a + s, :], start=(s == 0), stop=(s == 1))
                        mm.then_inc(down_done, 1)

                    for i in units(pe, NP // 2):
                        for b in range(2):
                            pe.wait_ge(w_in[b], WIN * i + WIN)
                            for k in range(KT):
                                up(i, KT * b + k)
                                if k >= 1:
                                    down(i, KT * b + k - 1)
                            down(i, KT * b + KT - 1)
                            for k in range(KT):
                                pe.wait_ge(u_done, U * i + KT * b + k + 1)
                                ln.pe_centre(pe, U * i, KT * b + k, u[:, k])
                                if k >= 1:
                                    ln.pe_var(pe, U * i, KT * b + k - 1)
                            ln.pe_var(pe, U * i, KT * b + KT - 1)

                @block.scalar
                def _(act):
                    for i in units(act, NP // 2):
                        for b in range(2):
                            act.wait_ge(w_in[b], WIN * i + WIN)
                            for k in range(KT):
                                v = KT * b + k
                                wait(act, down_done, before(U * i, v))
                                for q in range(4):
                                    act.wait_ge(up_done, 4 * (U * i + v) + q + 1)
                                    act.activation(hs[:, v % 2, q], hp[:, q % 2, 0:TW], ACT.Gelu,
                                                   bias=b1s[:, b, q:q + 1]).then_inc(gelu_done, 1)
                            for k in range(KT):
                                ln.act_square(act, U * i, KT * b + k)
                                if k >= 1:
                                    ln.act_seed(act, U * i, KT * b + k - 1, 1)
                            ln.act_seed(act, U * i, KT * b + KT - 1, 1)

                @block.vector
                def _(dve):
                    dve.wait_ge(consts, 7 * 16)
                    for i in units(dve, NP // 2):
                        for b in range(2):
                            j = 2 * i + b
                            dve.wait_ge(w_in[b], WIN * i + WIN)
                            wait(dve, down_done, U * i)
                            for q in range(4):
                                ts = dve.tensor_scalar(w2s[:, b, q], w2r[:, b, q],
                                                       wse[:, bass.ds(j, 1), q], None, ALU.mult)
                            ts.then_inc(w2_done, 1)
                            dve.tensor_scalar(b2t[:, b], b2r[:, b, 0:1], wsh[:, bass.ds(j, 1), 0], None, ALU.mult)\
                                .then_inc(b2_a, 1)
                            dve.wait_ge(b2_a, j + 1)
                            dve.scalar_tensor_tensor(out=b2s[:, b], in0=b2r[:, b, 1:2], scalar=wsh[:, bass.ds(j, 1), 1],
                                                     in1=b2t[:, b], op0=ALU.mult, op1=ALU.add).then_inc(b2_done, 1)
                            dve.wait_ge(b2_done, j + 1)
                            for k in range(KT):
                                v = KT * b + k
                                if k == 0:
                                    wait(dve, ln.centred, U * i + KT * b)
                                dve.wait_ge(tok_in[v % 2], TIN * (KT * i + v // 2) + TIN)
                                dve.wait_ge(down_done, U * i + v + 1)
                                dve.scalar_tensor_tensor(out=u[:, k], in0=yp[:, v % 2, 0:TW], scalar=b2s[:, b],
                                                         in1=xn[:, v % 2], op0=ALU.add, op1=ALU.add).then_inc(u_done, 1)
                            for k in range(KT):
                                v, n = KT * b + k, U * i + KT * b + k
                                ln.dve_norm(dve, U * i, v, EPS_T, nrm[:, v % 2])
                                dve.wait_ge(ln.normed, n + 1)
                                dve.tensor_scalar(o1[:, v % 2], nrm[:, v % 2], gam[:, 0:1], bet[:, 0:1], ALU.mult, ALU.add)\
                                    .then_inc(scaled, 1)
                                dve.wait_ge(scaled, n + 1)
                                wait(dve, out_st[v % 2], 16 * (KT * i + v // 2))
                                dve.tensor_tensor(o2[:, v % 2], o1[:, v % 2], tile(X, n), ALU.add).then_inc(out_done, 1)


def kernel(**inputs):
    import concourse.bacc as bacc
    import numpy as np
    from concourse.bass_utils import run_bass_kernel_spmd

    v = {k: np.ascontiguousarray(a) for k, a in inputs.items()}
    f = np.float32

    def zeros(*shape):
        return np.zeros(shape, f)

    a = {"x": v["x"].reshape(NP, P, PIX)}
    gate_w = zeros(2, C, 3, NQ, 2, 3)
    for lr, w in enumerate((v["L0_conv_w_l"], v["L0_conv_w_r"])):
        for im in range(2):
            for dt in range(3):
                gate_w[im, HALF * lr:HALF * lr + HALF, :, im + 2 - dt, lr, :] = w[0, :, dt].transpose(0, 2, 1)
    a["gate_w"] = gate_w.reshape(P, 3, GM)
    a["b_l"], a["b_r"] = v["L0_conv_b_l"], v["L0_conv_b_r"]
    gate_sel = zeros(4, NQ, 2, 3, 2, 3, 2, T)
    for h in range(2):
        for jj in range(4):
            for q in range(NQ):
                for lr in range(2):
                    for dy in range(3):
                        gate_sel[jj, q, lr, dy, h, dy, lr, (2 * (4 * h + jj) - 1 + q) % T] = 1
    a["gate_sel"] = gate_sel.reshape(4 * GM, 2, 3, 2 * T)
    w_gate = zeros(2, C, 2, E)
    conv_w = zeros(2, C, 9, 2, C)
    for im in range(2):
        w_gate[im, :, im] = v["L0_ffn_Wg"]
        conv_w[im, :, :, im] = v["L1_conv_weights"].reshape(C, C, 9).transpose(1, 2, 0)
    a["w_gate"] = w_gate.reshape(P, 2 * E)
    a["b_gate"] = np.tile(v["L0_ffn_bg"], SUB * 2)
    w1 = v["L0_ffn_W1"].transpose(1, 0, 2).reshape(C, E * H0)
    a["w1"] = np.concatenate([w1, w1])
    a["w2"] = v["L0_ffn_W2"].reshape(E, CH0, P, C).transpose(2, 0, 1, 3)
    a["b1"] = v["L0_ffn_b1"].reshape(E, CH0, P).transpose(2, 0, 1)
    a["b2"] = np.concatenate([v["L0_ffn_b2"].T, v["L0_ffn_b2"].T])
    a["conv_w"] = conv_w.reshape(P, 9, P)
    a["factor"] = v["L1_conv_real_scaling_factor"].reshape(C, 1)
    a["w_route"] = v["L1_ffn_Wr"]
    a["b_route"] = np.tile(v["L1_ffn_br"], 2)
    w1 = v["L1_ffn_W1"].transpose(1, 0, 2)
    a["w1_l1"] = np.concatenate([w1, w1])
    a["w2_l1"] = v["L1_ffn_W2"]
    a["b1_l1"] = v["L1_ffn_b1"].reshape(E, F1, 1)
    a["b2_l1"] = v["L1_ffn_b2"].reshape(E, C, 1)
    a["gamma"], a["beta"] = v["L1_ffn_gamma"].reshape(C, 1), v["L1_ffn_beta"].reshape(C, 1)
    block = np.kron(np.eye(2), np.ones((C, C))) / C
    a["centre"], a["average"], a["ident"] = (np.eye(P) - block).astype(f), block.astype(f), np.eye(P, dtype=f)

    nc = bacc.Bacc("TRN2", target_bir_lowering=False, num_devices=1)
    arrays = {f"in_{k}": np.ascontiguousarray(x) for k, x in a.items()}
    aps = {k: nc.dram_tensor(f"in_{k}", x.shape, mybir.dt.from_np(x.dtype), kind="ExternalInput").ap()
           for k, x in a.items()}
    out = nc.dram_tensor("out", (NP, P, PIX), F32, kind="ExternalOutput").ap()
    build(nc, aps, out)
    r = run_bass_kernel_spmd(nc, [arrays], core_ids=[0])
    return r.results[0]["out"].reshape(T, C, HH, WW)
```

```python
from contextlib import ExitStack

import concourse.bass as bass
from concourse import mybir

F32 = mybir.dt.float32
F32R = mybir.dt.float32r
I32 = mybir.dt.int32
ALU = mybir.AluOpType
ACT = mybir.ActivationFunctionType
AX = mybir.AxisListType

P = 128
T, C, HH, WW = 16, 64, 56, 56
PIX = HH * WW
NP = T // 2
ROWS = 8
KT = HH // ROWS
NT = NP * KT
TW = ROWS * WW
SUB = 4
GW = TW // SUB
HALF = 16
E = 8
H0 = 256
CH0 = H0 // P
F1 = 128
PADW = WW + 2
NQ = 4
GM = NQ * 2 * 3
CAPACITY = float(-(-T * PIX * 5 // (4 * E)))
EPS_C, EPS_T = 1e-6, 1e-5


def build(nc, A, out):
    top = ExitStack()

    def sem(ctx, name):
        return ctx.enter_context(nc.semaphore(name))

    def sbuf(ctx, name, shape, dt=F32):
        return ctx.enter_context(nc.sbuf_tensor(name, shape, dt))

    def psum(ctx, name, shape, dt=F32):
        return ctx.enter_context(nc.psum_tensor(name, shape, dt))

    def dram(name, shape, dt=F32):
        return nc.dram_tensor(name, shape, dt).ap()

    XN1 = dram("scr_xn1", [NT, P, TW])
    GPART = dram("scr_gate_part", [NP, GM, PIX])
    GATES = dram("scr_gates", [2 * T, PIX])
    Z = dram("scr_gated", [T + 2, 2 * HALF, PIX])
    SD2 = dram("scr_split2", [NT, 2, P, TW])
    WT = dram("scr_wtok", [NT, 2 * E, TW])
    SD4 = dram("scr_split4", [NT, 2, P, TW])
    XN4 = dram("scr_xn4", [NT, P, TW])
    W1D = dram("scr_w1split", [E, P, 2, F1])
    IDX = dram("scr_idx", [NP, 4], I32)
    WSEL = dram("scr_wsel", [NP, 4])

    X = sbuf(top, "X", [P, NT, TW])
    CEN = sbuf(top, "centre", [P, P])
    AVG = sbuf(top, "average", [P, P])
    EPS = sbuf(top, "eps", [P, 2])
    MSUM = sbuf(top, "msum", [P, NT])

    def tile(x, n):
        return x[:, bass.ds(n, 1), :].rearrange("p o w -> p (o w)")

    def split_rows(scratch, n, part):
        return scratch[bass.ds(n, 1), :, C * part:C * part + C].rearrange("o a c w -> (o a) c w")

    def exists(n):
        return not isinstance(n, int) or 0 <= n < NT

    def rows(ap):
        return ap.rearrange("p (r w) -> p r w", w=WW)

    def wait(engine, s, value):
        if not isinstance(value, int) or value > 0:
            engine.wait_ge(s, value)

    def units(engine, n):
        yield 0
        with engine.Fori(1, n) as i:
            yield i

    def before(base, m):
        return base + max(m - 1, 0)

    class Norm:

        def __init__(self, ctx, tag, nx, nv, depth=2, group=0):
            self.nx, self.nv, self.depth, self.group = nx, nv, depth, group
            self.xc = psum(ctx, tag + "_xc", [P, nx, 512])
            self.var = psum(ctx, tag + "_var", [P, nv, 512])
            self.sq = sbuf(ctx, tag + "_sq", [P, depth, TW])
            self.r = sbuf(ctx, tag + "_r", [P, depth, TW])
            self.rr = sbuf(ctx, tag + "_rr", [P, depth, TW])
            self.q = sbuf(ctx, tag + "_q", [P, depth, TW])
            self.g = sbuf(ctx, tag + "_g", [P, depth, TW])
            self.centred, self.squared, self.var_ready, self.seeded = (
                sem(ctx, tag + s) for s in ("_centred", "_squared", "_var_ready", "_seeded"))
            self.seed_squared, self.q_done, self.g_done, self.normed = (
                sem(ctx, tag + s) for s in ("_seed_squared", "_q_done", "_g_done", "_normed"))

        def freed(self, n, m, bufs):
            if self.group and m % self.group < bufs:
                return n - m % self.group
            return n + 1 - bufs

        def at(self, m, bufs):
            return (m % self.group if self.group else m) % bufs

        def pe_centre(self, pe, n, m, x):
            b = self.at(m, self.nx)
            wait(pe, self.normed, self.freed(n, m, self.nx))
            pe.matmul(self.xc[:, b, 0:TW], CEN[:], x, start=True, stop=True).then_inc(self.centred, 1)

        def act_square(self, act, n, m):
            act.wait_ge(self.centred, n + 1)
            wait(act, self.var_ready, self.freed(n, m, self.depth))
            act.activation(self.sq[:, self.at(m, self.depth)], self.xc[:, self.at(m, self.nx), 0:TW], ACT.Square)\
                .then_inc(self.squared, 1)

        def pe_var(self, pe, n, m):
            pe.wait_ge(self.squared, n + 1)
            wait(pe, self.q_done, self.freed(n, m, self.nv))
            pe.matmul(self.var[:, self.at(m, self.nv), 0:TW], AVG[:], self.sq[:, self.at(m, self.depth)],
                      start=True, stop=True).then_inc(self.var_ready, 1)

        def act_seed(self, act, n, m, eps_col):
            b = self.at(m, self.depth)
            act.wait_ge(self.var_ready, n + 1)
            wait(act, self.g_done, self.freed(n, m, self.depth))
            act.activation(self.r[:, b], self.var[:, self.at(m, self.nv), 0:TW], ACT.Abs_reciprocal_sqrt,
                           bias=EPS[:, eps_col:eps_col + 1]).then_inc(self.seeded, 1)
            act.wait_ge(self.seeded, n + 1)
            act.activation(self.rr[:, b], self.r[:, b], ACT.Square).then_inc(self.seed_squared, 1)

        def dve_newton(self, dve, n, m, eps):
            b = self.at(m, self.depth)
            dve.wait_ge(self.seed_squared, n + 1)
            dve.scalar_tensor_tensor(out=self.q[:, b], in0=self.var[:, self.at(m, self.nv), 0:TW], scalar=eps,
                                     in1=self.rr[:, b], op0=ALU.add, op1=ALU.mult).then_inc(self.q_done, 1)
            dve.wait_ge(self.q_done, n + 1)
            dve.scalar_tensor_tensor(out=self.g[:, b], in0=self.q[:, b], scalar=-3.0,
                                     in1=self.r[:, b], op0=ALU.add, op1=ALU.mult).then_inc(self.g_done, 1)

        def dve_scale(self, dve, n, m, dst, accum=None):
            dve.wait_ge(self.g_done, n + 1)
            xc, g = self.xc[:, self.at(m, self.nx), 0:TW], self.g[:, self.at(m, self.depth)]
            dve.scalar_tensor_tensor(out=dst, in0=xc, scalar=-0.5, in1=g, op0=ALU.mult, op1=ALU.mult,
                                     accum_out=accum).then_inc(self.normed, 1)

        def dve_norm(self, dve, n, m, eps, dst, accum=None):
            self.dve_newton(dve, n, m, eps)
            self.dve_scale(dve, n, m, dst, accum)

    with top:
        with ExitStack() as ctx:
            gw = sbuf(ctx, "gate_w", [P, 3, GM])
            xn = sbuf(ctx, "xn1", [P, 2, TW])
            gp = sbuf(ctx, "gate_part", [GM, 2, TW])
            gps = psum(ctx, "gate_psum", [P, 2, 512])
            ln = Norm(ctx, "ln1", 2, 2)
            consts, eps_set, x_in = sem(ctx, "p1_consts"), sem(ctx, "p1_eps"), sem(ctx, "p1_x")
            part_ready, part_copied = sem(ctx, "p1_part"), sem(ctx, "p1_part_copied")
            xn_stored = [sem(ctx, f"p1_xn_stored{b}") for b in range(2)]
            gp_stored = [sem(ctx, f"p1_gp_stored{b}") for b in range(2)]
            U = 2 * KT
            with nc.Block() as block:
                @block.sync
                def _(sp):
                    sp.dma_start(CEN[:], A["centre"]).then_inc(consts, 16)
                    sp.dma_start(AVG[:], A["average"]).then_inc(consts, 16)
                    sp.dma_start(gw[:], A["gate_w"]).then_inc(consts, 16)
                    for j in units(sp, NP):
                        wait(sp, x_in, 16 * j)
                        sp.dma_start(X[:, bass.ds(j * KT, KT), :].rearrange("p k w -> p (k w)"),
                                     A["x"][bass.ds(j, 1)].rearrange("o p w -> (o p) w")).then_inc(x_in, 16)

                @block.tensor
                def _(pe):
                    pe.wait_ge(consts, 48)

                    def gate(i, m):
                        pe.wait_ge(ln.normed, U * i + m + 1)
                        wait(pe, part_copied, before(U * i, m))
                        o = rows(gps[0:GM, m % 2, 0:TW])
                        src = rows(xn[:, m % 2])
                        pe.matmul(o, gw[:, 1, :], src, start=True, stop=False)
                        pe.matmul(o[:, :, 1:WW], gw[:, 0, :], src[:, :, 0:WW - 1], start=False, stop=False)
                        pe.matmul(o[:, :, 0:WW - 1], gw[:, 2, :], src[:, :, 1:WW], start=False, stop=True)\
                            .then_inc(part_ready, 1)

                    for i in units(pe, NT // U):
                        for m in range(U):
                            if m % KT == 0:
                                pe.wait_ge(x_in, 32 * i + 16 * (m // KT) + 16)
                            ln.pe_centre(pe, U * i + m, m, tile(X, U * i + m))
                            if m >= 1:
                                ln.pe_var(pe, U * i + m - 1, m - 1)
                            if m >= 2:
                                gate(i, m - 2)
                        ln.pe_var(pe, U * i + U - 1, U - 1)
                        gate(i, U - 2)
                        gate(i, U - 1)

                @block.scalar
                def _(act):
                    act.wait_ge(eps_set, 2)

                    def copy_part(i, m):
                        act.wait_ge(part_ready, U * i + m + 1)
                        wait(act, gp_stored[m % 2], 16 * (KT * i + m // 2))
                        act.activation(gp[:, m % 2], gps[0:GM, m % 2, 0:TW], ACT.Copy).then_inc(part_copied, 1)

                    for i in units(act, NT // U):
                        for m in range(U):
                            ln.act_square(act, U * i + m, m)
                            if m >= 1:
                                ln.act_seed(act, U * i + m - 1, m - 1, 0)
                            if m >= 3:
                                copy_part(i, m - 3)
                        ln.act_seed(act, U * i + U - 1, U - 1, 0)
                        for m in range(U - 3, U):
                            copy_part(i, m)

                @block.vector
                def _(dve):
                    dve.memset(EPS[:, 0:1], EPS_C).then_inc(eps_set, 1)
                    dve.memset(EPS[:, 1:2], EPS_T).then_inc(eps_set, 1)
                    for i in units(dve, NT // U):
                        for m in range(U):
                            wait(dve, xn_stored[m % 2], 16 * (KT * i + m // 2))
                            wait(dve, part_ready, before(U * i, m))
                            ln.dve_norm(dve, U * i + m, m, EPS_C, xn[:, m % 2])

                @block.gpsimd
                def _(pool):
                    def store_part(i, m):
                        pool.wait_ge(part_copied, U * i + m + 1)
                        pool.dma_start(GPART[bass.ds(2 * i + m // KT, 1), :, (m % KT) * TW:(m % KT + 1) * TW]
                                       .rearrange("o g w -> (o g) w"), gp[:, m % 2]).then_inc(gp_stored[m % 2], 16)

                    for i in units(pool, NT // U):
                        for m in range(U):
                            pool.wait_ge(ln.normed, U * i + m + 1)
                            pool.dma_start(XN1[bass.ds(U * i + m, 1)].rearrange("o p w -> (o p) w"), xn[:, m % 2])\
                                .then_inc(xn_stored[m % 2], 16)
                            if m >= 2:
                                store_part(i, m - 2)
                        store_part(i, U - 2)
                        store_part(i, U - 1)
                    for b in range(2):
                        pool.wait_ge(xn_stored[b], 16 * NT // 2)
                        pool.wait_ge(gp_stored[b], 16 * NT // 2)

        with ExitStack() as ctx:
            pb = [sbuf(ctx, f"gate_rows{h}", [4 * GM, HH + 2, WW]) for h in range(2)]
            gs = sbuf(ctx, "gate_sel", [4 * GM, 2, 3, 2 * T])
            gb = sbuf(ctx, "gate_bias", [2 * T, 1])
            gt = sbuf(ctx, "gates", [2 * T, PIX])
            gps = psum(ctx, "gate_sum", [2 * T, 2, 512])
            loaded, zeroed, summed, tanhed, stored = (sem(ctx, "p2_" + s) for s in
                                                      ("loaded", "zeroed", "summed", "tanhed", "stored"))
            with nc.Block() as block:
                @block.sync
                def _(sp):
                    for h in range(2):
                        sp.dma_start(pb[h][:, 1:HH + 1, :].rearrange("p r w -> p (r w)"),
                                     GPART[4 * h:4 * h + 4].rearrange("j g w -> (j g) w")).then_inc(loaded, 16)
                    sp.dma_start(gs[:], A["gate_sel"]).then_inc(loaded, 16)
                    sp.dma_start(gb[0:T, :], A["b_l"].partition_broadcast(T)).then_inc(loaded, 16)
                    sp.dma_start(gb[T:2 * T, :], A["b_r"].partition_broadcast(T)).then_inc(loaded, 16)
                    sp.wait_ge(tanhed, KT)
                    sp.dma_start(GATES, gt[:]).then_inc(stored, 16)
                    sp.wait_ge(stored, 16)

                @block.vector
                def _(dve):
                    for h in range(2):
                        for r in (0, HH + 1):
                            dve.memset(pb[h][:, r, :], 0.0).then_inc(zeroed, 1)

                @block.tensor
                def _(pe):
                    pe.wait_ge(loaded, 80)
                    pe.wait_ge(zeroed, 4)
                    for k in range(KT):
                        if k >= 2:
                            pe.wait_ge(tanhed, k - 1)
                        for h in range(2):
                            for dy in range(3):
                                mm = pe.matmul(rows(gps[:, k % 2, 0:TW]), gs[:, h, dy, :],
                                               pb[h][:, ROWS * k + dy:ROWS * k + dy + ROWS, :],
                                               start=(h == 0 and dy == 0), stop=(h == 1 and dy == 2))
                        mm.then_inc(summed, 1)

                @block.scalar
                def _(act):
                    for k in range(KT):
                        act.wait_ge(summed, k + 1)
                        act.activation(gt[:, TW * k:TW * (k + 1)], gps[:, k % 2, 0:TW], ACT.Tanh, bias=gb[:])\
                            .then_inc(tanhed, 1)

        with ExitStack() as ctx:
            gbc = sbuf(ctx, "gate_bc", [P, 2, PIX])
            xn = sbuf(ctx, "xn_again", [P, 2, PIX])
            z = sbuf(ctx, "gated", [P, 2, PIX])
            zeroed = sem(ctx, "p3_zeroed")
            loaded = [sem(ctx, f"p3_loaded{b}") for b in range(2)]
            gated, kept, moved, wrapped = (sem(ctx, "p3_" + s) for s in ("gated", "kept", "moved", "wrapped"))
            stored = [sem(ctx, f"p3_stored{b}") for b in range(2)]
            with nc.Block() as block:
                def pair(j):
                    return X[:, bass.ds(j * KT, KT), :].rearrange("p k w -> p (k w)")

                @block.sync
                def _(sp):
                    sp.wait_ge(zeroed, 1)
                    for i in units(sp, NP // 2):
                        for b in range(2):
                            j = 2 * i + b
                            wait(sp, moved, 2 * i)
                            for a in range(2):
                                for lr in range(2):
                                    r = C * a + HALF * lr
                                    sp.dma_start(gbc[r:r + HALF, b, :],
                                                 GATES[bass.ds(lr * T + 2 * j + a, 1), :]
                                                 .rearrange("o w -> (o w)").partition_broadcast(HALF))\
                                        .then_inc(loaded[b], 16)
                            sp.dma_start(xn[:, b, :].rearrange("p (k w) -> p k w", w=TW),
                                         XN1[bass.ds(j * KT, KT)].rearrange("k p w -> p k w"))\
                                .then_inc(loaded[b], 16)

                @block.gpsimd
                def _(pool):
                    pool.memset(gbc[:], 0.0).then_inc(zeroed, 1)

                @block.vector
                def _(dve):
                    for i in units(dve, NP // 2):
                        for b in range(2):
                            j = 2 * i + b
                            dve.wait_ge(loaded[b], 80 * i + 80)
                            wait(dve, stored[b], 32 * i)
                            dve.tensor_tensor(z[:, b], gbc[:, b], xn[:, b], ALU.mult).then_inc(gated, 1)
                            dve.tensor_tensor(pair(j), pair(j), xn[:, b], ALU.add).then_inc(kept, 1)
                            dve.wait_ge(gated, j + 1)
                            dve.wait_ge(kept, j + 1)
                            dve.tensor_tensor(pair(j), pair(j), z[:, b], ALU.subtract).then_inc(moved, 1)

                @block.scalar
                def _(act):
                    for i in units(act, NP // 2):
                        for b in range(2):
                            act.wait_ge(gated, 2 * i + b + 1)
                            for a in range(2):
                                act.dma_start(Z[bass.ds(4 * i + 2 * b + a + 1, 1)].rearrange("o c w -> (o c) w"),
                                              z[C * a:C * a + 2 * HALF, b, :]).then_inc(stored[b], 16)
                    for b in range(2):
                        act.wait_ge(stored[b], 32 * (NP // 2))
                    act.dma_start(Z[0], Z[T]).then_inc(wrapped, 16)
                    act.dma_start(Z[T + 1], Z[1]).then_inc(wrapped, 16)
                    act.wait_ge(wrapped, 32)

        moe0 = ExitStack()
        LG = sbuf(moe0, "logits", [GW, NT * SUB * 2, E])
        with ExitStack() as ctx:
            zs = sbuf(ctx, "shifted", [P, 2, PIX])
            wg = sbuf(ctx, "w_gate", [P, 2 * E])
            bg = sbuf(ctx, "b_gate", [GW, SUB * 2, E])
            xn = sbuf(ctx, "xn2", [P, 2, TW])
            hi = sbuf(ctx, "hi2", [P, 2, TW], F32R)
            lo = sbuf(ctx, "lo2", [P, 2, TW], F32R)
            lps = psum(ctx, "logit_psum", [P, 2, 512])
            ln = Norm(ctx, "ln2", 2, 2)
            consts, zeroed, added, hi_done, lo_done, lg_ready, lg_done = (
                sem(ctx, "p4_" + s) for s in ("consts", "zeroed", "added", "hi", "lo", "lg_ready", "lg_done"))
            z_in = [sem(ctx, f"p4_z{b}") for b in range(2)]
            stored = [sem(ctx, f"p4_stored{b}") for b in range(2)]
            U = 2 * KT
            with nc.Block() as block:
                @block.gpsimd
                def _(pool):
                    pool.memset(zs[:], 0.0).then_inc(zeroed, 1)
                    for i in units(pool, NT // U):
                        for m in range(U):
                            pool.wait_ge(hi_done, U * i + m + 1)
                            pool.dma_start(split_rows(SD2, U * i + m, 0), hi[:, m % 2].bitcast(F32))\
                                .then_inc(stored[m % 2], 16)
                            pool.wait_ge(lo_done, U * i + m + 1)
                            pool.dma_start(split_rows(SD2, U * i + m, 1), lo[:, m % 2].bitcast(F32))\
                                .then_inc(stored[m % 2], 16)
                    for b in range(2):
                        pool.wait_ge(stored[b], 32 * NT // 2)

                @block.sync
                def _(sp):
                    sp.dma_start(wg[:], A["w_gate"]).then_inc(consts, 16)
                    sp.dma_start(bg[:].rearrange("p s e -> p (s e)"), A["b_gate"].partition_broadcast(GW))\
                        .then_inc(consts, 16)
                    sp.wait_ge(zeroed, 1)
                    for i in units(sp, NT // U):
                        for b in range(2):
                            wait(sp, added, U * i)
                            for a in range(2):
                                for lr in range(2):
                                    r = C * a + HALF * lr
                                    slot = 4 * i + 2 * b + a + 1 + (1 - 2 * lr)
                                    sp.dma_start(zs[r:r + HALF, b, :],
                                                 Z[bass.ds(slot, 1), HALF * lr:HALF * lr + HALF]
                                                 .rearrange("o c w -> (o c) w")).then_inc(z_in[b], 16)

                @block.tensor
                def _(pe):
                    pe.wait_ge(consts, 32)

                    def logits(i, m):
                        pe.wait_ge(ln.normed, U * i + m + 1)
                        wait(pe, lg_done, before(U * i, m))
                        for s in range(SUB):
                            mm = pe.matmul(lps[0:GW, m % 2, s * 2 * E:(s + 1) * 2 * E], xn[:, m % 2, GW * s:GW * (s + 1)],
                                           wg[:], start=True, stop=True)
                        mm.then_inc(lg_ready, 1)

                    for i in units(pe, NT // U):
                        for m in range(U):
                            pe.wait_ge(added, U * i + m + 1)
                            ln.pe_centre(pe, U * i + m, m, tile(X, U * i + m))
                            if m >= 1:
                                ln.pe_var(pe, U * i + m - 1, m - 1)
                            if m >= 2:
                                logits(i, m - 2)
                        ln.pe_var(pe, U * i + U - 1, U - 1)
                        logits(i, U - 2)
                        logits(i, U - 1)

                @block.scalar
                def _(act):
                    for i in units(act, NT // U):
                        for m in range(U):
                            ln.act_square(act, U * i + m, m)
                            if m >= 1:
                                ln.act_seed(act, U * i + m - 1, m - 1, 1)
                        ln.act_seed(act, U * i + U - 1, U - 1, 1)

                @block.vector
                def _(dve):
                    dve.wait_ge(consts, 32)

                    def add_shifted(i, m):
                        if m % KT == 0:
                            dve.wait_ge(z_in[m // KT], 64 * i + 64)
                        x = tile(X, U * i + m)
                        dve.tensor_tensor(x, x, zs[:, m // KT, (m % KT) * TW:(m % KT + 1) * TW], ALU.add)\
                            .then_inc(added, 1)

                    def keep_logits(i, m):
                        dve.wait_ge(lg_ready, U * i + m + 1)
                        dve.tensor_tensor(LG[:, bass.ds((U * i + m) * SUB * 2, SUB * 2), :],
                                          lps[0:GW, m % 2, 0:SUB * 2 * E].rearrange("p (s e) -> p s e", e=E),
                                          bg[:], ALU.add).then_inc(lg_done, 1)

                    for i in units(dve, NT // U):
                        add_shifted(i, 0)
                        add_shifted(i, 1)
                        for m in range(U):
                            if m + 2 < U:
                                add_shifted(i, m + 2)
                            wait(dve, lg_ready, before(U * i, m))
                            ln.dve_norm(dve, U * i + m, m, EPS_T, xn[:, m % 2])
                            dve.wait_ge(ln.normed, U * i + m + 1)
                            wait(dve, stored[m % 2], 32 * (KT * i + m // 2))
                            dve.tensor_copy(hi[:, m % 2], xn[:, m % 2]).then_inc(hi_done, 1)
                            dve.wait_ge(hi_done, U * i + m + 1)
                            dve.tensor_tensor(lo[:, m % 2], xn[:, m % 2], hi[:, m % 2].bitcast(F32), ALU.subtract)\
                                .then_inc(lo_done, 1)
                            if m >= 2:
                                keep_logits(i, m - 2)
                        keep_logits(i, U - 2)
                        keep_logits(i, U - 1)

        with ExitStack() as ctx:
            G = NT * SUB * 2
            rank = sbuf(ctx, "rank", [GW, G, E])
            gt = sbuf(ctx, "beats", [GW, G, E])
            best = sbuf(ctx, "best", [GW, 2, G])
            w12 = sbuf(ctx, "w12", [GW, 2, G])
            th = sbuf(ctx, "th", [GW, 2, G])
            ident = sbuf(ctx, "ident", [P, P])
            wst = sbuf(ctx, "w_stage", [GW, 2, SUB * 2, E])
            wtt = sbuf(ctx, "wtt", [2 * E, 2, TW])
            wps = psum(ctx, "w_psum", [P, 2, 512])
            s_v, s_th, s_tr, s_cp, s_id, s_st = (sem(ctx, "p5_" + s) for s in ("v", "th", "tr", "cp", "id", "st"))
            stored = [sem(ctx, f"p5_stored{b}") for b in range(2)]
            steps = [0]
            with nc.Block() as block:
                @block.vector
                def _(dve):
                    def link(ins):
                        steps[0] += 1
                        ins.then_inc(s_v, 1)
                        dve.wait_ge(s_v, steps[0])

                    for e in range(E):
                        ms = dve.memset(rank[:, :, e], float(e))
                    link(ms)
                    for s in range(1, E):
                        lo_, hi_ = slice(0, E - s), slice(s, E)
                        link(dve.tensor_tensor(gt[:, :, lo_], LG[:, :, hi_], LG[:, :, lo_], ALU.is_gt))
                        link(dve.tensor_tensor(rank[:, :, lo_], rank[:, :, lo_], gt[:, :, lo_], ALU.add))
                        link(dve.tensor_tensor(rank[:, :, hi_], rank[:, :, hi_], gt[:, :, lo_], ALU.subtract))
                    for k in range(2):
                        link(dve.scalar_tensor_tensor(out=gt[:], in0=rank[:], scalar=float(k), in1=LG[:],
                                                      op0=ALU.is_equal, op1=ALU.mult))
                        link(dve.tensor_reduce(best[:, k, :], gt[:], AX.X, ALU.add))
                    link(dve.tensor_tensor(th[:, 0, :], best[:, 0, :], best[:, 1, :], ALU.subtract))
                    dve.wait_ge(s_th, 1)
                    link(dve.tensor_scalar(w12[:, 0, :], th[:, 1, :], 0.5, 0.5, ALU.mult, ALU.add))
                    link(dve.tensor_scalar(w12[:, 1, :], th[:, 1, :], -0.5, 0.5, ALU.mult, ALU.add))
                    for k in range(2):
                        dst = gt if k == 0 else LG
                        link(dve.scalar_tensor_tensor(out=dst[:], in0=rank[:], scalar=float(k),
                                                      in1=w12[:, k, :].unsqueeze(2).broadcast_to([GW, G, E]),
                                                      op0=ALU.is_equal, op1=ALU.mult))
                    for i in units(dve, NT // 2):
                        for b in range(2):
                            g = bass.ds((2 * i + b) * SUB * 2, SUB * 2)
                            wait(dve, s_tr, 2 * i)
                            dve.tensor_tensor(wst[:, b], LG[:, g, :], gt[:, g, :], ALU.add).then_inc(s_st, 1)

                before_tanh = 1 + 3 * (E - 1) + 4 + 1

                @block.scalar
                def _(act):
                    act.wait_ge(s_v, before_tanh)
                    act.activation(th[:, 1, :], th[:, 0, :], ACT.Tanh, scale=0.5).then_inc(s_th, 1)
                    for i in units(act, NT // 2):
                        for b in range(2):
                            act.wait_ge(s_tr, 2 * i + b + 1)
                            wait(act, stored[b], 16 * i)
                            act.activation(wtt[:, b], wps[0:2 * E, b, 0:TW], ACT.Copy).then_inc(s_cp, 1)

                @block.tensor
                def _(pe):
                    pe.wait_ge(s_id, 16)
                    for i in units(pe, NT // 2):
                        for b in range(2):
                            wait(pe, s_cp, 2 * i)
                            pe.wait_ge(s_st, 2 * i + b + 1)
                            for s in range(SUB):
                                w = wst[:, b, 2 * s:2 * s + 2, :].rearrange("p s e -> p (s e)")
                                tr = pe.transpose(wps[0:2 * E, b, GW * s:GW * (s + 1)], w, ident[0:GW, 0:GW])
                            tr.then_inc(s_tr, 1)

                @block.sync
                def _(sp):
                    sp.dma_start(ident[:], A["ident"]).then_inc(s_id, 16)
                    for i in units(sp, NT // 2):
                        for b in range(2):
                            sp.wait_ge(s_cp, 2 * i + b + 1)
                            sp.dma_start(WT[bass.ds(2 * i + b, 1)].rearrange("o r w -> (o r) w"), wtt[:, b])\
                                .then_inc(stored[b], 16)
                    for b in range(2):
                        sp.wait_ge(stored[b], 16 * NT // 2)
        moe0.close()

        with ExitStack() as ctx:
            w1raw = sbuf(ctx, "w1raw", [P, E * H0])
            w1hi = sbuf(ctx, "w1hi", [P, E * H0], F32R)
            w1lo = sbuf(ctx, "w1lo", [P, E * H0], F32R)
            w2 = sbuf(ctx, "w2", [P, E, CH0, C])
            b1 = sbuf(ctx, "b1", [P, E, CH0])
            b2 = sbuf(ctx, "b2", [P, E])
            S = sbuf(ctx, "tokens", [P, 2, 2, TW], F32R)
            WB = sbuf(ctx, "w_bc", [P, 2, E, TW])
            hs = sbuf(ctx, "hidden", [P, 2 * CH0, 2, TW])
            pr = sbuf(ctx, "weighted", [P, 2, TW])
            hp = psum(ctx, "hidden_psum", [P, 2, 2, 512])
            yp = psum(ctx, "y_psum", [P, 2, 512])
            consts, whi, wlo, up_done, gelu_done, down_done, weighted, summed = (
                sem(ctx, "p6_" + s) for s in ("consts", "whi", "wlo", "up", "gelu", "down", "weighted", "summed"))
            tok_in = [sem(ctx, f"p6_tok{b}") for b in range(2)]
            SN = E * CH0
            PER = 48

            with nc.Block() as block:
                @block.sync
                def _(sp):
                    def load(n, b):
                        sp.dma_start(S[:, b].bitcast(F32), SD2[bass.ds(n, 1)].rearrange("o a p w -> (o p) a w"))\
                            .then_inc(tok_in[b], 16)
                        for a in range(2):
                            sp.dma_start(WB[C * a:C * a + C, b], WT[bass.ds(n, 1), E * a:E * a + E]
                                         .rearrange("o e w -> (o e) w").partition_broadcast(C)).then_inc(tok_in[b], 16)

                    sp.dma_start(w1raw[:], A["w1"]).then_inc(consts, 16)
                    sp.dma_start(w2[:], A["w2"]).then_inc(consts, 16)
                    sp.dma_start(b1[:], A["b1"]).then_inc(consts, 16)
                    sp.dma_start(b2[:], A["b2"]).then_inc(consts, 16)
                    load(0, 0)
                    load(1, 1)
                    for i in units(sp, NT // 2 - 1):
                        for b in range(2):
                            n = 2 * i + b
                            sp.wait_ge(up_done, SN * n + SN)
                            sp.wait_ge(weighted, E * n + E)
                            load(n + 2, b)

                @block.tensor
                def _(pe):
                    pe.wait_ge(consts, 64)
                    pe.wait_ge(wlo, 1)

                    def up(i, b, s, first=False):
                        if s == 0:
                            pe.wait_ge(tok_in[b], PER * i + PER)
                        if not first:
                            wait(pe, gelu_done, SN * (2 * i + b) + s - 1)
                        for a in range(2):
                            o = hp[:, s % 2, a, 0:TW]
                            pe.matmul(o, w1hi[:, s * P:(s + 1) * P], S[:, b, a, :], start=True, stop=False)
                            mm = pe.matmul(o, w1lo[:, s * P:(s + 1) * P], S[:, b, a, :], start=False, stop=True)
                        mm.then_inc(up_done, 1)

                    def down(i, b, s):
                        e, c = divmod(s, CH0)
                        pe.wait_ge(gelu_done, SN * (2 * i + b) + s + 1)
                        if c == 0:
                            wait(pe, weighted, E * 2 * i + max(E * b + e - 1, 0))
                        for a in range(2):
                            mm = pe.matmul(yp[C * a:C * a + C, e % 2, 0:TW], w2[:, e, c, :], hs[:, s % (2 * CH0), a, :],
                                           start=(c == 0), stop=(c == CH0 - 1))
                        mm.then_inc(down_done, 1)

                    def ups(i, b, e, first=False):
                        for c in range(CH0):
                            up(i, b, CH0 * e + c, first)

                    def two_tiles(i, last):
                        for k in range(2 * E):
                            if k + 1 < 2 * E:
                                ups(i, (k + 1) // E, (k + 1) % E)
                            elif not last:
                                ups(i + 1, 0, 0)
                            for c in range(CH0):
                                down(i, k // E, CH0 * (k % E) + c)

                    ups(0, 0, 0, first=True)
                    for i in units(pe, NT // 2 - 1):
                        two_tiles(i, False)
                    two_tiles(NT // 2 - 1, True)

                @block.scalar
                def _(act):
                    act.wait_ge(consts, 64)
                    for i in units(act, NT // 2):
                        for k in range(2 * SN):
                            e, c = divmod(k % SN, CH0)
                            act.wait_ge(up_done, 2 * SN * i + k + 1)
                            wait(act, down_done, 2 * SN * i + k + 1 - 2 * CH0)
                            act.activation(hs[:, k % (2 * CH0)], hp[:, k % 2, :, 0:TW], ACT.Gelu, bias=b1[:, e, c:c + 1])\
                                .then_inc(gelu_done, 1)

                @block.vector
                def _(dve):
                    dve.wait_ge(consts, 64)
                    dve.tensor_copy(w1hi[:], w1raw[:]).then_inc(whi, 1)
                    dve.wait_ge(whi, 1)
                    dve.tensor_tensor(w1lo[:], w1raw[:], w1hi[:].bitcast(F32), ALU.subtract).then_inc(wlo, 1)
                    for i in units(dve, NT // 2):
                        for b in range(2):
                            x = tile(X, 2 * i + b)
                            dve.wait_ge(tok_in[b], PER * i + PER)
                            for e in range(E):
                                dve.wait_ge(down_done, SN * (2 * i + b) + CH0 * (e + 1))
                                dve.scalar_tensor_tensor(out=pr[:, e % 2], in0=yp[:, e % 2, 0:TW], scalar=b2[:, e:e + 1],
                                                         in1=WB[:, b, e, :], op0=ALU.add, op1=ALU.mult)\
                                    .then_inc(weighted, 1)
                                dve.wait_ge(weighted, E * (2 * i + b) + e + 1)
                                if e or b:
                                    dve.wait_ge(summed, E * (2 * i + b) + e)
                                dve.tensor_tensor(x, x, pr[:, e % 2], ALU.add).then_inc(summed, 1)

        with ExitStack() as ctx:
            cwraw = sbuf(ctx, "conv_raw", [P, 9, P])
            cw = sbuf(ctx, "conv_sign", [P, 9, P], F32R)
            sf = sbuf(ctx, "factor", [P, 1])
            pad_hi = sbuf(ctx, "pad_hi", [P, 2, HH + 2, PADW], F32R)
            pad_lo = sbuf(ctx, "pad_lo", [P, 2, HH + 2, PADW], F32R)
            xn3 = sbuf(ctx, "xn3", [P, 2, TW])
            xn4 = sbuf(ctx, "xn4", [P, 2, TW])
            hi = sbuf(ctx, "hi4", [P, 2, TW], F32R)
            lo = sbuf(ctx, "lo4", [P, 2, TW], F32R)
            cps = psum(ctx, "conv_psum", [P, 2, 512])
            ln3, ln4 = Norm(ctx, "ln3", 2, 1, depth=1), Norm(ctx, "ln4", 2, 1, depth=1)
            consts, signed, zeroed, pad_hi_done, pad_lo_done, conv_done, x3_done, hi_done, lo_done = (
                sem(ctx, "p7_" + s) for s in ("consts", "signed", "zeroed", "pad_hi", "pad_lo", "conv", "x3", "hi", "lo"))
            stored = [sem(ctx, f"p7_stored{b}") for b in range(2)]
            V = 2 * KT

            def every_step(engine, step):
                for i in units(engine, NP // 2 - 1):
                    for m in range(V):
                        step(V * i + m, m)
                for m in range(V):
                    step(NT - V + m, m)

            with nc.Block() as block:
                @block.sync
                def _(sp):
                    sp.dma_start(cwraw[:], A["conv_w"]).then_inc(consts, 16)
                    for a in range(2):
                        sp.dma_start(sf[C * a:C * a + C, :], A["factor"]).then_inc(consts, 16)

                    def store(n, m):
                        sp.wait_ge(ln4.normed, n + 1)
                        sp.dma_start(XN4[bass.ds(n, 1)].rearrange("o p w -> (o p) w"), xn4[:, m % 2])\
                            .then_inc(stored[m % 2], 16)
                        sp.wait_ge(hi_done, n + 1)
                        sp.dma_start(split_rows(SD4, n, 0), hi[:, m % 2].bitcast(F32)).then_inc(stored[m % 2], 16)
                        sp.wait_ge(lo_done, n + 1)
                        sp.dma_start(split_rows(SD4, n, 1), lo[:, m % 2].bitcast(F32)).then_inc(stored[m % 2], 16)

                    every_step(sp, store)
                    for b in range(2):
                        sp.wait_ge(stored[b], 48 * NT // 2)

                @block.tensor
                def _(pe):
                    pe.wait_ge(signed, 1)
                    pe.wait_ge(zeroed, 2)

                    def conv(n, m):
                        pair, k = divmod(m, KT)
                        pe.wait_ge(pad_lo_done, n + 1 + min(1, KT - 1 - k))
                        wait(pe, x3_done, n - 1)
                        o = rows(cps[:, m % 2, 0:TW])
                        for t9 in range(9):
                            dy, dx = divmod(t9, 3)
                            for part, src in enumerate((pad_hi, pad_lo)):
                                mm = pe.matmul(o, cw[:, t9, :], src[:, pair, ROWS * k + dy:ROWS * k + dy + ROWS, dx:dx + WW],
                                               start=(t9 == 0 and part == 0), stop=(t9 == 8 and part == 1))
                        mm.then_inc(conv_done, 1)

                    def centre4(n, m):
                        pe.wait_ge(x3_done, n + 1)
                        ln4.pe_centre(pe, n, m, tile(X, n))

                    def step(n, m):
                        if exists(n + KT):
                            ln3.pe_centre(pe, n + KT, m + KT, tile(X, n + KT))
                        if exists(n - 2):
                            ln4.pe_var(pe, n - 2, m)
                        conv(n, m)
                        if exists(n - 1):
                            centre4(n - 1, m + 1)
                        if exists(n + KT):
                            ln3.pe_var(pe, n + KT, m + KT)

                    for k in range(KT):
                        ln3.pe_centre(pe, k, k, tile(X, k))
                        if k >= 1:
                            ln3.pe_var(pe, k - 1, k - 1)
                    ln3.pe_var(pe, KT - 1, KT - 1)
                    every_step(pe, step)
                    ln4.pe_var(pe, NT - 2, 0)
                    centre4(NT - 1, 1)
                    ln4.pe_var(pe, NT - 1, 1)

                @block.scalar
                def _(act):
                    act.wait_ge(consts, 48)
                    act.activation(cw[:], cwraw[:], ACT.Sign).then_inc(signed, 1)

                    def step(n, m):
                        if exists(n + KT):
                            ln3.act_square(act, n + KT, m + KT)
                        if exists(n - 2):
                            ln4.act_seed(act, n - 2, m, 1)
                        if exists(n - 1):
                            ln4.act_square(act, n - 1, m + 1)
                        if exists(n + KT):
                            ln3.act_seed(act, n + KT, m + KT, 0)

                    for k in range(KT):
                        ln3.act_square(act, k, k)
                        if k >= 1:
                            ln3.act_seed(act, k - 1, k - 1, 0)
                    ln3.act_seed(act, KT - 1, KT - 1, 0)
                    every_step(act, step)
                    ln4.act_seed(act, NT - 2, 0, 1)
                    ln4.act_square(act, NT - 1, 1)
                    ln4.act_seed(act, NT - 1, 1, 1)

                @block.vector
                def _(dve):
                    dve.wait_ge(consts, 48)
                    dve.wait_ge(zeroed, 2)

                    def norm3(n, m):
                        pair, k = divmod(m, KT)
                        wait(dve, pad_lo_done, n - 1)
                        ln3.dve_norm(dve, n, m, EPS_C, xn3[:, m % 2])
                        dve.wait_ge(ln3.normed, n + 1)
                        if k == 0:
                            wait(dve, conv_done, n - KT)
                        dve.tensor_copy(pad_hi[:, pair, ROWS * k + 1:ROWS * k + 1 + ROWS, 1:WW + 1], rows(xn3[:, m % 2]))\
                            .then_inc(pad_hi_done, 1)

                    def norm4(n, m):
                        wait(dve, stored[m % 2], past_stores(n, m))
                        ln4.dve_norm(dve, n, m, EPS_T, xn4[:, m % 2], accum=MSUM[:, bass.ds(n, 1)])
                        dve.wait_ge(ln4.normed, n + 1)
                        dve.tensor_copy(hi[:, m % 2], xn4[:, m % 2]).then_inc(hi_done, 1)

                    def past_stores(n, m):
                        return 24 * (n - m % 2)

                    def step(n, m):
                        if exists(n - 1) and exists(n + KT - 1):
                            norm3(n + KT - 1, (m + KT - 1) % V)
                        if exists(n - 2):
                            norm4(n - 2, m)
                        dve.wait_ge(conv_done, n + 1)
                        x = tile(X, n)
                        dve.scalar_tensor_tensor(out=x, in0=cps[:, m % 2, 0:TW], scalar=sf[:, 0:1], in1=x,
                                                 op0=ALU.mult, op1=ALU.add).then_inc(x3_done, 1)

                    for k in range(KT):
                        norm3(k, k)
                    every_step(dve, step)
                    norm4(NT - 2, 0)
                    norm4(NT - 1, 1)

                @block.gpsimd
                def _(pool):
                    pool.memset(pad_hi[:].bitcast(F32), 0.0).then_inc(zeroed, 1)
                    pool.memset(pad_lo[:].bitcast(F32), 0.0).then_inc(zeroed, 1)

                    def lo3(n, m):
                        pair, k = divmod(m, KT)
                        inside = (slice(None), pair, slice(ROWS * k + 1, ROWS * k + 1 + ROWS), slice(1, WW + 1))
                        pool.wait_ge(pad_hi_done, n + 1)
                        if k == 0:
                            wait(pool, conv_done, n - KT)
                        pool.tensor_tensor(pad_lo[inside], rows(xn3[:, m % 2]), pad_hi[inside].bitcast(F32), ALU.subtract)\
                            .then_inc(pad_lo_done, 1)

                    def lo4(n, m):
                        pool.wait_ge(hi_done, n + 1)
                        pool.tensor_tensor(lo[:, m % 2], xn4[:, m % 2], hi[:, m % 2].bitcast(F32), ALU.subtract)\
                            .then_inc(lo_done, 1)

                    def step(n, m):
                        if exists(n - 1) and exists(n + KT - 1):
                            lo3(n + KT - 1, (m + KT - 1) % V)
                        if exists(n - 2):
                            lo4(n - 2, m)

                    for k in range(KT):
                        lo3(k, k)
                    every_step(pool, step)
                    lo4(NT - 2, 0)
                    lo4(NT - 1, 1)

        with ExitStack() as ctx:
            wr = sbuf(ctx, "w_route", [P, E])
            br = sbuf(ctx, "b_route", [NP, 2, E])
            ones = sbuf(ctx, "ones8", [NP, NP])
            ms = sbuf(ctx, "mean", [P, NP])
            ms2 = sbuf(ctx, "mean_scaled", [P, NP])
            names = ("lg", "shift", "ex", "rw", "rs", "ex2", "rank", "beats", "tmp", "iota")
            t3 = {n: sbuf(ctx, "r_" + n, [NP, 2, E]) for n in names}
            mx, sm, ri = (sbuf(ctx, "r_" + n, [NP, 2]) for n in ("mx", "sm", "ri"))
            loads, scale = sbuf(ctx, "r_loads", [NP, E]), sbuf(ctx, "r_scale", [NP, E])
            pick = sbuf(ctx, "r_pick", [NP, 2, 2])
            pidx = sbuf(ctx, "r_pidx", [NP, 2, 2])
            pidi = sbuf(ctx, "r_pidi", [NP, 2, 2], I32)
            dd, ee, wse = (sbuf(ctx, "r_" + n, [NP, 2]) for n in ("dd", "ee", "wse"))
            wsel = sbuf(ctx, "r_wsel", [NP, 2, 2])
            lp = [psum(ctx, f"r_lg{a}", [NP, 512]) for a in range(2)]
            ldp = psum(ctx, "r_ldp", [NP, 512])
            w1raw = sbuf(ctx, "w1raw_l1", [P, E, F1])
            w1s = sbuf(ctx, "w1split_l1", [P, E, 2, F1], F32R)
            w1_in, w1_hi, w1_lo = (sem(ctx, "p8_" + s) for s in ("w1_in", "w1_hi", "w1_lo"))
            consts, s_v, s_mm, s_a, s_out = (sem(ctx, "p8_" + s) for s in ("consts", "v", "mm", "a", "out"))
            steps, marks = [0], {}
            with nc.Block() as block:
                @block.vector
                def _(dve):
                    def link(ins, mark=None):
                        steps[0] += 1
                        ins.then_inc(s_v, 1)
                        dve.wait_ge(s_v, steps[0])
                        marks[mark] = steps[0]

                    def bc(x):
                        return x.unsqueeze(2).broadcast_to([NP, 2, E])

                    def shifted_exp(src, dst, mark, count):
                        link(dve.tensor_reduce(mx[:], src[:], AX.X, ALU.max))
                        link(dve.tensor_tensor(t3["shift"][:], src[:], bc(mx[:]), ALU.subtract), mark)
                        dve.wait_ge(s_a, count)
                        link(dve.tensor_reduce(sm[:], t3["ex"][:], AX.X, ALU.add))
                        link(dve.reciprocal(ri[:], sm[:]))
                        link(dve.tensor_tensor(dst[:], t3["ex"][:], bc(ri[:]), ALU.mult))

                    dve.wait_ge(consts, 48)
                    link(dve.memset(ones[:], 1.0))
                    for e in range(E):
                        mset = dve.memset(t3["iota"][:, :, e], float(e))
                    link(mset)
                    link(dve.tensor_copy(t3["rank"][:], t3["iota"][:]))
                    link(dve.tensor_reduce(ms[:], MSUM[:].rearrange("p (j k) -> p j k", k=KT), AX.X, ALU.add))
                    link(dve.tensor_scalar(ms2[:], ms[:], 1.0 / PIX, None, ALU.mult), "mean")
                    dve.wait_ge(s_mm, 1)
                    for a in range(2):
                        link(dve.tensor_tensor(t3["lg"][:, a], lp[a][:, 0:E], br[:, a], ALU.add))
                    shifted_exp(t3["lg"], t3["rw"], "exp1", 1)
                    marks["rw"] = steps[0]
                    dve.wait_ge(s_mm, 2)
                    link(dve.tensor_scalar(loads[:], ldp[:, 0:E], float(PIX), None, ALU.mult))
                    link(dve.reciprocal(scale[:], loads[:]))
                    link(dve.tensor_scalar(scale[:], scale[:], CAPACITY, 1.0, ALU.mult, ALU.min))
                    for a in range(2):
                        link(dve.tensor_tensor(t3["lg"][:, a], t3["rw"][:, a], scale[:], ALU.mult))
                    shifted_exp(t3["lg"], t3["rs"], "exp2", 2)
                    for s in range(1, E):
                        l_, h_ = slice(0, E - s), slice(s, E)
                        rs, rk, bt = t3["rs"], t3["rank"], t3["beats"]
                        link(dve.tensor_tensor(bt[:, :, l_], rs[:, :, h_], rs[:, :, l_], ALU.is_gt))
                        link(dve.tensor_tensor(rk[:, :, l_], rk[:, :, l_], bt[:, :, l_], ALU.add))
                        link(dve.tensor_tensor(rk[:, :, h_], rk[:, :, h_], bt[:, :, l_], ALU.subtract))
                    for k in range(2):
                        for src, dst in ((t3["rs"], pick), (t3["iota"], pidx)):
                            link(dve.scalar_tensor_tensor(out=t3["tmp"][:], in0=t3["rank"][:], scalar=float(k),
                                                          in1=src[:], op0=ALU.is_equal, op1=ALU.mult))
                            link(dve.tensor_reduce(dst[:, :, k], t3["tmp"][:], AX.X, ALU.add))
                    link(dve.tensor_copy(pidi[:], pidx[:]))
                    link(dve.tensor_tensor(dd[:], pick[:, :, 1], pick[:, :, 0], ALU.subtract), "exp3")
                    dve.wait_ge(s_a, 3)
                    link(dve.tensor_scalar(wse[:], ee[:], 1.0, None, ALU.add))
                    link(dve.reciprocal(wsel[:, :, 0], wse[:]))
                    link(dve.tensor_tensor(wsel[:, :, 1], wsel[:, :, 0], ee[:], ALU.mult), "out")

                @block.scalar
                def _(act):
                    for n, mark in enumerate(("exp1", "exp2")):
                        act.wait_ge(s_v, marks[mark])
                        act.activation(t3["ex"][:], t3["shift"][:], ACT.Exp).then_inc(s_a, 1)
                    act.wait_ge(s_v, marks["exp3"])
                    act.activation(ee[:], dd[:], ACT.Exp).then_inc(s_a, 1)

                @block.tensor
                def _(pe):
                    pe.wait_ge(consts, 48)
                    pe.wait_ge(s_v, marks["mean"])
                    for a in range(2):
                        mm = pe.matmul(lp[a][:, 0:E], ms2[C * a:C * a + C, :], wr[C * a:C * a + C, :],
                                       start=True, stop=True)
                    mm.then_inc(s_mm, 1)
                    pe.wait_ge(s_v, marks["rw"])
                    for a in range(2):
                        mm = pe.matmul(ldp[:, 0:E], ones[:], t3["rw"][:, a], start=(a == 0), stop=(a == 1))
                    mm.then_inc(s_mm, 1)

                @block.gpsimd
                def _(pool):
                    pool.wait_ge(w1_in, 16)
                    pool.tensor_copy(w1s[:, :, 0, :], w1raw[:]).then_inc(w1_hi, 1)
                    pool.wait_ge(w1_hi, 1)
                    pool.tensor_tensor(w1s[:, :, 1, :], w1raw[:], w1s[:, :, 0, :].bitcast(F32), ALU.subtract)\
                        .then_inc(w1_lo, 1)

                @block.sync
                def _(sp):
                    sp.dma_start(w1raw[:], A["w1_l1"]).then_inc(w1_in, 16)
                    sp.dma_start(wr[0:C, :], A["w_route"]).then_inc(consts, 16)
                    sp.dma_start(wr[C:P, :], A["w_route"]).then_inc(consts, 16)
                    sp.dma_start(br[:].rearrange("p a e -> p (a e)"), A["b_route"].partition_broadcast(NP))\
                        .then_inc(consts, 16)
                    sp.wait_ge(w1_lo, 1)
                    sp.dma_start(W1D.rearrange("e p s f -> p e (s f)"), w1s[:].bitcast(F32).rearrange("p e s f -> p e (s f)"))\
                        .then_inc(s_out, 16)
                    sp.wait_ge(s_v, marks["out"])
                    sp.dma_start(IDX, pidi[:].rearrange("p a s -> p (a s)")).then_inc(s_out, 16)
                    sp.dma_start(WSEL, wsel[:].rearrange("p a s -> p (a s)")).then_inc(s_out, 16)
                    sp.wait_ge(s_out, 48)

        with ExitStack() as ctx:
            w1s = sbuf(ctx, "w1sel", [P, 2, 4, 2, F1], F32R)
            w2r = sbuf(ctx, "w2raw", [P, 2, 4, C])
            w2s = sbuf(ctx, "w2sel", [P, 2, 4, C])
            b1s = sbuf(ctx, "b1sel", [P, 2, 4])
            b2r = sbuf(ctx, "b2raw", [P, 2, 2])
            b2t = sbuf(ctx, "b2tmp", [P, 2, 1])
            b2s = sbuf(ctx, "b2sel", [P, 2, 1])
            wse = sbuf(ctx, "w_all", [P, NP, 4])
            wsh = sbuf(ctx, "w_half", [P, NP, 2])
            gam = sbuf(ctx, "gamma", [P, 1])
            bet = sbuf(ctx, "beta", [P, 1])
            idr = sbuf(ctx, "idx", [1, NP * 4], I32)
            S = sbuf(ctx, "tokens4", [P, KT, 2, TW], F32R)
            u = sbuf(ctx, "tokens_plus_y", [P, KT, TW])
            hs = sbuf(ctx, "hidden1", [P, 2, 4, TW])
            nrm = sbuf(ctx, "ln5_out", [P, 2, TW])
            o2 = sbuf(ctx, "out_tile", [P, 2, TW])
            hp = psum(ctx, "hidden1_psum", [P, 2, 512])
            yp = psum(ctx, "y1_psum", [P, 1, 512])
            ln = Norm(ctx, "ln5", 3, 2, group=KT)
            consts, idx_in, w2_done, b2_a, b2_done, up_done, gelu_done, down_done, u_done, scaled, out_done = (
                sem(ctx, "p9_" + s) for s in ("consts", "idx", "w2", "b2a", "b2", "up", "gelu", "down", "u",
                                              "scaled", "out"))
            w_in = [sem(ctx, f"p9_w{b}") for b in range(2)]
            split_in = [sem(ctx, f"p9_split{k}") for k in range(KT)]
            tok_in = [sem(ctx, f"p9_tok{k}") for k in range(KT)]
            stored = [sem(ctx, f"p9_stored{b}") for b in range(2)]
            WIN = 16 * (4 * 3 + 4)

            def every_pair(engine, body):
                for i in units(engine, NP // 2 - 1):
                    for b in range(2):
                        body(2 * i + b, b, False)
                for b in range(2):
                    body(NP - 2 + b, b, b == 1)

            with nc.Block() as block:
                @block.sync
                def _(sp):
                    sp.dma_start(idr[:], IDX.rearrange("(o j) s -> o (j s)", o=1)).then_inc(idx_in, 16)
                    sp.dma_start(wse[:], WSEL.rearrange("j s -> (j s)").partition_broadcast(P)
                                 .rearrange("p (j s) -> p j s", s=4)).then_inc(consts, 16)
                    for a in range(2):
                        sp.dma_start(wsh[C * a:C * a + C], WSEL[:, 2 * a:2 * a + 2].partition_broadcast(C))\
                            .then_inc(consts, 16)
                        sp.dma_start(gam[C * a:C * a + C, :], A["gamma"]).then_inc(consts, 16)
                        sp.dma_start(bet[C * a:C * a + C, :], A["beta"]).then_inc(consts, 16)
                    sp.wait_ge(idx_in, 16)

                    def load_weights(p, b):
                        for q in range(4):
                            e = sp.value_load(idr[0:1, bass.ds(p * 4 + q, 1)], min_val=0, max_val=E - 1)
                            sp.dma_start(w1s[:, b, q].bitcast(F32), W1D[bass.ds(e, 1)].rearrange("o p s f -> (o p) s f"))\
                                .then_inc(w_in[b], 16)
                            sp.dma_start(w2r[:, b, q], A["w2_l1"][bass.ds(e, 1)].rearrange("o f c -> (o f) c"))\
                                .then_inc(w_in[b], 16)
                            sp.dma_start(b1s[:, b, q:q + 1], A["b1_l1"][bass.ds(e, 1)].rearrange("o f u -> (o f) u"))\
                                .then_inc(w_in[b], 16)
                            a, s = divmod(q, 2)
                            sp.dma_start(b2r[C * a:C * a + C, b, s:s + 1],
                                         A["b2_l1"][bass.ds(e, 1)].rearrange("o c u -> (o c) u")).then_inc(w_in[b], 16)

                    def load_split(p, k):
                        sp.dma_start(S[:, k].bitcast(F32), SD4[bass.ds(KT * p + k, 1)].rearrange("o a p w -> (o p) a w"))\
                            .then_inc(split_in[k], 16)

                    def load_tokens(p, k):
                        sp.dma_start(u[:, k], XN4[bass.ds(KT * p + k, 1)].rearrange("o p w -> (o p) w"))\
                            .then_inc(tok_in[k], 16)

                    def pair(p, b, last):
                        if not last:
                            wait(sp, gelu_done, 4 * KT * p)
                            wait(sp, w2_done, p)
                            wait(sp, b2_done, p)
                            load_weights(p + 1, 1 - b)
                            for k in range(KT):
                                sp.wait_ge(up_done, 4 * (KT * p + k) + 4)
                                load_split(p + 1, k)
                        for k in range(KT):
                            if not last:
                                sp.wait_ge(ln.centred, KT * p + k + 1)
                                load_tokens(p + 1, k)
                            sp.wait_ge(out_done, KT * p + k + 1)
                            sp.dma_start(out[bass.ds(p, 1), :, TW * k:TW * (k + 1)].rearrange("o p w -> (o p) w"),
                                         o2[:, (KT * b + k) % 2]).then_inc(stored[(KT * b + k) % 2], 16)

                    load_weights(0, 0)
                    for k in range(KT):
                        load_split(0, k)
                        load_tokens(0, k)
                    every_pair(sp, pair)
                    for b in range(2):
                        sp.wait_ge(stored[b], 16 * NT // 2)

                @block.tensor
                def _(pe):
                    def up(p, b, k):
                        pe.wait_ge(split_in[k], 16 * p + 16)
                        for q in range(4):
                            wait(pe, gelu_done, 4 * (KT * p + k) + q - 1)
                            pe.matmul(hp[:, q % 2, 0:TW], w1s[:, b, q, 0, :], S[:, k, q // 2, :], start=True, stop=False)
                            pe.matmul(hp[:, q % 2, 0:TW], w1s[:, b, q, 1, :], S[:, k, q // 2, :], start=False, stop=True)\
                                .then_inc(up_done, 1)

                    def down(p, b, k):
                        n = KT * p + k
                        pe.wait_ge(gelu_done, 4 * n + 4)
                        wait(pe, u_done, n)
                        if k == 0:
                            pe.wait_ge(w2_done, p + 1)
                        for s in range(2):
                            for a in range(2):
                                mm = pe.matmul(yp[C * a:C * a + C, 0, 0:TW], w2s[:, b, 2 * a + s, :],
                                               hs[:, (KT * b + k) % 2, 2 * a + s, :], start=(s == 0), stop=(s == 1))
                        mm.then_inc(down_done, 1)

                    def pair(p, b, last):
                        pe.wait_ge(w_in[b], WIN // 2 * (p - b) + WIN)
                        for k in range(KT + 1):
                            if k < KT:
                                up(p, b, k)
                            if k >= 1:
                                down(p, b, k - 1)
                        for k in range(KT + 1):
                            if k < KT:
                                pe.wait_ge(u_done, KT * p + k + 1)
                                ln.pe_centre(pe, KT * p + k, k, u[:, k])
                            if k >= 1:
                                ln.pe_var(pe, KT * p + k - 1, k - 1)

                    every_pair(pe, pair)

                @block.scalar
                def _(act):
                    act.wait_ge(consts, 7 * 16)

                    def pair(p, b, last):
                        act.wait_ge(w_in[b], WIN // 2 * (p - b) + WIN)
                        for k in range(KT):
                            n = KT * p + k
                            wait(act, down_done, n - 1)
                            for q in range(4):
                                act.wait_ge(up_done, 4 * n + q + 1)
                                act.activation(hs[:, (KT * b + k) % 2, q], hp[:, q % 2, 0:TW], ACT.Gelu,
                                               bias=b1s[:, b, q:q + 1]).then_inc(gelu_done, 1)
                        for k in range(KT + 3):
                            if k < KT:
                                ln.act_square(act, KT * p + k, k)
                            if 1 <= k < KT + 1:
                                ln.act_seed(act, KT * p + k - 1, k - 1, 1)
                            if k >= 3:
                                n, v = KT * p + k - 3, (KT * b + k - 3) % 2
                                act.wait_ge(ln.normed, n + 1)
                                act.activation(nrm[:, v], nrm[:, v], ACT.Identity, scale=gam[:, 0:1], bias=bet[:, 0:1])\
                                    .then_inc(scaled, 1)

                    every_pair(act, pair)

                @block.vector
                def _(dve):
                    dve.wait_ge(consts, 7 * 16)

                    def weigh(p, b):
                        dve.wait_ge(w_in[b], WIN // 2 * (p - b) + WIN)
                        for q in range(4):
                            ts = dve.tensor_scalar(w2s[:, b, q], w2r[:, b, q], wse[:, bass.ds(p, 1), q], None, ALU.mult)
                        ts.then_inc(w2_done, 1)
                        dve.tensor_scalar(b2t[:, b], b2r[:, b, 0:1], wsh[:, bass.ds(p, 1), 0], None, ALU.mult)\
                            .then_inc(b2_a, 1)
                        dve.wait_ge(b2_a, p + 1)
                        dve.scalar_tensor_tensor(out=b2s[:, b], in0=b2r[:, b, 1:2], scalar=wsh[:, bass.ds(p, 1), 1],
                                                 in1=b2t[:, b], op0=ALU.mult, op1=ALU.add).then_inc(b2_done, 1)

                    def pair(p, b, last):
                        dve.wait_ge(b2_done, p + 1)
                        for k in range(KT):
                            dve.wait_ge(tok_in[k], 16 * p + 16)
                            dve.wait_ge(down_done, KT * p + k + 1)
                            dve.scalar_tensor_tensor(out=u[:, k], in0=yp[:, 0, 0:TW], scalar=b2s[:, b], in1=u[:, k],
                                                     op0=ALU.add, op1=ALU.add).then_inc(u_done, 1)
                        if not last:
                            weigh(p + 1, 1 - b)
                        for k in range(KT):
                            n, v = KT * p + k, KT * b + k
                            ln.dve_newton(dve, n, k, EPS_T)
                            wait(dve, out_done, n - 1)
                            ln.dve_scale(dve, n, k, nrm[:, v % 2])

                    weigh(0, 0)
                    every_pair(dve, pair)

                @block.gpsimd
                def _(pool):
                    def pair(p, b, last):
                        for k in range(KT):
                            n, v = KT * p + k, KT * b + k
                            pool.wait_ge(scaled, n + 1)
                            wait(pool, stored[v % 2], 8 * (n - v % 2))
                            pool.tensor_tensor(o2[:, v % 2], nrm[:, v % 2], tile(X, n), ALU.add).then_inc(out_done, 1)

                    every_pair(pool, pair)


def kernel(**inputs):
    import concourse.bacc as bacc
    import numpy as np
    from concourse.bass_utils import run_bass_kernel_spmd

    v = {k: np.ascontiguousarray(a) for k, a in inputs.items()}
    f = np.float32

    def zeros(*shape):
        return np.zeros(shape, f)

    a = {"x": v["x"].reshape(NP, P, PIX)}
    gate_w = zeros(2, C, 3, NQ, 2, 3)
    for lr, w in enumerate((v["L0_conv_w_l"], v["L0_conv_w_r"])):
        for im in range(2):
            for dt in range(3):
                gate_w[im, HALF * lr:HALF * lr + HALF, :, im + 2 - dt, lr, :] = w[0, :, dt].transpose(0, 2, 1)
    a["gate_w"] = gate_w.reshape(P, 3, GM)
    a["b_l"], a["b_r"] = v["L0_conv_b_l"], v["L0_conv_b_r"]
    gate_sel = zeros(4, NQ, 2, 3, 2, 3, 2, T)
    for h in range(2):
        for jj in range(4):
            for q in range(NQ):
                for lr in range(2):
                    for dy in range(3):
                        gate_sel[jj, q, lr, dy, h, dy, lr, (2 * (4 * h + jj) - 1 + q) % T] = 1
    a["gate_sel"] = gate_sel.reshape(4 * GM, 2, 3, 2 * T)
    w_gate = zeros(2, C, 2, E)
    conv_w = zeros(2, C, 9, 2, C)
    for im in range(2):
        w_gate[im, :, im] = v["L0_ffn_Wg"]
        conv_w[im, :, :, im] = v["L1_conv_weights"].reshape(C, C, 9).transpose(1, 2, 0)
    a["w_gate"] = w_gate.reshape(P, 2 * E)
    a["b_gate"] = np.tile(v["L0_ffn_bg"], SUB * 2)
    w1 = v["L0_ffn_W1"].transpose(1, 0, 2).reshape(C, E * H0)
    a["w1"] = np.concatenate([w1, w1])
    a["w2"] = v["L0_ffn_W2"].reshape(E, CH0, P, C).transpose(2, 0, 1, 3)
    a["b1"] = v["L0_ffn_b1"].reshape(E, CH0, P).transpose(2, 0, 1)
    a["b2"] = np.concatenate([v["L0_ffn_b2"].T, v["L0_ffn_b2"].T])
    a["conv_w"] = conv_w.reshape(P, 9, P)
    a["factor"] = v["L1_conv_real_scaling_factor"].reshape(C, 1)
    a["w_route"] = v["L1_ffn_Wr"]
    a["b_route"] = np.tile(v["L1_ffn_br"], 2)
    w1 = v["L1_ffn_W1"].transpose(1, 0, 2)
    a["w1_l1"] = np.concatenate([w1, w1])
    a["w2_l1"] = v["L1_ffn_W2"]
    a["b1_l1"] = v["L1_ffn_b1"].reshape(E, F1, 1)
    a["b2_l1"] = v["L1_ffn_b2"].reshape(E, C, 1)
    a["gamma"], a["beta"] = v["L1_ffn_gamma"].reshape(C, 1), v["L1_ffn_beta"].reshape(C, 1)
    block = np.kron(np.eye(2), np.ones((C, C))) / C
    a["centre"], a["average"], a["ident"] = (np.eye(P) - block).astype(f), block.astype(f), np.eye(P, dtype=f)

    nc = bacc.Bacc("TRN2", target_bir_lowering=False, num_devices=1)
    arrays = {f"in_{k}": np.ascontiguousarray(x) for k, x in a.items()}
    aps = {k: nc.dram_tensor(f"in_{k}", x.shape, mybir.dt.from_np(x.dtype), kind="ExternalInput").ap()
           for k, x in a.items()}
    out = nc.dram_tensor("out", (NP, P, PIX), F32, kind="ExternalOutput").ap()
    build(nc, aps, out)
    r = run_bass_kernel_spmd(nc, [arrays], core_ids=[0])
    return r.results[0]["out"].reshape(T, C, HH, WW)
```

```python
from contextlib import ExitStack

import concourse.bass as bass
from concourse import mybir

F32 = mybir.dt.float32
F32R = mybir.dt.float32r
I32 = mybir.dt.int32
ALU = mybir.AluOpType
ACT = mybir.ActivationFunctionType
AX = mybir.AxisListType

P = 128
T, C, HH, WW = 16, 64, 56, 56
PIX = HH * WW
NP = T // 2
ROWS = 8
KT = HH // ROWS
NT = NP * KT
TW = ROWS * WW
SUB = 4
GW = TW // SUB
HALF = 16
E = 8
H0 = 256
CH0 = H0 // P
F1 = 128
PADW = WW + 2
NQ = 4
GM = NQ * 2 * 3
GS = 32
CAPACITY = float(-(-T * PIX * 5 // (4 * E)))
EPS_C, EPS_T = 1e-6, 1e-5


def build(nc, A, out):
    top = ExitStack()

    def sem(ctx, name):
        return ctx.enter_context(nc.semaphore(name))

    def sbuf(ctx, name, shape, dt=F32):
        return ctx.enter_context(nc.sbuf_tensor(name, shape, dt))

    def psum(ctx, name, shape, dt=F32):
        return ctx.enter_context(nc.psum_tensor(name, shape, dt))

    def dram(name, shape, dt=F32):
        return nc.dram_tensor(name, shape, dt).ap()

    XLR = dram("scr_xlr", [NT, 4 * HALF, TW])
    GPART = dram("scr_gate_part", [NT, P, TW // 4])
    Z = dram("scr_gated", [NT + 2 * KT, 4 * HALF, TW])
    SD2 = dram("scr_split2", [NT, 2, P, TW])
    WT = dram("scr_wtok", [NT, 2 * E, TW])
    SD4 = dram("scr_split4", [NT, 2, P, TW])
    XN4 = dram("scr_xn4", [NT, P, TW])
    W1D = dram("scr_w1split", [E, P, 2, F1])
    IDX = dram("scr_idx", [NP, 4], I32)
    WSEL = dram("scr_wsel", [NP, 4])

    X = sbuf(top, "X", [P, NT, TW])
    CEN = sbuf(top, "centre", [P, P])
    AVG = sbuf(top, "average", [P, P])
    EPS = sbuf(top, "eps", [P, 2])
    MSUM = sbuf(top, "msum", [P, NT])

    def tile(x, n):
        return x[:, bass.ds(n, 1), :].rearrange("p o w -> p (o w)")

    def split_rows(scratch, n, part):
        return scratch[bass.ds(n, 1), :, C * part:C * part + C].rearrange("o a c w -> (o a) c w")

    def exists(n):
        return not isinstance(n, int) or 0 <= n < NT

    def rows(ap):
        return ap.rearrange("p (r w) -> p r w", w=WW)

    def wait(engine, s, value):
        if not isinstance(value, int) or value > 0:
            engine.wait_ge(s, value)

    def units(engine, n):
        yield 0
        with engine.Fori(1, n) as i:
            yield i

    def every_tile(engine, step, unit, lag):
        for i in units(engine, NT // unit):
            for m in range(unit):
                step(unit * i + m, m)
        for m in range(lag):
            step(NT + m, m)

    class Norm:

        def __init__(self, ctx, tag, nx, nv, depth=2, group=0, xc=None, split=None):
            self.nx, self.nv, self.depth, self.group = nx, nv, depth, group
            self.xc = xc if xc is not None else psum(ctx, tag + "_xc", [P, nx, 512])
            self.var = psum(ctx, tag + "_var", [P, nv, 512])
            self.split, self.average = split is not None, split
            if split:
                self.sq_hi = sbuf(ctx, tag + "_sq_hi", [P, depth, TW], F32R)
                self.sq_lo = sbuf(ctx, tag + "_sq_lo", [P, depth, TW], F32R)
                self.squared_hi, self.squared_lo = sem(ctx, tag + "_squared_hi"), sem(ctx, tag + "_squared_lo")
            self.sq = sbuf(ctx, tag + "_sq", [P, depth, TW])
            self.r = sbuf(ctx, tag + "_r", [P, depth, TW])
            self.rr = sbuf(ctx, tag + "_rr", [P, depth, TW])
            self.q = sbuf(ctx, tag + "_q", [P, depth, TW])
            self.g = sbuf(ctx, tag + "_g", [P, depth, TW])
            self.centred, self.squared, self.var_ready, self.seeded = (
                sem(ctx, tag + s) for s in ("_centred", "_squared", "_var_ready", "_seeded"))
            self.seed_squared, self.q_done, self.g_done, self.normed = (
                sem(ctx, tag + s) for s in ("_seed_squared", "_q_done", "_g_done", "_normed"))

        def freed(self, n, m, bufs):
            if self.group and m % self.group < bufs:
                return n - m % self.group
            return n + 1 - bufs

        def at(self, m, bufs):
            return (m % self.group if self.group else m) % bufs

        def pe_centre(self, pe, n, m, x):
            b = self.at(m, self.nx)
            wait(pe, self.normed, self.freed(n, m, self.nx))
            pe.matmul(self.xc[:, b, 0:TW], CEN[:], x, start=True, stop=True).then_inc(self.centred, 1)

        def act_square(self, act, n, m):
            act.wait_ge(self.centred, n + 1)
            wait(act, self.var_ready, self.freed(n, m, self.depth))
            if self.split:
                act.activation(self.sq_hi[:, self.at(m, self.depth)], self.xc[:, self.at(m, self.nx), 0:TW], ACT.Square)\
                    .then_inc(self.squared_hi, 1)
            act.activation(self.sq[:, self.at(m, self.depth)], self.xc[:, self.at(m, self.nx), 0:TW], ACT.Square)\
                .then_inc(self.squared, 1)

        def pool_square_lo(self, pool, n, m):
            b = self.at(m, self.depth)
            pool.wait_ge(self.squared_hi, n + 1)
            pool.wait_ge(self.squared, n + 1)
            pool.tensor_tensor(self.sq_lo[:, b], self.sq[:, b], self.sq_hi[:, b].bitcast(F32), ALU.subtract)\
                .then_inc(self.squared_lo, 1)

        def pe_var(self, pe, n, m):
            b = self.at(m, self.depth)
            if self.split:
                pe.wait_ge(self.squared_lo, n + 1)
                wait(pe, self.q_done, self.freed(n, m, self.nv))
                var = self.var[:, self.at(m, self.nv), 0:TW]
                pe.matmul(var, self.average[:], self.sq_hi[:, b], start=True, stop=False)
                pe.matmul(var, self.average[:], self.sq_lo[:, b], start=False, stop=True).then_inc(self.var_ready, 1)
                return
            pe.wait_ge(self.squared, n + 1)
            wait(pe, self.q_done, self.freed(n, m, self.nv))
            pe.matmul(self.var[:, self.at(m, self.nv), 0:TW], AVG[:], self.sq[:, self.at(m, self.depth)],
                      start=True, stop=True).then_inc(self.var_ready, 1)

        def act_seed(self, act, n, m, eps_col):
            self.act_r(act, n, m, eps_col)
            self.act_rr(act, n, m)

        def act_r(self, act, n, m, eps_col):
            b = self.at(m, self.depth)
            act.wait_ge(self.var_ready, n + 1)
            wait(act, self.g_done, self.freed(n, m, self.depth))
            act.activation(self.r[:, b], self.var[:, self.at(m, self.nv), 0:TW], ACT.Abs_reciprocal_sqrt,
                           bias=EPS[:, eps_col:eps_col + 1]).then_inc(self.seeded, 1)

        def act_rr(self, act, n, m):
            b = self.at(m, self.depth)
            act.wait_ge(self.seeded, n + 1)
            act.activation(self.rr[:, b], self.r[:, b], ACT.Square).then_inc(self.seed_squared, 1)

        def dve_newton(self, dve, n, m, eps):
            b = self.at(m, self.depth)
            dve.wait_ge(self.seed_squared, n + 1)
            dve.scalar_tensor_tensor(out=self.q[:, b], in0=self.var[:, self.at(m, self.nv), 0:TW], scalar=eps,
                                     in1=self.rr[:, b], op0=ALU.add, op1=ALU.mult).then_inc(self.q_done, 1)
            dve.wait_ge(self.q_done, n + 1)
            dve.scalar_tensor_tensor(out=self.g[:, b], in0=self.q[:, b], scalar=-3.0,
                                     in1=self.r[:, b], op0=ALU.add, op1=ALU.mult).then_inc(self.g_done, 1)

        def dve_scale(self, dve, n, m, dst, accum=None, half_gamma=-0.5):
            dve.wait_ge(self.g_done, n + 1)
            xc, g = self.xc[:, self.at(m, self.nx), 0:TW], self.g[:, self.at(m, self.depth)]
            dve.scalar_tensor_tensor(out=dst, in0=xc, scalar=half_gamma, in1=g, op0=ALU.mult, op1=ALU.mult,
                                     accum_out=accum).then_inc(self.normed, 1)

        def dve_norm(self, dve, n, m, eps, dst, accum=None):
            self.dve_newton(dve, n, m, eps)
            self.dve_scale(dve, n, m, dst, accum)

    with top:
        moe0 = ExitStack()
        w1hi = sbuf(moe0, "w1hi", [P, E * H0], F32R)
        w1lo = sbuf(moe0, "w1lo", [P, E * H0], F32R)

        gates = ExitStack()
        pb = [sbuf(gates, f"gate_rows{h}", [4 * GM, HH + 2, WW]) for h in range(2)]
        gs = sbuf(gates, "gate_sel", [4 * GM, 2, 3, 2 * T])
        gb = sbuf(gates, "gate_bias", [2 * T, 1])
        gbc = sbuf(gates, "gate_bc", [P, 4, P])
        loaded = sem(gates, "gates_loaded")

        with ExitStack() as ctx:
            UNIT = 8
            SW = TW // 4
            gw = sbuf(ctx, "gate_w", [P, 3, GS])
            xn = sbuf(ctx, "xn1", [P, 4, TW])
            gp = sbuf(ctx, "gate_part", [P, 2, 4, SW])
            gps = psum(ctx, "gate_psum", [P, 2, 512])
            ln = Norm(ctx, "ln1", 4, 2)
            w1raw = sbuf(ctx, "w1raw", [P, E * H0])
            w1_in, w1_hi, w1_lo = (sem(ctx, "p1_" + s) for s in ("w1_in", "w1_hi", "w1_lo"))
            consts, eps_set, x_in, added = (sem(ctx, "p1_" + s) for s in ("consts", "eps", "x", "added"))
            part_ready, part_copied = sem(ctx, "p1_part"), sem(ctx, "p1_part_copied")
            xn_stored = [sem(ctx, f"p1_xn_stored{b}") for b in range(4)]
            gp_stored = [sem(ctx, f"p1_gp_stored{b}") for b in range(2)]
            with nc.Block() as block:
                @block.sync
                def _(sp):
                    def load(n, tiles):
                        sp.dma_start(X[:, bass.ds(n, tiles), :], A["x"][bass.ds(n, tiles)].rearrange("k p w -> p k w"))\
                            .then_inc(x_in, 16)

                    def step(n, m):
                        if m == 0 and exists(n) and exists(n - UNIT):
                            sp.wait_ge(x_in, 2 * n + 16)
                            load(n, UNIT)
                        if exists(n - UNIT):
                            sp.wait_ge(ln.normed, n - UNIT + 1)
                            for a in range(2):
                                sp.dma_start(XLR[bass.ds(n - UNIT, 1), 2 * HALF * a:2 * HALF * (a + 1)]
                                             .rearrange("o c w -> (o c) w"),
                                             xn[C * a:C * a + 2 * HALF, m % 4]).then_inc(xn_stored[m % 4], 16)
                        if m % 4 == 3 and exists(n - UNIT):
                            sp.wait_ge(part_copied, n - UNIT + 1)
                            sp.dma_start(GPART[bass.ds(n - UNIT - 3, 4)].rearrange("n p w -> p n w"), gp[:, m // 4])\
                                .then_inc(gp_stored[m // 4], 16)

                    sp.dma_start(CEN[:], A["centre"]).then_inc(consts, 16)
                    load(0, 1)
                    sp.dma_start(AVG[:], A["average"]).then_inc(consts, 16)
                    sp.dma_start(gw[:], A["gate_w"]).then_inc(consts, 16)
                    sp.wait_ge(x_in, 16)
                    load(1, UNIT - 1)
                    sp.dma_start(w1raw[:], A["w1"]).then_inc(w1_in, 16)
                    every_tile(sp, step, UNIT, 0)
                    sp.dma_start(gs[:], A["gate_sel"]).then_inc(loaded, 16)
                    sp.dma_start(gbc[:], A["gate_bc"]).then_inc(loaded, 16)
                    sp.dma_start(gb[0:T, :], A["b_l"].partition_broadcast(T)).then_inc(loaded, 16)
                    sp.dma_start(gb[T:2 * T, :], A["b_r"].partition_broadcast(T)).then_inc(loaded, 16)
                    for j in range(NP):
                        if j == NP - 2:
                            for m in range(UNIT):
                                step(NT + m, m)
                        groups = KT * (j + 1) // 4 + 1 if j < NP - 2 else NT // 4
                        for b in range(2):
                            sp.wait_ge(gp_stored[b], 16 * ((groups + 1 - b) // 2))
                        h, jj = divmod(j, 4)
                        sp.dma_start(pb[h][GM * jj:GM * (jj + 1), 1:HH + 1, :].rearrange("p (x r) w -> p x (r w)", r=2),
                                     GPART[KT * j:KT * (j + 1)].rearrange("k (q g) w -> g (k q) w", g=GS)[0:GM])\
                            .then_inc(loaded, 16)
                    for b in range(4):
                        sp.wait_ge(xn_stored[b], 32 * NT // 4)
                    for b in range(2):
                        sp.wait_ge(gp_stored[b], 16 * NT // 8)

                @block.tensor
                def _(pe):
                    pe.wait_ge(consts, 48)

                    def gate(n, m):
                        pe.wait_ge(ln.normed, n + 1)
                        wait(pe, part_copied, n - 1)
                        for q in range(4):
                            o = rows(gps[GS * q:GS * (q + 1), m % 2, 0:SW])
                            src = rows(xn[:, m % 4, SW * q:SW * (q + 1)])
                            pe.matmul(o, gw[:, 1, :], src, start=True, stop=False)
                            pe.matmul(o[:, :, 1:WW], gw[:, 0, :], src[:, :, 0:WW - 1], start=False, stop=False)
                            mm = pe.matmul(o[:, :, 0:WW - 1], gw[:, 2, :], src[:, :, 1:WW], start=False, stop=True)
                        mm.then_inc(part_ready, 1)

                    def step(n, m):
                        if exists(n):
                            if isinstance(n, int):
                                pe.wait_ge(x_in, 16 if n == 0 else 32)
                            elif m == 0:
                                pe.wait_ge(x_in, 2 * n + 32)
                            ln.pe_centre(pe, n, m, tile(X, n))
                        if exists(n - 1):
                            ln.pe_var(pe, n - 1, m - 1)
                        if exists(n - 3):
                            gate(n - 3, m - 3)

                    every_tile(pe, step, UNIT, 3)

                @block.scalar
                def _(act):
                    act.wait_ge(eps_set, 2)

                    def copy_part(n, m):
                        act.wait_ge(part_ready, n + 1)
                        if m % 4 == 0:
                            wait(act, gp_stored[m // 4], 2 * (n - m))
                        act.activation(gp[:, m // 4, m % 4], gps[:, m % 2, 0:SW], ACT.Copy).then_inc(part_copied, 1)

                    def step(n, m):
                        if exists(n):
                            ln.act_square(act, n, m)
                        if exists(n - 1):
                            ln.act_seed(act, n - 1, m - 1, 0)
                        if exists(n - 4):
                            copy_part(n - 4, (m - 4) % UNIT)
                        if isinstance(n, int) and n == UNIT - 1:
                            act.wait_ge(w1_in, 16)
                            act.activation(w1hi[:], w1raw[:], ACT.Copy).then_inc(w1_hi, 1)

                    every_tile(act, step, UNIT, 4)

                @block.vector
                def _(dve):
                    dve.memset(EPS[:, 0:1], EPS_C).then_inc(eps_set, 1)
                    dve.memset(EPS[:, 1:2], EPS_T).then_inc(eps_set, 1)

                    def step(n, m):
                        ln.dve_newton(dve, n, m, EPS_C)
                        wait(dve, xn_stored[m % 4], 8 * (n - m % 4))
                        wait(dve, part_ready, n - 3)
                        wait(dve, added, n - 3)
                        ln.dve_scale(dve, n, m, xn[:, m % 4])

                    every_tile(dve, step, UNIT, 0)

                @block.gpsimd
                def _(pool):
                    def step(n, m):
                        pool.wait_ge(ln.normed, n + 1)
                        x = tile(X, n)
                        pool.tensor_tensor(x, x, xn[:, m % 4], ALU.add).then_inc(added, 1)
                        if isinstance(n, int) and n == UNIT - 1:
                            pool.wait_ge(w1_hi, 1)
                            pool.tensor_tensor(w1lo[:], w1raw[:], w1hi[:].bitcast(F32), ALU.subtract).then_inc(w1_lo, 1)

                    every_tile(pool, step, UNIT, 0)

        with ExitStack() as ctx:
            gt = sbuf(ctx, "gates", [P, 2, TW])
            z = sbuf(ctx, "gated", [P, 4, KT, TW])
            gps = psum(ctx, "gate_sum", [2 * T, 2, 512])
            bps = psum(ctx, "gate_bc_psum", [P, 4, 512])
            zeroed, summed, tanhed, spread, gated, stored = (
                sem(ctx, "p2_" + s) for s in ("zeroed", "summed", "tanhed", "spread", "gated", "stored"))
            z_in = sem(ctx, "p2_z_in")
            with nc.Block() as block:
                def pair_rows(j):
                    return z[C * (j % 2):C * (j % 2) + C, j // 2]

                @block.sync
                def _(sp):
                    for j in range(NP):
                        sp.dma_start(pair_rows(j), XLR[KT * j:KT * (j + 1)].rearrange("k c w -> c k w"))\
                            .then_inc(z_in, 16)
                    for k in range(KT):
                        sp.wait_ge(gated, 4 * (k + 1))
                        for h in range(2):
                            sp.dma_start(Z[KT:KT + NT].rearrange("(f h k) c w -> h k c f w", h=2, k=KT)[h, k],
                                         z[C * h:C * h + C, :, k, :]).then_inc(stored, 16)
                        sp.dma_start(Z[k], pair_rows(NP - 1)[:, k]).then_inc(stored, 16)
                        sp.dma_start(Z[KT + NT + k], pair_rows(0)[:, k]).then_inc(stored, 16)
                    sp.wait_ge(stored, 16 * 4 * KT)

                @block.gpsimd
                def _(pool):
                    pool.memset(gt[:], 0.0).then_inc(zeroed, 1)

                @block.vector
                def _(dve):
                    for h in range(2):
                        for r in (0, HH + 1):
                            dve.memset(pb[h][:, r, :], 0.0).then_inc(zeroed, 1)
                    dve.wait_ge(z_in, 16 * NP)
                    for k in range(KT):
                        for f in range(4):
                            dve.wait_ge(spread, 4 * k + f + 1)
                            dve.tensor_tensor(z[:, f, k], bps[:, f, 0:TW], z[:, f, k], ALU.mult).then_inc(gated, 1)

                @block.tensor
                def _(pe):
                    pe.wait_ge(loaded, 16 * (4 + NP))
                    pe.wait_ge(zeroed, 5)

                    def gate_sum(k):
                        if k >= 2:
                            pe.wait_ge(tanhed, k - 1)
                        for h in range(2):
                            for dy in range(3):
                                mm = pe.matmul(rows(gps[:, k % 2, 0:TW]), gs[:, h, dy, :],
                                               pb[h][:, ROWS * k + dy:ROWS * k + dy + ROWS, :],
                                               start=(h == 0 and dy == 0), stop=(h == 1 and dy == 2))
                        mm.then_inc(summed, 1)

                    gate_sum(0)
                    for k in range(KT):
                        if k + 1 < KT:
                            gate_sum(k + 1)
                        pe.wait_ge(tanhed, k + 1)
                        for f in range(4):
                            if k >= 1:
                                pe.wait_ge(gated, 4 * (k - 1) + f + 1)
                            pe.matmul(bps[:, f, 0:TW], gbc[:, f, :], gt[:, k % 2], start=True, stop=True).then_inc(spread, 1)

                @block.scalar
                def _(act):
                    act.wait_ge(zeroed, 5)
                    act.wait_ge(loaded, 16 * (4 + NP))
                    for k in range(KT):
                        act.wait_ge(summed, k + 1)
                        if k >= 2:
                            act.wait_ge(spread, 4 * (k - 1))
                        act.activation(gt[0:2 * T, k % 2], gps[:, k % 2, 0:TW], ACT.Tanh, bias=gb[:]).then_inc(tanhed, 1)

        gates.close()
        LG = sbuf(moe0, "logits", [GW, NT * SUB * 2, E])
        with ExitStack() as ctx:
            UNIT = 8
            zs = sbuf(ctx, "shifted", [P, 2, 4, TW])
            zo = sbuf(ctx, "own", [P, 2, 4, TW])
            wg = sbuf(ctx, "w_gate", [P, 2 * E])
            bg = sbuf(ctx, "b_gate", [GW, SUB * 2, E])
            xn = sbuf(ctx, "xn2", [P, 4, TW])
            hi = sbuf(ctx, "hi2", [P, 4, TW], F32R)
            lo = sbuf(ctx, "lo2", [P, 4, TW], F32R)
            lps = psum(ctx, "logit_psum", [P, 2, 512])
            ln = Norm(ctx, "ln2", 4, 2)
            consts, zeroed, moved, added, hi_done, lo_done, lg_ready, lg_done = (
                sem(ctx, "p3_" + s) for s in ("consts", "zeroed", "moved", "added", "hi", "lo", "lg_ready", "lg_done"))
            z_in = [sem(ctx, f"p3_z{b}") for b in range(2)]
            hi_stored = [sem(ctx, f"p3_hi_stored{b}") for b in range(4)]
            lo_stored = [sem(ctx, f"p3_lo_stored{b}") for b in range(4)]
            with nc.Block() as block:
                @block.sync
                def _(sp):
                    def load(n, b):
                        def gated(tile_of, a, c0, c1):
                            return Z[bass.ds(tile_of, 4), 2 * HALF * a + c0:2 * HALF * a + c1].rearrange("k c w -> c k w")

                        left, right = (0, HALF), (HALF, 2 * HALF)
                        for a in range(2):
                            sp.dma_start(zo[C * a:C * a + 2 * HALF, b], gated(n + KT, a, 0, 2 * HALF)).then_inc(z_in[b], 16)
                        sp.dma_start(zs[0:HALF, b], gated(n + KT, 1, *left)).then_inc(z_in[b], 16)
                        sp.dma_start(zs[HALF:2 * HALF, b], gated(n, 1, *right)).then_inc(z_in[b], 16)
                        sp.dma_start(zs[C:C + HALF, b], gated(n + 2 * KT, 0, *left)).then_inc(z_in[b], 16)
                        sp.dma_start(zs[C + HALF:C + 2 * HALF, b], gated(n + KT, 0, *right)).then_inc(z_in[b], 16)

                    def step(n, m):
                        if m % 4 == 0 and exists(n):
                            wait(sp, added, n - 4)
                            load(n, m // 4)
                        if exists(n - 7):
                            sp.wait_ge(hi_done, n - 6)
                            sp.dma_start(split_rows(SD2, n - 7, 0), hi[:, (m - 7) % 4].bitcast(F32))\
                                .then_inc(hi_stored[(m - 7) % 4], 16)
                            sp.wait_ge(lo_done, n - 6)
                            sp.dma_start(split_rows(SD2, n - 7, 1), lo[:, (m - 7) % 4].bitcast(F32))\
                                .then_inc(lo_stored[(m - 7) % 4], 16)

                    sp.dma_start(wg[:], A["w_gate"]).then_inc(consts, 16)
                    sp.dma_start(bg[:].rearrange("p s e -> p (s e)"), A["b_gate"].partition_broadcast(GW))\
                        .then_inc(consts, 16)
                    every_tile(sp, step, UNIT, 7)
                    for b in range(4):
                        sp.wait_ge(hi_stored[b], 16 * NT // 4)
                        sp.wait_ge(lo_stored[b], 16 * NT // 4)

                @block.gpsimd
                def _(pool):
                    for b in range(2):
                        for a in range(2):
                            pool.memset(zs[C * a + 2 * HALF:C * (a + 1), b], 0.0).then_inc(zeroed, 1)
                    pool.wait_ge(zeroed, 8)

                    def step(n, m):
                        if exists(n):
                            if m % 4 == 0:
                                pool.wait_ge(z_in[m // 4], 12 * (n - m) + 96)
                            d = zs[:, m // 4, m % 4]
                            pool.tensor_tensor(d, d, zo[:, m // 4, m % 4], ALU.subtract).then_inc(moved, 1)
                        if exists(n - 5):
                            b = (m - 5) % 4
                            pool.wait_ge(hi_done, n - 4)
                            wait(pool, lo_stored[b], 4 * (n - 5 - b))
                            pool.tensor_tensor(lo[:, b], xn[:, b], hi[:, b].bitcast(F32), ALU.subtract).then_inc(lo_done, 1)

                    every_tile(pool, step, UNIT, 5)

                @block.tensor
                def _(pe):
                    pe.wait_ge(consts, 32)

                    def logits(n, m):
                        pe.wait_ge(ln.normed, n + 1)
                        wait(pe, lg_done, n - 1)
                        for s in range(SUB):
                            mm = pe.matmul(lps[0:GW, m % 2, s * 2 * E:(s + 1) * 2 * E], xn[:, m % 4, GW * s:GW * (s + 1)],
                                           wg[:], start=True, stop=True)
                        mm.then_inc(lg_ready, 1)

                    def step(n, m):
                        if exists(n - 2):
                            ln.pe_var(pe, n - 2, m - 2)
                        if exists(n):
                            pe.wait_ge(added, n + 1)
                            ln.pe_centre(pe, n, m, tile(X, n))
                        if exists(n - 4):
                            logits(n - 4, m - 4)

                    every_tile(pe, step, UNIT, 4)

                @block.scalar
                def _(act):
                    def step(n, m):
                        if exists(n - 1):
                            ln.act_square(act, n - 1, m - 1)
                        if exists(n - 2):
                            ln.act_seed(act, n - 2, m - 2, 1)
                        if exists(n - 4):
                            b = m % 4
                            act.wait_ge(ln.normed, n - 3)
                            wait(act, hi_stored[b], 4 * (n - 4 - b))
                            act.activation(hi[:, b], xn[:, b], ACT.Copy).then_inc(hi_done, 1)

                    every_tile(act, step, UNIT, 4)

                @block.vector
                def _(dve):
                    for b in range(2):
                        for a in range(2):
                            dve.memset(zo[C * a + 2 * HALF:C * (a + 1), b], 0.0).then_inc(zeroed, 1)
                    dve.wait_ge(consts, 32)

                    def keep_logits(n, m):
                        dve.wait_ge(lg_ready, n + 1)
                        dve.tensor_tensor(LG[:, bass.ds(n * SUB * 2, SUB * 2), :],
                                          lps[0:GW, m % 2, 0:SUB * 2 * E].rearrange("p (s e) -> p s e", e=E),
                                          bg[:], ALU.add).then_inc(lg_done, 1)

                    def norm(n, m):
                        ln.dve_newton(dve, n, m, EPS_T)
                        wait(dve, lg_ready, n - 3)
                        wait(dve, lo_done, n - 3)
                        ln.dve_scale(dve, n, m, xn[:, m % 4])

                    def step(n, m):
                        if exists(n):
                            x = tile(X, n)
                            dve.wait_ge(moved, n + 1)
                            dve.tensor_tensor(x, x, zs[:, m // 4, m % 4], ALU.add).then_inc(added, 1)
                        if exists(n - 3):
                            norm(n - 3, m - 3)
                        if exists(n - 5):
                            keep_logits(n - 5, m - 5)

                    every_tile(dve, step, UNIT, 5)

        with ExitStack() as ctx:
            w2 = sbuf(ctx, "w2", [P, E, CH0, C])
            b1 = sbuf(ctx, "b1", [P, E, CH0])
            b2 = sbuf(ctx, "b2", [P, E])
            S = sbuf(ctx, "tokens", [P, 2, 2, TW], F32R)
            WB = sbuf(ctx, "w_bc", [P, 2, E, TW])
            hs = sbuf(ctx, "hidden", [P, 2 * CH0, 2, TW])
            pr = sbuf(ctx, "weighted", [P, 2, TW])
            hp = psum(ctx, "hidden_psum", [P, 2, 2, 512])
            yp = psum(ctx, "y_psum", [P, 2, 512])
            G = 2 * SUB * 2
            countdown = sbuf(ctx, "countdown", [GW, G, E])
            key = sbuf(ctx, "key", [GW, G, E])
            chosen = sbuf(ctx, "chosen", [GW, 2, G, E])
            rest = sbuf(ctx, "rest", [GW, G, E])
            best = sbuf(ctx, "best", [GW, 2, G])
            first = sbuf(ctx, "first", [GW, G])
            gap = sbuf(ctx, "gap", [GW, G])
            th = sbuf(ctx, "th", [GW, G])
            w12 = sbuf(ctx, "w12", [GW, 2, G])
            ident = sbuf(ctx, "ident", [P, P])
            wst = sbuf(ctx, "w_stage", [GW, 2, SUB, 32])
            wtt = sbuf(ctx, "w_strips", [P, 2, GW])
            wps = psum(ctx, "w_psum", [P, 2, 512])
            consts, up_done, gelu_done, down_done, weighted, summed = (
                sem(ctx, "p4_" + s) for s in ("consts", "up", "gelu", "down", "weighted", "summed"))
            prepared, top2_done, tanh_done, transposed, copied = (
                sem(ctx, "p4_" + s) for s in ("prepared", "top2", "tanh", "transposed", "copied"))
            tok_in = [sem(ctx, f"p4_tok{b}") for b in range(2)]
            wb_in = [sem(ctx, f"p4_wb{b}") for b in range(2)]
            wt_stored = [sem(ctx, f"p4_wt_stored{b}") for b in range(2)]
            SN = E * CH0
            NU = NT // 2
            TOP2_STEPS = 17
            GAP_STEP = 11
            SLOT = (0, 0, 1, 2, 3, 4, 5, 6, 7, 8, 9, 10, 13, 13, 14, 14, 15)

            def every_unit(engine, body):
                for u in units(engine, NU - 2):
                    body(u, True, True, False)
                body(NU - 2, False, True, False)
                body(NU - 1, False, False, True)

            with nc.Block() as block:
                @block.sync
                def _(sp):
                    def load_tokens(n, b):
                        sp.dma_start(S[:, b].bitcast(F32), SD2[bass.ds(n, 1)].rearrange("o a p w -> (o p) a w"))\
                            .then_inc(tok_in[b], 16)

                    def load_weights(n, b):
                        for a in range(2):
                            sp.dma_start(WB[C * a:C * a + C, b], WT[bass.ds(n, 1), E * a:E * a + E]
                                         .rearrange("o e w -> (o e) w").partition_broadcast(C)).then_inc(wb_in[b], 16)

                    def store_weights(u):
                        for b in range(2):
                            sp.wait_ge(copied, 2 * u + b + 1)
                            for s in range(SUB):
                                sp.dma_start(WT[bass.ds(2 * u + b, 1), :, GW * s:GW * (s + 1)]
                                             .rearrange("o r w -> (o r) w"), wtt[32 * s:32 * s + 2 * E, b])\
                                    .then_inc(wt_stored[b], 16)

                    def body(u, top2, move, last):
                        if not move:
                            return
                        store_weights(u + 1)
                        for b in range(2):
                            n = 2 * u + b
                            sp.wait_ge(wt_stored[b], 16 * SUB * (u + 2))
                            sp.wait_ge(up_done, SN * n + SN)
                            sp.wait_ge(weighted, E * n + E)
                            load_tokens(n + 2, b)
                            load_weights(n + 2, b)

                    for b in range(2):
                        load_tokens(b, b)
                    sp.dma_start(w2[:], A["w2"]).then_inc(consts, 16)
                    sp.dma_start(b1[:], A["b1"]).then_inc(consts, 16)
                    sp.dma_start(b2[:], A["b2"]).then_inc(consts, 16)
                    sp.dma_start(ident[:], A["ident"]).then_inc(consts, 16)
                    store_weights(0)
                    for b in range(2):
                        sp.wait_ge(wt_stored[b], 16 * SUB)
                        load_weights(b, b)
                    every_unit(sp, body)

                @block.tensor
                def _(pe):
                    pe.wait_ge(consts, 64)

                    def transpose(u):
                        pe.wait_ge(top2_done, TOP2_STEPS * (u + 1))
                        wait(pe, copied, 2 * u)
                        for b in range(2):
                            pe.transpose(wps[:, b, 0:GW], wst[:, b].rearrange("p s r -> p (s r)"), ident[0:GW, 0:GW])\
                                .then_inc(transposed, 1)

                    def up(u, b, s):
                        if s == 0:
                            pe.wait_ge(tok_in[b], 16 * u + 16)
                        wait(pe, gelu_done, SN * (2 * u + b) + s - 1)
                        for a in range(2):
                            o = hp[:, s % 2, a, 0:TW]
                            pe.matmul(o, w1hi[:, s * P:(s + 1) * P], S[:, b, a, :], start=True, stop=False)
                            mm = pe.matmul(o, w1lo[:, s * P:(s + 1) * P], S[:, b, a, :], start=False, stop=True)
                        mm.then_inc(up_done, 1)

                    def ups(u, b, e):
                        for c in range(CH0):
                            up(u, b, CH0 * e + c)

                    def downs(u, b, e):
                        for c in range(CH0):
                            s = CH0 * e + c
                            pe.wait_ge(gelu_done, SN * (2 * u + b) + s + 1)
                            if c == 0:
                                wait(pe, weighted, E * (2 * u + b) + e - 1)
                            for a in range(2):
                                mm = pe.matmul(yp[C * a:C * a + C, e % 2, 0:TW], w2[:, e, c, :], hs[:, s % (2 * CH0), a, :],
                                               start=(c == 0), stop=(c == CH0 - 1))
                            mm.then_inc(down_done, 1)

                    def body(u, top2, move, last):
                        for k in range(2 * E):
                            if k == 1 and move:
                                transpose(u + 1)
                            if k + 1 < 2 * E:
                                ups(u, (k + 1) // E, (k + 1) % E)
                            elif not last:
                                ups(u + 1, 0, 0)
                            downs(u, k // E, k % E)

                    ups(0, 0, 0)
                    transpose(0)
                    every_unit(pe, body)

                @block.scalar
                def _(act):
                    def tanh(u):
                        act.wait_ge(top2_done, TOP2_STEPS * u + GAP_STEP + 1)
                        act.activation(th[:], gap[:], ACT.Tanh, scale=0.5).then_inc(tanh_done, 1)

                    def copy_weights(u):
                        for b in range(2):
                            act.wait_ge(transposed, 2 * u + b + 1)
                            wait(act, wt_stored[b], 16 * SUB * u)
                            act.activation(wtt[:, b], wps[:, b, 0:GW], ACT.Copy).then_inc(copied, 1)

                    def body(u, top2, move, last):
                        for k in range(4 * E):
                            e, c = divmod(k % SN, CH0)
                            act.wait_ge(up_done, 2 * SN * u + k + 1)
                            wait(act, down_done, 2 * SN * u + k + 1 - 2 * CH0)
                            act.activation(hs[:, k % (2 * CH0)], hp[:, k % 2, :, 0:TW], ACT.Gelu, bias=b1[:, e, c:c + 1])\
                                .then_inc(gelu_done, 1)
                            if k == 2 * CH0 + 1 and move:
                                copy_weights(u + 1)
                            if k == CH0 * (SLOT[GAP_STEP] + 3) - 1 and top2:
                                tanh(u + 2)

                    tanh(0)
                    act.wait_ge(consts, 64)
                    copy_weights(0)
                    tanh(1)
                    every_unit(act, body)

                @block.vector
                def _(dve):
                    def top2_step(u, s):
                        L = LG[:, bass.ds(u * G, G), :]
                        over = [GW, G, E]
                        wait(dve, top2_done, TOP2_STEPS * u + s)
                        second, t = s >= 6, s % 6
                        if s < GAP_STEP and t == 0:
                            ins = dve.tensor_reduce(best[:, int(second)], rest[:] if second else L, AX.X, ALU.max)
                        elif s < GAP_STEP and t == 1:
                            ins = dve.tensor_tensor(key[:], rest[:] if second else L,
                                                    best[:, int(second)].unsqueeze(2).broadcast_to(over), ALU.is_equal)
                        elif s < GAP_STEP and t == 2:
                            ins = dve.tensor_tensor(key[:], key[:], countdown[:], ALU.mult)
                        elif s < GAP_STEP and t == 3:
                            ins = dve.tensor_reduce(first[:], key[:], AX.X, ALU.max)
                        elif s < GAP_STEP and t == 4:
                            ins = dve.tensor_tensor(chosen[:, int(second)], key[:],
                                                    first[:].unsqueeze(2).broadcast_to(over), ALU.is_equal)
                        elif s == 5:
                            ins = dve.scalar_tensor_tensor(out=rest[:], in0=chosen[:, 0], scalar=-3.0e38, in1=L,
                                                           op0=ALU.mult, op1=ALU.add)
                        elif s == GAP_STEP:
                            ins = dve.tensor_tensor(gap[:], best[:, 0], best[:, 1], ALU.subtract)
                        elif s in (12, 13):
                            if s == 12:
                                dve.wait_ge(tanh_done, u + 1)
                            ins = dve.tensor_scalar(w12[:, s - 12], th[:], 0.5 if s == 12 else -0.5, 0.5, ALU.mult, ALU.add)
                        elif s in (14, 15):
                            ins = dve.tensor_tensor(chosen[:, s - 14], chosen[:, s - 14],
                                                    w12[:, s - 14].unsqueeze(2).broadcast_to(over), ALU.mult)
                        else:
                            wait(dve, transposed, 2 * u)
                            ins = dve.tensor_tensor(stage_of_experts(), by_tile(chosen[:, 0]), by_tile(chosen[:, 1]), ALU.add)
                        ins.then_inc(top2_done, 1)

                    def by_tile(x):
                        return x.rearrange("p (s a) e -> p s (a e)", a=2)

                    def stage_of_experts():
                        return wst[:].rearrange("p b s r -> p (b s) r")[:, :, 0:2 * E]

                    def body(u, top2, move, last):
                        for k in range(2 * E):
                            b, e = divmod(k, E)
                            n = 2 * u + b
                            x = tile(X, n)
                            if e == 0:
                                dve.wait_ge(wb_in[b], 32 * u + 32)
                            dve.wait_ge(down_done, SN * n + CH0 * (e + 1))
                            dve.scalar_tensor_tensor(out=pr[:, e % 2], in0=yp[:, e % 2, 0:TW], scalar=b2[:, e:e + 1],
                                                     in1=WB[:, b, e, :], op0=ALU.add, op1=ALU.mult).then_inc(weighted, 1)
                            if top2:
                                for s in range(TOP2_STEPS):
                                    if SLOT[s] == k:
                                        top2_step(u + 2, s)
                            dve.wait_ge(weighted, E * n + e + 1)
                            wait(dve, summed, E * n + e)
                            dve.tensor_tensor(x, x, pr[:, e % 2], ALU.add).then_inc(summed, 1)

                    for e in range(E):
                        dve.memset(countdown[:, :, e], float(E - e)).then_inc(prepared, 1)
                    dve.memset(wst[:], 0.0).then_inc(prepared, 1)
                    dve.wait_ge(prepared, E + 1)
                    for s in range(TOP2_STEPS):
                        top2_step(0, s)
                    dve.wait_ge(consts, 64)
                    for s in range(TOP2_STEPS):
                        top2_step(1, s)
                    every_unit(dve, body)
        moe0.close()

        with ExitStack() as ctx:
            cwraw = sbuf(ctx, "conv_raw", [P, 9, P])
            cw = sbuf(ctx, "conv_sign", [P, 9, P], F32R)
            sf = sbuf(ctx, "factor", [P, 1])
            AVGR = sbuf(ctx, "average_r", [P, P], F32R)
            pad_hi = sbuf(ctx, "pad_hi", [P, 2, HH + 2, PADW], F32R)
            pad_lo = sbuf(ctx, "pad_lo", [P, 2, HH + 2, PADW], F32R)
            xn3 = sbuf(ctx, "xn3", [P, 2, TW])
            xn4 = sbuf(ctx, "xn4", [P, 2, TW])
            hi = sbuf(ctx, "hi4", [P, 2, TW], F32R)
            lo = sbuf(ctx, "lo4", [P, 2, TW], F32R)
            cps = psum(ctx, "conv_psum", [P, 2, 512])
            ln3 = Norm(ctx, "ln3", 2, 1, depth=1, split=AVGR)
            ln4 = Norm(ctx, "ln4", 2, 1, depth=1, split=AVGR)
            consts, signed, zeroed, pad_hi_done, pad_lo_done, conv_done, x3_done, hi_done, lo_done = (
                sem(ctx, "p5_" + s) for s in ("consts", "signed", "zeroed", "pad_hi", "pad_lo", "conv", "x3", "hi", "lo"))
            average_ready = sem(ctx, "p5_average")
            stored = [sem(ctx, f"p5_stored{b}") for b in range(2)]
            V = 2 * KT
            LEAD = 3

            def borders(pad):
                p = pad[:].bitcast(F32)
                return p[:, :, 0, :], p[:, :, HH + 1, :], p[:, :, 1:HH + 1, 0], p[:, :, 1:HH + 1, WW + 1]

            def every_step(engine, step):
                for i in units(engine, NP // 2 - 1):
                    for m in range(V):
                        step(V * i + m, m)
                for m in range(V):
                    step(NT - V + m, m)

            with nc.Block() as block:
                @block.sync
                def _(sp):
                    sp.dma_start(cwraw[:], A["conv_w"]).then_inc(consts, 16)
                    for a in range(2):
                        sp.dma_start(sf[C * a:C * a + C, :], A["factor"]).then_inc(consts, 16)

                    def store(n, m):
                        sp.wait_ge(ln4.normed, n + 1)
                        sp.dma_start(XN4[bass.ds(n, 1)].rearrange("o p w -> (o p) w"), xn4[:, m % 2])\
                            .then_inc(stored[m % 2], 16)
                        sp.wait_ge(hi_done, n + 1)
                        sp.dma_start(split_rows(SD4, n, 0), hi[:, m % 2].bitcast(F32)).then_inc(stored[m % 2], 16)
                        sp.wait_ge(lo_done, n + 1)
                        sp.dma_start(split_rows(SD4, n, 1), lo[:, m % 2].bitcast(F32)).then_inc(stored[m % 2], 16)

                    every_step(sp, store)
                    for b in range(2):
                        sp.wait_ge(stored[b], 48 * NT // 2)

                @block.tensor
                def _(pe):
                    pe.wait_ge(average_ready, 1)

                    def conv(n, m):
                        pair, k = divmod(m, KT)
                        pe.wait_ge(pad_lo_done, n + 1 + min(1, KT - 1 - k))
                        wait(pe, x3_done, n - 1)
                        o = rows(cps[:, m % 2, 0:TW])
                        for t9 in range(9):
                            dy, dx = divmod(t9, 3)
                            for part, src in enumerate((pad_hi, pad_lo)):
                                mm = pe.matmul(o, cw[:, t9, :], src[:, pair, ROWS * k + dy:ROWS * k + dy + ROWS, dx:dx + WW],
                                               start=(t9 == 0 and part == 0), stop=(t9 == 8 and part == 1))
                        mm.then_inc(conv_done, 1)

                    def centre4(n, m):
                        pe.wait_ge(x3_done, n + 1)
                        ln4.pe_centre(pe, n, m, tile(X, n))

                    def step(n, m):
                        if exists(n + LEAD):
                            ln3.pe_centre(pe, n + LEAD, m + LEAD, tile(X, n + LEAD))
                        conv(n, m)
                        if exists(n - 2):
                            ln4.pe_var(pe, n - 2, m)
                        if exists(n - 1):
                            centre4(n - 1, m + 1)
                        if exists(n + LEAD):
                            ln3.pe_var(pe, n + LEAD, m + LEAD)

                    for k in range(LEAD):
                        ln3.pe_centre(pe, k, k, tile(X, k))
                        if k >= 1:
                            ln3.pe_var(pe, k - 1, k - 1)
                    ln3.pe_var(pe, LEAD - 1, LEAD - 1)
                    pe.wait_ge(signed, 1)
                    pe.wait_ge(zeroed, 8)
                    every_step(pe, step)
                    ln4.pe_var(pe, NT - 2, 0)
                    centre4(NT - 1, 1)
                    ln4.pe_var(pe, NT - 1, 1)

                @block.scalar
                def _(act):
                    act.activation(AVGR[:], AVG[:], ACT.Copy).then_inc(average_ready, 1)

                    def step(n, m):
                        if exists(n + LEAD):
                            ln3.act_square(act, n + LEAD, m + LEAD)
                        if exists(n - 2):
                            ln4.act_seed(act, n - 2, m, 1)
                        if exists(n - 1):
                            ln4.act_square(act, n - 1, m + 1)
                        if exists(n + LEAD):
                            ln3.act_seed(act, n + LEAD, m + LEAD, 0)

                    for k in range(LEAD):
                        ln3.act_square(act, k, k)
                        if k >= 1:
                            ln3.act_seed(act, k - 1, k - 1, 0)
                    ln3.act_seed(act, LEAD - 1, LEAD - 1, 0)
                    act.wait_ge(consts, 48)
                    act.activation(cw[:], cwraw[:], ACT.Sign).then_inc(signed, 1)
                    every_step(act, step)
                    ln4.act_seed(act, NT - 2, 0, 1)
                    ln4.act_square(act, NT - 1, 1)
                    ln4.act_seed(act, NT - 1, 1, 1)

                @block.vector
                def _(dve):
                    for border in borders(pad_hi):
                        dve.memset(border, 0.0).then_inc(zeroed, 1)

                    def norm3(n, m):
                        pair, k = divmod(m, KT)
                        wait(dve, pad_lo_done, n - 1)
                        ln3.dve_norm(dve, n, m, EPS_C, xn3[:, m % 2])
                        dve.wait_ge(ln3.normed, n + 1)
                        if k == 0:
                            wait(dve, conv_done, n - KT)
                        dve.tensor_copy(pad_hi[:, pair, ROWS * k + 1:ROWS * k + 1 + ROWS, 1:WW + 1], rows(xn3[:, m % 2]))\
                            .then_inc(pad_hi_done, 1)

                    def norm4(n, m):
                        wait(dve, stored[m % 2], past_stores(n, m))
                        ln4.dve_norm(dve, n, m, EPS_T, xn4[:, m % 2], accum=MSUM[:, bass.ds(n, 1)])
                        dve.wait_ge(ln4.normed, n + 1)
                        dve.tensor_copy(hi[:, m % 2], xn4[:, m % 2]).then_inc(hi_done, 1)

                    def past_stores(n, m):
                        return 24 * (n - m % 2)

                    def step(n, m):
                        if exists(n - 1) and exists(n + LEAD - 1):
                            norm3(n + LEAD - 1, (m + LEAD - 1) % V)
                        dve.wait_ge(conv_done, n + 1)
                        x = tile(X, n)
                        dve.scalar_tensor_tensor(out=x, in0=cps[:, m % 2, 0:TW], scalar=sf[:, 0:1], in1=x,
                                                 op0=ALU.mult, op1=ALU.add).then_inc(x3_done, 1)
                        if exists(n - 2):
                            norm4(n - 2, m)

                    for k in range(LEAD):
                        norm3(k, k)
                    dve.wait_ge(consts, 48)
                    every_step(dve, step)
                    norm4(NT - 2, 0)
                    norm4(NT - 1, 1)

                @block.gpsimd
                def _(pool):
                    for border in borders(pad_lo):
                        pool.memset(border, 0.0).then_inc(zeroed, 1)

                    def lo3(n, m):
                        pair, k = divmod(m, KT)
                        inside = (slice(None), pair, slice(ROWS * k + 1, ROWS * k + 1 + ROWS), slice(1, WW + 1))
                        pool.wait_ge(pad_hi_done, n + 1)
                        if k == 0:
                            wait(pool, conv_done, n - KT)
                        pool.tensor_tensor(pad_lo[inside], rows(xn3[:, m % 2]), pad_hi[inside].bitcast(F32), ALU.subtract)\
                            .then_inc(pad_lo_done, 1)

                    def lo4(n, m):
                        pool.wait_ge(hi_done, n + 1)
                        pool.tensor_tensor(lo[:, m % 2], xn4[:, m % 2], hi[:, m % 2].bitcast(F32), ALU.subtract)\
                            .then_inc(lo_done, 1)

                    def step(n, m):
                        if exists(n + LEAD):
                            ln3.pool_square_lo(pool, n + LEAD, m + LEAD)
                        if exists(n - 1) and exists(n + LEAD - 1):
                            lo3(n + LEAD - 1, (m + LEAD - 1) % V)
                        if exists(n - 1):
                            ln4.pool_square_lo(pool, n - 1, m + 1)
                        if exists(n - 2):
                            lo4(n - 2, m)

                    for k in range(LEAD):
                        ln3.pool_square_lo(pool, k, k)
                        lo3(k, k)
                    every_step(pool, step)
                    ln4.pool_square_lo(pool, NT - 1, 1)
                    lo4(NT - 2, 0)
                    lo4(NT - 1, 1)

        with ExitStack() as ctx:
            wr = sbuf(ctx, "w_route", [P, E])
            br = sbuf(ctx, "b_route", [NP, 2, E])
            ones = sbuf(ctx, "ones8", [NP, NP])
            ms = sbuf(ctx, "mean", [P, NP])
            ms2 = sbuf(ctx, "mean_scaled", [P, NP])
            names = ("lg", "shift", "ex", "rw", "rs", "ex2", "rank", "beats", "tmp", "iota")
            t3 = {n: sbuf(ctx, "r_" + n, [NP, 2, E]) for n in names}
            mx, sm, ri = (sbuf(ctx, "r_" + n, [NP, 2]) for n in ("mx", "sm", "ri"))
            loads, scale = sbuf(ctx, "r_loads", [NP, E]), sbuf(ctx, "r_scale", [NP, E])
            pick = sbuf(ctx, "r_pick", [NP, 2, 2])
            pidx = sbuf(ctx, "r_pidx", [NP, 2, 2])
            pidi = sbuf(ctx, "r_pidi", [NP, 2, 2], I32)
            dd, ee, wse = (sbuf(ctx, "r_" + n, [NP, 2]) for n in ("dd", "ee", "wse"))
            wsel = sbuf(ctx, "r_wsel", [NP, 2, 2])
            lp = [psum(ctx, f"r_lg{a}", [NP, 512]) for a in range(2)]
            ldp = psum(ctx, "r_ldp", [NP, 512])
            w1raw = sbuf(ctx, "w1raw_l1", [P, E, F1])
            w1s = sbuf(ctx, "w1split_l1", [P, E, 2, F1], F32R)
            w1_in, w1_hi, w1_lo = (sem(ctx, "p6_" + s) for s in ("w1_in", "w1_hi", "w1_lo"))
            consts, s_v, s_mm, s_a, s_out = (sem(ctx, "p6_" + s) for s in ("consts", "v", "mm", "a", "out"))
            steps, marks = [0], {}
            with nc.Block() as block:
                @block.vector
                def _(dve):
                    def link(ins, mark=None):
                        steps[0] += 1
                        ins.then_inc(s_v, 1)
                        dve.wait_ge(s_v, steps[0])
                        marks[mark] = steps[0]

                    def bc(x):
                        return x.unsqueeze(2).broadcast_to([NP, 2, E])

                    def shifted_exp(src, dst, mark, count):
                        link(dve.tensor_reduce(mx[:], src[:], AX.X, ALU.max))
                        link(dve.tensor_tensor(t3["shift"][:], src[:], bc(mx[:]), ALU.subtract), mark)
                        dve.wait_ge(s_a, count)
                        link(dve.tensor_reduce(sm[:], t3["ex"][:], AX.X, ALU.add))
                        link(dve.reciprocal(ri[:], sm[:]))
                        link(dve.tensor_tensor(dst[:], t3["ex"][:], bc(ri[:]), ALU.mult))

                    dve.wait_ge(consts, 48)
                    link(dve.memset(ones[:], 1.0))
                    for e in range(E):
                        mset = dve.memset(t3["iota"][:, :, e], float(e))
                    link(mset)
                    link(dve.tensor_copy(t3["rank"][:], t3["iota"][:]))
                    link(dve.tensor_reduce(ms[:], MSUM[:].rearrange("p (j k) -> p j k", k=KT), AX.X, ALU.add))
                    link(dve.tensor_scalar(ms2[:], ms[:], 1.0 / PIX, None, ALU.mult), "mean")
                    dve.wait_ge(s_mm, 1)
                    for a in range(2):
                        link(dve.tensor_tensor(t3["lg"][:, a], lp[a][:, 0:E], br[:, a], ALU.add))
                    shifted_exp(t3["lg"], t3["rw"], "exp1", 1)
                    marks["rw"] = steps[0]
                    dve.wait_ge(s_mm, 2)
                    link(dve.tensor_scalar(loads[:], ldp[:, 0:E], float(PIX), None, ALU.mult))
                    link(dve.reciprocal(scale[:], loads[:]))
                    link(dve.tensor_scalar(scale[:], scale[:], CAPACITY, 1.0, ALU.mult, ALU.min))
                    for a in range(2):
                        link(dve.tensor_tensor(t3["lg"][:, a], t3["rw"][:, a], scale[:], ALU.mult))
                    shifted_exp(t3["lg"], t3["rs"], "exp2", 2)
                    for s in range(1, E):
                        l_, h_ = slice(0, E - s), slice(s, E)
                        rs, rk, bt = t3["rs"], t3["rank"], t3["beats"]
                        link(dve.tensor_tensor(bt[:, :, l_], rs[:, :, h_], rs[:, :, l_], ALU.is_gt))
                        link(dve.tensor_tensor(rk[:, :, l_], rk[:, :, l_], bt[:, :, l_], ALU.add))
                        link(dve.tensor_tensor(rk[:, :, h_], rk[:, :, h_], bt[:, :, l_], ALU.subtract))
                    for k in range(2):
                        for src, dst in ((t3["rs"], pick), (t3["iota"], pidx)):
                            link(dve.scalar_tensor_tensor(out=t3["tmp"][:], in0=t3["rank"][:], scalar=float(k),
                                                          in1=src[:], op0=ALU.is_equal, op1=ALU.mult))
                            link(dve.tensor_reduce(dst[:, :, k], t3["tmp"][:], AX.X, ALU.add))
                    link(dve.tensor_copy(pidi[:], pidx[:]))
                    link(dve.tensor_tensor(dd[:], pick[:, :, 1], pick[:, :, 0], ALU.subtract), "exp3")
                    dve.wait_ge(s_a, 3)
                    link(dve.tensor_scalar(wse[:], ee[:], 1.0, None, ALU.add))
                    link(dve.reciprocal(wsel[:, :, 0], wse[:]))
                    link(dve.tensor_tensor(wsel[:, :, 1], wsel[:, :, 0], ee[:], ALU.mult), "out")

                @block.scalar
                def _(act):
                    for n, mark in enumerate(("exp1", "exp2")):
                        act.wait_ge(s_v, marks[mark])
                        act.activation(t3["ex"][:], t3["shift"][:], ACT.Exp).then_inc(s_a, 1)
                    act.wait_ge(s_v, marks["exp3"])
                    act.activation(ee[:], dd[:], ACT.Exp).then_inc(s_a, 1)

                @block.tensor
                def _(pe):
                    pe.wait_ge(consts, 48)
                    pe.wait_ge(s_v, marks["mean"])
                    for a in range(2):
                        mm = pe.matmul(lp[a][:, 0:E], ms2[C * a:C * a + C, :], wr[C * a:C * a + C, :],
                                       start=True, stop=True)
                    mm.then_inc(s_mm, 1)
                    pe.wait_ge(s_v, marks["rw"])
                    for a in range(2):
                        mm = pe.matmul(ldp[:, 0:E], ones[:], t3["rw"][:, a], start=(a == 0), stop=(a == 1))
                    mm.then_inc(s_mm, 1)

                @block.gpsimd
                def _(pool):
                    pool.wait_ge(w1_in, 16)
                    pool.tensor_copy(w1s[:, :, 0, :], w1raw[:]).then_inc(w1_hi, 1)
                    pool.wait_ge(w1_hi, 1)
                    pool.tensor_tensor(w1s[:, :, 1, :], w1raw[:], w1s[:, :, 0, :].bitcast(F32), ALU.subtract)\
                        .then_inc(w1_lo, 1)

                @block.sync
                def _(sp):
                    sp.dma_start(w1raw[:], A["w1_l1"]).then_inc(w1_in, 16)
                    sp.dma_start(wr[0:C, :], A["w_route"]).then_inc(consts, 16)
                    sp.dma_start(wr[C:P, :], A["w_route"]).then_inc(consts, 16)
                    sp.dma_start(br[:].rearrange("p a e -> p (a e)"), A["b_route"].partition_broadcast(NP))\
                        .then_inc(consts, 16)
                    sp.wait_ge(w1_lo, 1)
                    sp.dma_start(W1D.rearrange("e p s f -> p e (s f)"), w1s[:].bitcast(F32).rearrange("p e s f -> p e (s f)"))\
                        .then_inc(s_out, 16)
                    sp.wait_ge(s_v, marks["out"])
                    sp.dma_start(IDX, pidi[:].rearrange("p a s -> p (a s)")).then_inc(s_out, 16)
                    sp.dma_start(WSEL, wsel[:].rearrange("p a s -> p (a s)")).then_inc(s_out, 16)
                    sp.wait_ge(s_out, 48)

        with ExitStack() as ctx:
            w1s = sbuf(ctx, "w1sel", [P, 2, 4, 2, F1], F32R)
            w2r = sbuf(ctx, "w2raw", [P, 2, 4, C])
            w2s = sbuf(ctx, "w2sel", [P, 2, 4, C])
            b1s = sbuf(ctx, "b1sel", [P, 2, 4])
            b2r = sbuf(ctx, "b2raw", [P, 2, 2])
            b2t = sbuf(ctx, "b2tmp", [P, 2, 1])
            b2s = sbuf(ctx, "b2sel", [P, 2, 1])
            wse = sbuf(ctx, "w_all", [P, NP, 4])
            wsh = sbuf(ctx, "w_half", [P, NP, 2])
            gam = sbuf(ctx, "gamma", [P, 1])
            hgam = sbuf(ctx, "minus_half_gamma", [P, 1])
            bet = sbuf(ctx, "beta", [P, 1])
            idr = sbuf(ctx, "idx", [1, NP * 4], I32)
            S = sbuf(ctx, "tokens4", [P, KT, 2, TW], F32R)
            u = sbuf(ctx, "tokens_plus_y", [P, KT, TW])
            hs = sbuf(ctx, "hidden1", [P, 2, 4, TW])
            nrm = sbuf(ctx, "ln5_out", [P, KT, TW])
            o2 = sbuf(ctx, "out_tile", [P, 2, TW])
            hp = psum(ctx, "hidden1_psum", [P, 2, 512])
            xc = psum(ctx, "ln5_xc_psum", [P, 4, 512])
            yp = xc[:, 3]
            ln = Norm(ctx, "ln5", 4, 2, group=KT, xc=xc)
            consts, idx_in, w2_done, b2_a, b2_done, up_done, gelu_done, down_done, u_done, scaled, out_done = (
                sem(ctx, "p7_" + s) for s in ("consts", "idx", "w2", "b2a", "b2", "up", "gelu", "down", "u",
                                              "scaled", "out"))
            w_in = [sem(ctx, f"p7_w{b}") for b in range(2)]
            split_in = [sem(ctx, f"p7_split{k}") for k in range(KT)]
            tok_in = [sem(ctx, f"p7_tok{k}") for k in range(KT)]
            stored = [sem(ctx, f"p7_stored{b}") for b in range(2)]
            WIN = 16 * (4 * 3 + 4)

            def every_pair(engine, body):
                for i in units(engine, NP // 2 - 1):
                    for b in range(2):
                        body(2 * i + b, b, False)
                for b in range(2):
                    body(NP - 2 + b, b, b == 1)

            with nc.Block() as block:
                @block.sync
                def _(sp):
                    sp.dma_start(idr[:], IDX.rearrange("(o j) s -> o (j s)", o=1)).then_inc(idx_in, 16)
                    sp.dma_start(wse[:], WSEL.rearrange("j s -> (j s)").partition_broadcast(P)
                                 .rearrange("p (j s) -> p j s", s=4)).then_inc(consts, 16)
                    for a in range(2):
                        sp.dma_start(wsh[C * a:C * a + C], WSEL[:, 2 * a:2 * a + 2].partition_broadcast(C))\
                            .then_inc(consts, 16)
                        sp.dma_start(gam[C * a:C * a + C, :], A["gamma"]).then_inc(consts, 16)
                        sp.dma_start(bet[C * a:C * a + C, :], A["beta"]).then_inc(consts, 16)

                    def load_weights(p, b):
                        for q in range(4):
                            e = sp.value_load(idr[0:1, bass.ds(p * 4 + q, 1)], min_val=0, max_val=E - 1)
                            sp.dma_start(w1s[:, b, q].bitcast(F32), W1D[bass.ds(e, 1)].rearrange("o p s f -> (o p) s f"))\
                                .then_inc(w_in[b], 16)
                            sp.dma_start(w2r[:, b, q], A["w2_l1"][bass.ds(e, 1)].rearrange("o f c -> (o f) c"))\
                                .then_inc(w_in[b], 16)
                            sp.dma_start(b1s[:, b, q:q + 1], A["b1_l1"][bass.ds(e, 1)].rearrange("o f u -> (o f) u"))\
                                .then_inc(w_in[b], 16)
                            a, s = divmod(q, 2)
                            sp.dma_start(b2r[C * a:C * a + C, b, s:s + 1],
                                         A["b2_l1"][bass.ds(e, 1)].rearrange("o c u -> (o c) u")).then_inc(w_in[b], 16)

                    def load_split(p, k):
                        sp.dma_start(S[:, k].bitcast(F32), SD4[bass.ds(KT * p + k, 1)].rearrange("o a p w -> (o p) a w"))\
                            .then_inc(split_in[k], 16)

                    def load_tokens(p, k):
                        sp.dma_start(u[:, k], XN4[bass.ds(KT * p + k, 1)].rearrange("o p w -> (o p) w"))\
                            .then_inc(tok_in[k], 16)

                    def store(p, b, k):
                        v = (KT * b + k) % 2
                        sp.wait_ge(out_done, KT * p + k + 1)
                        sp.dma_start(out[bass.ds(KT * p + k, 1)].rearrange("o p w -> (o p) w"), o2[:, v])\
                            .then_inc(stored[v], 16)

                    def pair(p, b, last):
                        if not last:
                            wait(sp, gelu_done, 4 * KT * p)
                            wait(sp, w2_done, p)
                            wait(sp, b2_done, p)
                            load_weights(p + 1, 1 - b)
                        for k in range(KT):
                            if not last:
                                sp.wait_ge(up_done, 4 * (KT * p + k) + 4)
                                load_split(p + 1, k)
                            if exists(p - 1):
                                store(p - 1, 1 - b, k)
                        if not last:
                            for k in range(KT):
                                sp.wait_ge(ln.centred, KT * p + k + 1)
                                load_tokens(p + 1, k)

                    load_split(0, 0)
                    sp.wait_ge(idx_in, 16)
                    load_weights(0, 0)
                    load_tokens(0, 0)
                    for k in range(1, KT):
                        load_split(0, k)
                        load_tokens(0, k)
                    every_pair(sp, pair)
                    for k in range(KT):
                        store(NP - 1, 1, k)
                    for b in range(2):
                        sp.wait_ge(stored[b], 16 * NT // 2)

                @block.tensor
                def _(pe):
                    def up(p, b, k, image):
                        for q in (2 * image, 2 * image + 1):
                            wait(pe, gelu_done, 4 * (KT * p + k) + q - 1)
                            pe.matmul(hp[:, q % 2, 0:TW], w1s[:, b, q, 0, :], S[:, k, q // 2, :], start=True, stop=False)
                            pe.matmul(hp[:, q % 2, 0:TW], w1s[:, b, q, 1, :], S[:, k, q // 2, :], start=False, stop=True)\
                                .then_inc(up_done, 1)

                    def down(p, b, k, slot):
                        n = KT * p + k
                        if slot == 0:
                            pe.wait_ge(gelu_done, 4 * n + 4)
                            wait(pe, u_done, n)
                            if k == 0:
                                pe.wait_ge(w2_done, p + 1)
                                wait(pe, ln.normed, KT * (p - 1) + 4)
                        for a in range(2):
                            mm = pe.matmul(yp[C * a:C * a + C, 0:TW], w2s[:, b, 2 * a + slot, :],
                                           hs[:, (KT * b + k) % 2, 2 * a + slot, :], start=(slot == 0), stop=(slot == 1))
                        if slot == 1:
                            mm.then_inc(down_done, 1)

                    def centre(p, k):
                        pe.wait_ge(u_done, KT * p + k + 1)
                        ln.pe_centre(pe, KT * p + k, k, u[:, k])

                    def pair(p, b, last):
                        pe.wait_ge(w_in[b], WIN // 2 * (p - b) + WIN)
                        for k in range(KT):
                            pe.wait_ge(split_in[k], 16 * p + 16)
                            for half in range(2):
                                up(p, b, k, half)
                                if k >= 1:
                                    down(p, b, k - 1, half)
                        centre(p, 0)
                        centre(p, 1)
                        down(p, b, KT - 1, 0)
                        down(p, b, KT - 1, 1)
                        centre(p, 2)
                        pe.wait_ge(u_done, KT * p + KT)
                        centre(p, 3)
                        for k in range(KT):
                            ln.pe_var(pe, KT * p + k, k)
                            if 4 <= k + 2 < KT:
                                centre(p, k + 2)

                    every_pair(pe, pair)

                @block.scalar
                def _(act):
                    def pair(p, b, last):
                        act.wait_ge(w_in[b], WIN // 2 * (p - b) + WIN)
                        for k in range(KT):
                            n = KT * p + k
                            wait(act, down_done, n - 1)
                            for q in range(4):
                                act.wait_ge(up_done, 4 * n + q + 1)
                                act.activation(hs[:, (KT * b + k) % 2, q], hp[:, q % 2, 0:TW], ACT.Gelu,
                                               bias=b1s[:, b, q:q + 1]).then_inc(gelu_done, 1)
                        for k in range(KT + 1):
                            if k < KT:
                                ln.act_square(act, KT * p + k, k)
                            if k >= 1:
                                ln.act_seed(act, KT * p + k - 1, k - 1, 1)

                    every_pair(act, pair)

                @block.vector
                def _(dve):
                    dve.wait_ge(consts, 7 * 16)

                    def weigh(p, b):
                        dve.wait_ge(w_in[b], WIN // 2 * (p - b) + WIN)
                        for q in range(4):
                            ts = dve.tensor_scalar(w2s[:, b, q], w2r[:, b, q], wse[:, bass.ds(p, 1), q], None, ALU.mult)
                        ts.then_inc(w2_done, 1)
                        dve.tensor_scalar(b2t[:, b], b2r[:, b, 0:1], wsh[:, bass.ds(p, 1), 0], None, ALU.mult)\
                            .then_inc(b2_a, 1)
                        dve.wait_ge(b2_a, p + 1)
                        dve.scalar_tensor_tensor(out=b2s[:, b], in0=b2r[:, b, 1:2], scalar=wsh[:, bass.ds(p, 1), 1],
                                                 in1=b2t[:, b], op0=ALU.mult, op1=ALU.add).then_inc(b2_done, 1)

                    def finish(p, b, k):
                        n, v = KT * p + k, KT * b + k
                        dve.wait_ge(ln.normed, n + 1)
                        wait(dve, stored[v % 2], 8 * (n - v % 2))
                        dve.scalar_tensor_tensor(out=o2[:, v % 2], in0=nrm[:, k], scalar=bet[:, 0:1],
                                                 in1=tile(X, n), op0=ALU.add, op1=ALU.add).then_inc(out_done, 1)

                    def pair(p, b, last):
                        dve.wait_ge(b2_done, p + 1)
                        for k in range(KT):
                            dve.wait_ge(tok_in[k], 16 * p + 16)
                            dve.wait_ge(down_done, KT * p + k + 1)
                            dve.scalar_tensor_tensor(out=u[:, k], in0=yp[:, 0:TW], scalar=b2s[:, b], in1=u[:, k],
                                                     op0=ALU.add, op1=ALU.add).then_inc(u_done, 1)
                            if exists(p - 1):
                                finish(p - 1, 1 - b, k)
                        if not last:
                            weigh(p + 1, 1 - b)
                        for k in range(KT):
                            ln.dve_newton(dve, KT * p + k, k, EPS_T)
                            ln.dve_scale(dve, KT * p + k, k, nrm[:, k], half_gamma=hgam[:, 0:1])
                            if last and k >= 1:
                                finish(p, b, k - 1)

                    dve.tensor_scalar(hgam[:], gam[:], -0.5, None, ALU.mult).then_inc(scaled, 1)
                    dve.wait_ge(scaled, 1)
                    weigh(0, 0)
                    every_pair(dve, pair)
                    finish(NP - 1, 1, KT - 1)


def kernel(**inputs):
    import concourse.bacc as bacc
    import numpy as np
    from concourse.bass_utils import run_bass_kernel_spmd

    v = {k: np.ascontiguousarray(a) for k, a in inputs.items()}
    f = np.float32

    def zeros(*shape):
        return np.zeros(shape, f)

    a = {"x": v["x"].reshape(NP, P, KT, TW).transpose(0, 2, 1, 3).reshape(NT, P, TW)}
    gate_w, gate_cols = zeros(2, C, 3, NQ, 2, 3), zeros(P, 3, GS)
    for lr, w in enumerate((v["L0_conv_w_l"], v["L0_conv_w_r"])):
        for im in range(2):
            for dt in range(3):
                gate_w[im, HALF * lr:HALF * lr + HALF, :, im + 2 - dt, lr, :] = w[0, :, dt].transpose(0, 2, 1)
    gate_cols[:, :, :GM] = gate_w.reshape(P, 3, GM)
    a["gate_w"] = gate_cols
    a["b_l"], a["b_r"] = v["L0_conv_b_l"], v["L0_conv_b_r"]
    gate_sel = zeros(4, NQ, 2, 3, 2, 3, 2, T)
    for h in range(2):
        for jj in range(4):
            for q in range(NQ):
                for lr in range(2):
                    for dy in range(3):
                        gate_sel[jj, q, lr, dy, h, dy, lr, (2 * (4 * h + jj) - 1 + q) % T] = 1
    a["gate_sel"] = gate_sel.reshape(4 * GM, 2, 3, 2 * T)
    gate_bc = zeros(P, 4, 4, 2, HALF)
    for t in range(T):
        for lr in range(2):
            gate_bc[lr * T + t, t // 4, t % 4, lr] = 1
    a["gate_bc"] = gate_bc.reshape(P, 4, P)
    w_gate = zeros(2, C, 2, E)
    conv_w = zeros(2, C, 9, 2, C)
    for im in range(2):
        w_gate[im, :, im] = v["L0_ffn_Wg"]
        conv_w[im, :, :, im] = v["L1_conv_weights"].reshape(C, C, 9).transpose(1, 2, 0)
    a["w_gate"] = w_gate.reshape(P, 2 * E)
    a["b_gate"] = np.tile(v["L0_ffn_bg"], SUB * 2)
    w1 = v["L0_ffn_W1"].transpose(1, 0, 2).reshape(C, E * H0)
    a["w1"] = np.concatenate([w1, w1])
    a["w2"] = v["L0_ffn_W2"].reshape(E, CH0, P, C).transpose(2, 0, 1, 3)
    a["b1"] = v["L0_ffn_b1"].reshape(E, CH0, P).transpose(2, 0, 1)
    a["b2"] = np.concatenate([v["L0_ffn_b2"].T, v["L0_ffn_b2"].T])
    a["conv_w"] = conv_w.reshape(P, 9, P)
    a["factor"] = v["L1_conv_real_scaling_factor"].reshape(C, 1)
    a["w_route"] = v["L1_ffn_Wr"]
    a["b_route"] = np.tile(v["L1_ffn_br"], 2)
    w1 = v["L1_ffn_W1"].transpose(1, 0, 2)
    a["w1_l1"] = np.concatenate([w1, w1])
    a["w2_l1"] = v["L1_ffn_W2"]
    a["b1_l1"] = v["L1_ffn_b1"].reshape(E, F1, 1)
    a["b2_l1"] = v["L1_ffn_b2"].reshape(E, C, 1)
    a["gamma"], a["beta"] = v["L1_ffn_gamma"].reshape(C, 1), v["L1_ffn_beta"].reshape(C, 1)
    block = np.kron(np.eye(2), np.ones((C, C))) / C
    a["centre"], a["average"], a["ident"] = (np.eye(P) - block).astype(f), block.astype(f), np.eye(P, dtype=f)

    nc = bacc.Bacc("TRN2", target_bir_lowering=False, num_devices=1)
    arrays = {f"in_{k}": np.ascontiguousarray(x) for k, x in a.items()}
    aps = {k: nc.dram_tensor(f"in_{k}", x.shape, mybir.dt.from_np(x.dtype), kind="ExternalInput").ap()
           for k, x in a.items()}
    out = nc.dram_tensor("out", (NT, P, TW), F32, kind="ExternalOutput").ap()
    build(nc, aps, out)
    r = run_bass_kernel_spmd(nc, [arrays], core_ids=[0])
    return r.results[0]["out"].reshape(NP, KT, P, TW).transpose(0, 2, 1, 3).reshape(T, C, HH, WW)
```
